# Optimizing a Trainium2 kernel written in Bass

```python
import numpy as np
import jax
import jax.numpy as jnp

def _softmax(x, axis=-1):
    return jax.nn.softmax(x, axis=axis)

def _gelu(x):
    return jax.nn.gelu(x, approximate=True)

def _silu(x):
    return jax.nn.silu(x)

def _sigmoid(x):
    return jax.nn.sigmoid(x)

def _layernorm(x, axis=-1, eps=1e-05):
    m = jnp.mean(x, axis=axis, keepdims=True)
    v = jnp.var(x, axis=axis, keepdims=True)
    return (x - m) / jnp.sqrt(v + eps)

def _scatter_add(tgt, idx, src, axis=0):
    return tgt.at[idx].add(src)

def _segment_sum(src, seg, n):
    return jax.ops.segment_sum(src, seg, n)
kernel_name = 'mk_macaron_d2_jaxref_r8_e40b61'

def setup_inputs(seed: int=0):
    np.random.seed(seed)
    _w = jnp.asarray

    def _L0_attn_setup():
        import jax, jax.numpy as jnp
        import numpy as np
        B, S, D = (4, 512, 128)
        H, HD = (16, 64)
        EPS = 1e-06

        def _feature_map(t):
            return jax.nn.elu(t) + 1.0
        key = jax.random.key(seed)
        ks = jax.random.split(key, 9)
        sd = 1.0 / np.sqrt(D)
        x = jax.random.normal(ks[0], (B, S, D), dtype=jnp.float32)
        wq = jax.random.normal(ks[1], (D, H, HD), dtype=jnp.float32) * sd
        bq = jnp.zeros((H, HD), dtype=jnp.float32)
        wk = jax.random.normal(ks[2], (D, H, HD), dtype=jnp.float32) * sd
        bk = jnp.zeros((H, HD), dtype=jnp.float32)
        wv = jax.random.normal(ks[3], (D, H, HD), dtype=jnp.float32) * sd
        bv = jnp.zeros((H, HD), dtype=jnp.float32)
        wo = jax.random.normal(ks[4], (H, HD, D), dtype=jnp.float32) * (1.0 / np.sqrt(H * HD))
        bo = jnp.zeros((D,), dtype=jnp.float32)
        return {'x': x, 'wq': wq, 'bq': bq, 'wk': wk, 'bk': bk, 'wv': wv, 'bv': bv, 'wo': wo, 'bo': bo}
    _L0_attn_in = _L0_attn_setup()

    def _L0_ffn_setup():
        import jax, jax.numpy as jnp
        import numpy as np
        D = 128
        H = 16
        DH = D // H
        DC = D // 4
        HID = 256
        G = 2
        EPG = 4
        E = G * EPG
        TOPK = 2
        EPS = 1e-06
        B, T = (2, 256)

        def _rope_sincos(t, dh):
            inv_freq = 1.0 / 10000.0 ** (jnp.arange(0, dh, 2, dtype=jnp.float32) / dh)
            ang = jnp.arange(t, dtype=jnp.float32)[:, None] * inv_freq[None, :]
            return (jnp.sin(ang), jnp.cos(ang))

        def _apply_rope(x, sin, cos):
            x1 = x[..., ::2]
            x2 = x[..., 1::2]
            r = jnp.stack([x1 * cos - x2 * sin, x1 * sin + x2 * cos], axis=-1)
            return r.reshape(x.shape)

        def _swiglu(x):
            a, b = jnp.split(x, 2, axis=-1)
            return jax.nn.silu(a) * b

        def _rmsnorm(x, w):
            return x * jax.lax.rsqrt(jnp.mean(x * x, axis=-1, keepdims=True) + EPS) * w
        key = jax.random.key(seed)
        ks = jax.random.split(key, 14)
        s = 0.02
        return {'src': jax.random.normal(ks[0], (B, T, D), jnp.float32), 'Wq': jax.random.normal(ks[1], (D, D), jnp.float32) * s, 'Wk_c': jax.random.normal(ks[2], (D, DC), jnp.float32) * s, 'Wv_c': jax.random.normal(ks[3], (D, DC), jnp.float32) * s, 'Wk': jax.random.normal(ks[4], (DC, D), jnp.float32) * s, 'Wv': jax.random.normal(ks[5], (DC, D), jnp.float32) * s, 'Wo': jax.random.normal(ks[6], (D, D), jnp.float32) * s, 'W_shared_in': jax.random.normal(ks[7], (D, 2 * HID), jnp.float32) * s, 'W_shared_out': jax.random.normal(ks[8], (HID, D), jnp.float32) * s, 'W1_shared': jax.random.normal(ks[9], (D, 2 * HID), jnp.float32) * s, 'W2_experts': jax.random.normal(ks[10], (E, HID, D), jnp.float32) * s, 'Wg_gate': jax.random.normal(ks[11], (D, G), jnp.float32) * s, 'We_gate': jax.random.normal(ks[12], (D, E), jnp.float32) * s, 'group_bias': jnp.zeros((G,), jnp.float32), 'expert_bias': jnp.zeros((E,), jnp.float32), 'norm1_w': jnp.ones((D,), jnp.float32), 'norm2_w': jnp.ones((D,), jnp.float32)}
    _L0_ffn_in = _L0_ffn_setup()

    def _L1_attn_setup():
        import jax, jax.numpy as jnp
        import numpy as np
        HIDDEN = 128
        NUM_HEADS = 16
        HEAD_SIZE = 64
        key = jax.random.key(seed)
        ks = jax.random.split(key, 5)
        B, S = (2, 256)
        scale = 1.0 / np.sqrt(HIDDEN)
        x = jax.random.normal(ks[0], (B, S, HIDDEN), dtype=jnp.float32)
        W_qkv = jax.random.normal(ks[1], (HIDDEN, 3 * NUM_HEADS * HEAD_SIZE), dtype=jnp.float32) * scale
        b_qkv = jnp.zeros((3 * NUM_HEADS * HEAD_SIZE,), dtype=jnp.float32)
        W_out = jax.random.normal(ks[2], (NUM_HEADS * HEAD_SIZE, HIDDEN), dtype=jnp.float32) * scale
        b_out = jnp.zeros((HIDDEN,), dtype=jnp.float32)
        return {'x': x, 'W_qkv': W_qkv, 'b_qkv': b_qkv, 'W_out': W_out, 'b_out': b_out}
    _L1_attn_in = _L1_attn_setup()

    def _L1_ffn_setup():
        import jax, jax.numpy as jnp
        import numpy as np
        B, S, D, E, F = (2, 128, 128, 14, 256)
        key = jax.random.key(seed)
        k0, k1, k2, k3 = jax.random.split(key, 4)
        h = jax.random.normal(k0, (B, S, D), jnp.float32)
        gate_w = jax.random.normal(k1, (E, D), jnp.float32) * 0.02
        w1 = jax.random.normal(k2, (E, D, F), jnp.float32) * (1.0 / np.sqrt(D).astype(np.float32))
        b1 = jnp.zeros((E, F), jnp.float32)
        w2 = jax.random.normal(k3, (E, F, D), jnp.float32) * (1.0 / np.sqrt(F).astype(np.float32))
        b2 = jnp.zeros((E, D), jnp.float32)
        return {'h': h, 'gate_w': gate_w, 'w1': w1, 'b1': b1, 'w2': w2, 'b2': b2}
    _L1_ffn_in = _L1_ffn_setup()
    _d = {'L0_attn_x': _L0_attn_in['x'], 'L0_attn_wq': _L0_attn_in['wq'], 'L0_attn_bq': _L0_attn_in['bq'], 'L0_attn_wk': _L0_attn_in['wk'], 'L0_attn_bk': _L0_attn_in['bk'], 'L0_attn_wv': _L0_attn_in['wv'], 'L0_attn_bv': _L0_attn_in['bv'], 'L0_attn_wo': _L0_attn_in['wo'], 'L0_attn_bo': _L0_attn_in['bo'], 'L0_ffn_Wq': _L0_ffn_in['Wq'], 'L0_ffn_Wk_c': _L0_ffn_in['Wk_c'], 'L0_ffn_Wv_c': _L0_ffn_in['Wv_c'], 'L0_ffn_Wk': _L0_ffn_in['Wk'], 'L0_ffn_Wv': _L0_ffn_in['Wv'], 'L0_ffn_Wo': _L0_ffn_in['Wo'], 'L0_ffn_W_shared_in': _L0_ffn_in['W_shared_in'], 'L0_ffn_W_shared_out': _L0_ffn_in['W_shared_out'], 'L0_ffn_W1_shared': _L0_ffn_in['W1_shared'], 'L0_ffn_W2_experts': _L0_ffn_in['W2_experts'], 'L0_ffn_Wg_gate': _L0_ffn_in['Wg_gate'], 'L0_ffn_We_gate': _L0_ffn_in['We_gate'], 'L0_ffn_group_bias': _L0_ffn_in['group_bias'], 'L0_ffn_expert_bias': _L0_ffn_in['expert_bias'], 'L0_ffn_norm1_w': _L0_ffn_in['norm1_w'], 'L0_ffn_norm2_w': _L0_ffn_in['norm2_w'], 'L1_attn_W_qkv': _L1_attn_in['W_qkv'], 'L1_attn_b_qkv': _L1_attn_in['b_qkv'], 'L1_attn_W_out': _L1_attn_in['W_out'], 'L1_attn_b_out': _L1_attn_in['b_out'], 'L1_ffn_gate_w': _L1_ffn_in['gate_w'], 'L1_ffn_w1': _L1_ffn_in['w1'], 'L1_ffn_b1': _L1_ffn_in['b1'], 'L1_ffn_w2': _L1_ffn_in['w2'], 'L1_ffn_b2': _L1_ffn_in['b2']}
    _x0 = _d['L0_attn_x']
    _d['L0_attn_x'] = jax.random.normal(jax.random.fold_in(jax.random.key(seed), 1), (4, 1024, 128), dtype=_x0.dtype)
    del _x0
    return _d

def reference(L0_attn_x, L0_attn_wq, L0_attn_bq, L0_attn_wk, L0_attn_bk, L0_attn_wv, L0_attn_bv, L0_attn_wo, L0_attn_bo, L0_ffn_Wq, L0_ffn_Wk_c, L0_ffn_Wv_c, L0_ffn_Wk, L0_ffn_Wv, L0_ffn_Wo, L0_ffn_W_shared_in, L0_ffn_W_shared_out, L0_ffn_W1_shared, L0_ffn_W2_experts, L0_ffn_Wg_gate, L0_ffn_We_gate, L0_ffn_group_bias, L0_ffn_expert_bias, L0_ffn_norm1_w, L0_ffn_norm2_w, L1_attn_W_qkv, L1_attn_b_qkv, L1_attn_W_out, L1_attn_b_out, L1_ffn_gate_w, L1_ffn_w1, L1_ffn_b1, L1_ffn_w2, L1_ffn_b2):

    def _L0_attn_ref(x, wq, bq, wk, bk, wv, bv, wo, bo):
        import jax, jax.numpy as jnp
        import numpy as np
        B, S, D = (4, 512, 128)
        H, HD = (16, 64)
        EPS = 1e-06

        def _feature_map(t):
            return jax.nn.elu(t) + 1.0
        q = jnp.einsum('nsf,fhd->nshd', x, wq) + bq
        k = jnp.einsum('nsf,fhd->nshd', x, wk) + bk
        v = jnp.einsum('nsf,fhd->nshd', x, wv) + bv
        qm = _feature_map(q)
        km = _feature_map(k)
        kv = jnp.einsum('nshd,nshm->nhmd', km, v)
        z = 1.0 / (jnp.einsum('nlhd,nhd->nlh', qm, jnp.sum(km, axis=1)) + EPS)
        y = jnp.einsum('nlhd,nhmd,nlh->nlhm', qm, kv, z)
        out = jnp.einsum('nlhm,hmf->nlf', y, wo) + bo
        return out

    def _L0_ffn_ref(src, Wq, Wk_c, Wv_c, Wk, Wv, Wo, W_shared_in, W_shared_out, W1_shared, W2_experts, Wg_gate, We_gate, group_bias, expert_bias, norm1_w, norm2_w):
        import jax, jax.numpy as jnp
        import numpy as np
        D = 128
        H = 16
        DH = D // H
        DC = D // 4
        HID = 256
        G = 2
        EPG = 4
        E = G * EPG
        TOPK = 2
        EPS = 1e-06
        B, T = (2, 256)

        def _rope_sincos(t, dh):
            inv_freq = 1.0 / 10000.0 ** (jnp.arange(0, dh, 2, dtype=jnp.float32) / dh)
            ang = jnp.arange(t, dtype=jnp.float32)[:, None] * inv_freq[None, :]
            return (jnp.sin(ang), jnp.cos(ang))

        def _apply_rope(x, sin, cos):
            x1 = x[..., ::2]
            x2 = x[..., 1::2]
            r = jnp.stack([x1 * cos - x2 * sin, x1 * sin + x2 * cos], axis=-1)
            return r.reshape(x.shape)

        def _swiglu(x):
            a, b = jnp.split(x, 2, axis=-1)
            return jax.nn.silu(a) * b

        def _rmsnorm(x, w):
            return x * jax.lax.rsqrt(jnp.mean(x * x, axis=-1, keepdims=True) + EPS) * w
        Bb, Tt, C = src.shape
        q = (src @ Wq).reshape(Bb, Tt, H, DH).transpose(0, 2, 1, 3)
        k = (src @ Wk_c @ Wk).reshape(Bb, Tt, H, DH).transpose(0, 2, 1, 3)
        v = (src @ Wv_c @ Wv).reshape(Bb, Tt, H, DH).transpose(0, 2, 1, 3)
        sin, cos = _rope_sincos(Tt, DH)
        q = _apply_rope(q, sin, cos)
        k = _apply_rope(k, sin, cos)
        attn = jnp.einsum('bhqd,bhkd->bhqk', q, k) / np.sqrt(DH).astype(np.float32)
        attn = jax.nn.softmax(attn, axis=-1)
        sa = jnp.einsum('bhqk,bhkd->bhqd', attn, v)
        sa = sa.transpose(0, 2, 1, 3).reshape(Bb, Tt, C) @ Wo
        x = _rmsnorm(src + sa, norm1_w)
        S = Bb * Tt
        flat = x.reshape(S, C)
        shared = _swiglu(flat @ W_shared_in) @ W_shared_out
        g_probs = jax.nn.softmax(flat @ Wg_gate + group_bias, -1)
        g_idx = jnp.argmax(g_probs, axis=-1)
        e_logits = flat @ We_gate + expert_bias
        e_group = jnp.arange(E) // EPG
        in_group = e_group[None, :] == g_idx[:, None]
        e_probs = jax.nn.softmax(jnp.where(in_group, e_logits, -jnp.inf), -1)
        g_prob = jnp.take_along_axis(g_probs, g_idx[:, None], axis=1)
        p_expert = e_probs * g_prob
        topv, topi = jax.lax.top_k(p_expert, TOPK)
        w = jnp.zeros((S, E), flat.dtype).at[jnp.arange(S)[:, None], topi].set(topv)
        h = _swiglu(flat @ W1_shared)
        routed = jnp.zeros_like(shared)
        for e in range(E):
            routed = routed + h @ W2_experts[e] * w[:, e:e + 1]
        out = x + (shared + routed).reshape(Bb, Tt, C)
        return _rmsnorm(out, norm2_w)

    def _L1_attn_ref(x, W_qkv, b_qkv, W_out, b_out):
        import jax, jax.numpy as jnp
        import numpy as np
        HIDDEN = 128
        NUM_HEADS = 16
        HEAD_SIZE = 64
        B, S, _ = x.shape
        qkv = x @ W_qkv + b_qkv
        qkv = qkv.reshape(B, S, 3 * NUM_HEADS, HEAD_SIZE)
        Q = qkv[:, :, :NUM_HEADS, :]
        K = qkv[:, :, NUM_HEADS:2 * NUM_HEADS, :]
        V = qkv[:, :, 2 * NUM_HEADS:, :]
        scores = jnp.einsum('bqhi,bkhi->bhqk', Q, K) / jnp.sqrt(jnp.float32(HEAD_SIZE))
        mask = jnp.triu(jnp.full((S, S), -10000.0, dtype=scores.dtype), k=1)
        scores = scores + mask
        probs = jax.nn.softmax(scores, axis=-1)
        vals = jnp.einsum('bkhi,bhqk->bqhi', V, probs)
        vals = vals.reshape(B, S, NUM_HEADS * HEAD_SIZE)
        return vals @ W_out + b_out

    def _L1_ffn_ref(h, gate_w, w1, b1, w2, b2):
        import jax, jax.numpy as jnp
        import numpy as np
        B, S, D, E, F = (2, 128, 128, 14, 256)
        Bb, Ss, Dd = h.shape
        x = h.reshape(Bb * Ss, Dd)
        logits = x @ gate_w.T
        probs = jax.nn.softmax(logits, axis=-1)
        top2_p, top2_i = jax.lax.top_k(probs, 2)
        w = top2_p / jnp.maximum(top2_p.sum(-1, keepdims=True), 1e-10)
        hh = jnp.einsum('nd,edf->nef', x, w1) + b1
        hh = jax.nn.gelu(hh, approximate=False)
        all_out = jnp.einsum('nef,efd->ned', hh, w2) + b2
        n = jnp.arange(x.shape[0])
        out0 = all_out[n, top2_i[:, 0]]
        out1 = all_out[n, top2_i[:, 1]]
        moe_out = w[:, 0:1] * out0 + w[:, 1:2] * out1
        result = jnp.clip(x + moe_out, -100.0, 100.0).reshape(Bb, Ss, Dd)
        return result
    x = L0_attn_x
    x = x + 0.5 * _L0_ffn_ref(_layernorm(x, axis=-1), L0_ffn_Wq, L0_ffn_Wk_c, L0_ffn_Wv_c, L0_ffn_Wk, L0_ffn_Wv, L0_ffn_Wo, L0_ffn_W_shared_in, L0_ffn_W_shared_out, L0_ffn_W1_shared, L0_ffn_W2_experts, L0_ffn_Wg_gate, L0_ffn_We_gate, L0_ffn_group_bias, L0_ffn_expert_bias, L0_ffn_norm1_w, L0_ffn_norm2_w)
    x = x + _L0_attn_ref(_layernorm(x, axis=-1), L0_attn_wq, L0_attn_bq, L0_attn_wk, L0_attn_bk, L0_attn_wv, L0_attn_bv, L0_attn_wo, L0_attn_bo)
    x = x + 0.5 * _L0_ffn_ref(_layernorm(x, axis=-1), L0_ffn_Wq, L0_ffn_Wk_c, L0_ffn_Wv_c, L0_ffn_Wk, L0_ffn_Wv, L0_ffn_Wo, L0_ffn_W_shared_in, L0_ffn_W_shared_out, L0_ffn_W1_shared, L0_ffn_W2_experts, L0_ffn_Wg_gate, L0_ffn_We_gate, L0_ffn_group_bias, L0_ffn_expert_bias, L0_ffn_norm1_w, L0_ffn_norm2_w)
    x = x + 0.5 * _L1_ffn_ref(_layernorm(x, axis=-1), L1_ffn_gate_w, L1_ffn_w1, L1_ffn_b1, L1_ffn_w2, L1_ffn_b2)
    x = x + _L1_attn_ref(_layernorm(x, axis=-1), L1_attn_W_qkv, L1_attn_b_qkv, L1_attn_W_out, L1_attn_b_out)
    x = x + 0.5 * _L1_ffn_ref(_layernorm(x, axis=-1), L1_ffn_gate_w, L1_ffn_w1, L1_ffn_b1, L1_ffn_w2, L1_ffn_b2)
    return x

_drawn_inputs = setup_inputs


def setup_inputs(seed=0):
    import zlib

    import numpy as np

    out = dict(_drawn_inputs(seed))
    spreads = {'L0_attn_bq': (0.0, 2.0),
     'L0_attn_bk': (0.0, 2.0),
     'L0_attn_bv': (0.0, 0.1),
     'L0_attn_bo': (0.0, 0.1),
     'L0_ffn_group_bias': (0.0, 0.8),
     'L0_ffn_expert_bias': (0.0, 0.8),
     'L0_ffn_norm1_w': (1.0, 0.2),
     'L0_ffn_norm2_w': (1.0, 0.2),
     'L1_attn_b_qkv': (0.0, 0.1),
     'L1_attn_b_out': (0.0, 0.1),
     'L1_ffn_b1': (0.0, 0.409),
     'L1_ffn_b2': (0.0, 0.299)}
    factors = {'L0_attn_wq': 6.91,
     'L0_attn_wk': 4.683,
     'L0_ffn_Wq': 8.0,
     'L0_ffn_Wk_c': 8.0,
     'L0_ffn_Wv_c': 8.0,
     'L0_ffn_Wk': 8.0,
     'L0_ffn_Wv': 8.0,
     'L0_ffn_Wo': 8.0,
     'L0_ffn_W_shared_in': 5.421,
     'L0_ffn_W_shared_out': 5.377,
     'L0_ffn_W1_shared': 8.0,
     'L0_ffn_W2_experts': 8.0,
     'L0_ffn_Wg_gate': 8.0,
     'L0_ffn_We_gate': 8.0}
    for name, (base, spread) in spreads.items():
        noise = np.random.default_rng([zlib.crc32(name.encode()), seed]).standard_normal(out[name].shape)
        drawn = base * np.exp(spread * noise) if base else spread * noise
        out[name] = jnp.asarray(drawn.astype(out[name].dtype))
    for name, factor in factors.items():
        out[name] = (out[name] * factor).astype(out[name].dtype)
    return out
```

```python
from contextlib import ExitStack
from itertools import count

import numpy as np

import concourse.bass as bass
from concourse import mybir

F32 = mybir.dt.float32
BF16 = mybir.dt.bfloat16
ALU = mybir.AluOpType
ACT = mybir.ActivationFunctionType
AX = mybir.AxisListType

P = 128
BATCH, SEQ, D = 4, 1024, 128
TOKENS = BATCH * SEQ
BT = 512
TPB = BT // P
NBLK = TOKENS // BT
NT = TOKENS // P
HALVES = SEQ // BT

H0, DH = 16, 8
GH = 4
NG = H0 // GH
PARTS = 3
STK = PARTS * PARTS * DH
KMAX = 96
KROWS = KMAX + PARTS
VW = 32
KT = SEQ // P

HID, E0, EPG = 256, 8, 4
GA = 2
H1, HD = 16, 64
NP = H1 // 2
E1, F1 = 14, 256

LN_EPS, RMS_EPS, LIN_EPS = 1e-5, 1e-6, 1e-6
MASK_ROW, MASK_COL = 250.0, -320.0


class Chain:

    def __init__(self, engine, sem, start=0):
        self.engine, self.sem, self.start, self.n = engine, sem, start, 0

    def tick(self, ins):
        ins.then_inc(self.sem, 1)
        self.n += 1

    def wait(self):
        self.engine.wait_ge(self.sem, self.start + self.n)

    def link(self, ins):
        self.tick(ins)
        self.wait()


def bc(ap, dims):
    return bass.AP(ap.tensor, ap.offset, [list(ap.ap[0])] + [list(d) for d in dims])


def build(nc, a, out, upto=99):
    with ExitStack() as ctx:
        X = ctx.enter_context(nc.sbuf_tensor("X", [P, NT + TPB, D], F32))
        XN = ctx.enter_context(nc.sbuf_tensor("XN", [P, NT, D], F32))
        XNT = ctx.enter_context(nc.sbuf_tensor("XNT", [P, TOKENS], F32))
        IDN = ctx.enter_context(nc.sbuf_tensor("IDN", [P, P], F32))
        PS = ctx.enter_context(nc.psum_tensor("PS", [P, 8, BT], F32))
        PW = ctx.enter_context(nc.sbuf_tensor("PW", [P, TPB], F32))
        scratch = dict(
            QK=nc.dram_tensor("qk_parts", [2, BATCH * NG, PARTS, GH * DH, SEQ], BF16, kind="Internal").ap(),
            V=nc.dram_tensor("v_heads", [BATCH * NG, SEQ, GH * DH], F32, kind="Internal").ap(),
            O=nc.dram_tensor("o_heads", [BATCH * NG, P, SEQ], F32, kind="Internal").ap(),
        )
        g = dict(X=X, XN=XN, XNT=XNT, IDN=IDN, PS=PS, PW=PW, **scratch)
        start(nc, a, g)
        stages = [
            lambda: layernorm(nc, g), lambda: rope_project(nc, a, g), lambda: rope_attention(nc, a, g),
            lambda: ffn0(nc, a, g),
            lambda: layernorm(nc, g), lambda: linear_attention(nc, a, g),
            lambda: layernorm(nc, g), lambda: rope_project(nc, a, g), lambda: rope_attention(nc, a, g),
            lambda: ffn0(nc, a, g),
            lambda: layernorm(nc, g), lambda: ffn1(nc, a, g),
            lambda: layernorm(nc, g), lambda: causal(nc, a, g),
            lambda: layernorm(nc, g), lambda: ffn1(nc, a, g),
        ]
        for s in stages[:upto]:
            s()
        finish(nc, g, out)


STAGES = count()


def stage(nc, ctx):
    number = next(STAGES)
    sems = []

    def sb(name, shape, dt=F32):
        return ctx.enter_context(nc.sbuf_tensor(f"{name}_{number}", shape, dt))

    def sem(name):
        if not sems:
            ctx.callback(clear)
        sems.append(nc.alloc_semaphore(f"{name}_{number}"))
        return sems[-1]

    def clear():
        nc.clear_and_free_semaphores(sems)
        nc.all_engine_barrier()
    return sb, sem


def start(nc, a, g):
    X, IDN, PW = g["X"], g["IDN"], g["PW"]
    with ExitStack() as ctx:
        sb, sem = stage(nc, ctx)
        loaded = sem("loaded")
        with nc.Block() as block:
            @block.sync
            def _(sp):
                sp.dma_start(X[:, 0:NT, :], a["L0_attn_x"].rearrange("b (t p) d -> p (b t) d", p=P)).then_inc(loaded, 16)
                sp.dma_start(IDN[:, :], a["c_ident"]).then_inc(loaded, 16)
                sp.wait_ge(loaded, 32)

            @block.gpsimd
            def _(pool):
                pool.memset(X[:, NT:NT + TPB, :], 0.0)
                pool.memset(PW[:, :], -0.5)


def finish(nc, g, out):
    X = g["X"]
    with ExitStack() as ctx:
        sb, sem = stage(nc, ctx)
        stored = sem("stored")
        with nc.Block() as block:
            @block.sync
            def _(sp):
                sp.dma_start(out.rearrange("b (t p) d -> p (b t) d", p=P), X[:, 0:NT, :]).then_inc(stored, 16)
                sp.wait_ge(stored, 16)


def layernorm(nc, g):
    X, XN, XNT, IDN, PS, PW = (g[k] for k in ("X", "XN", "XNT", "IDN", "PS", "PW"))
    with ExitStack() as ctx:
        sb, sem = stage(nc, ctx)
        st = sb("ln_st", [P, 2, TPB, 6])
        mv = sb("ln_mv", [P, 2, TPB, 2])
        ve = sb("ln_ve", [P, 2, TPB])
        rs = sb("ln_rs", [P, 2, TPB])
        xn = sb("ln_xn", [P, 2, TPB, D])
        eps = sb("ln_eps", [P, TPB])
        mark = sb("ln_mark", [P, 1])
        s_st, s_mv, s_ve, s_rs, s_xn, s_t, s_c = (sem("ln_" + n) for n in
                                                  ("stats", "meanvar", "vareps", "rstd", "normed", "turned", "copied"))
        with nc.Block() as block:
            @block.vector
            def _(dve):
                def stats(n, u):
                    for j in range(TPB):
                        dve.bn_stats(st[:, u, j, :], X[:, TPB * n + j, :]).then_inc(s_st, 1)
                    dve.wait_ge(s_st, (TPB + 1) * n + TPB)
                    dve.memset(mark[:, :], 0.0).then_inc(s_st, 1)
                    for j in range(TPB):
                        dve.bn_aggr(mv[:, u, j, :], st[:, u, j, :]).then_inc(s_mv, 1)

                dve.memset(eps[:, :], LN_EPS)
                stats(0, 0)
                with dve.Fori(0, NBLK // 2) as it:
                    for u in range(2):
                        n = 2 * it + u
                        stats(n + 1, 1 - u)
                        dve.wait_ge(s_rs, n + 1)
                        dve.wait_ge(s_c, 2 * n)
                        for j in range(TPB):
                            dve.tensor_scalar(xn[:, u, j, :], X[:, TPB * n + j, :], mv[:, u, j, 0:1],
                                              rs[:, u, j:j + 1], ALU.subtract, ALU.mult).then_inc(s_xn, 1)

            @block.gpsimd
            def _(pool):
                with pool.Fori(0, NBLK // 2) as it:
                    for u in range(2):
                        n = 2 * it + u
                        pool.wait_ge(s_mv, TPB * n + TPB)
                        pool.tensor_tensor(ve[:, u, :], mv[:, u, :, 1], eps[:, :], ALU.add).then_inc(s_ve, 1)
                        pool.wait_ge(s_ve, n + 1)
                        pool.wait_ge(s_xn, TPB * n)
                        pool.tensor_tensor(rs[:, u, :], ve[:, u, :], PW[:, :], ALU.pow).then_inc(s_rs, 1)

            @block.tensor
            def _(pe):
                with pe.Fori(0, NBLK // 2) as it:
                    for u in range(2):
                        n = 2 * it + u
                        pe.wait_ge(s_xn, TPB * n + TPB)
                        pe.wait_ge(s_c, 2 * n)
                        for j in range(TPB):
                            mm = pe.transpose(PS[:, u, j * P:(j + 1) * P], xn[:, u, j, :], IDN[:, :])
                        mm.then_inc(s_t, 1)

            @block.scalar
            def _(act):
                act.drain().then_inc(s_c, 2)
                with act.Fori(0, NBLK // 2) as it:
                    for u in range(2):
                        n = 2 * it + u
                        act.wait_ge(s_xn, TPB * n + TPB)
                        act.activation(XN[:, bass.ds(TPB * n, TPB), :], xn[:, u, :, :], ACT.Copy).then_inc(s_c, 1)
                        act.wait_ge(s_t, n + 1)
                        act.activation(XNT[:, bass.ds(BT * n, BT)], PS[:, u, :], ACT.Copy).then_inc(s_c, 1)


def rope_project(nc, a, g):
    XNT, IDN, PS = g["XNT"], g["IDN"], g["PS"]
    DC = a["L0_ffn_Wk_c"].shape[1]
    with ExitStack() as ctx:
        sb, sem = stage(nc, ctx)
        wq = sb("rp_wq", [P, D])
        wc = sb("rp_wc", [P, 2, DC])
        wkv = sb("rp_wkv", [DC, 2, D])
        wcT = sb("rp_wcT", [DC, 2, P])
        W = sb("rp_W", [P, 5, D])
        ROT = sb("rp_rot", [P, 2, SEQ])
        xs = sb("rp_xs", [P, 2, BT])
        t1 = sb("rp_t1", [P, 2, BT])
        t2 = sb("rp_t2", [P, 2, BT])
        qk = sb("rp_qk", [P, 2, BT])
        res = sb("rp_res", [P, 2, BT])
        parts = sb("rp_parts", [P, 2, PARTS, 2, BT], BF16)
        vs = sb("rp_vs", [P, 2, TPB, D])
        s_ld, s_w, s_wt, s_xs, s_pj, s_rd, s_v, s_chain, s_pt, s_st, s_vst, s_qk, s_h = (sem("rp_" + n) for n in (
            "loaded", "weights", "wturned", "x_ready", "projected", "psum_read", "v_copied", "chain", "parts_done",
            "qk_stored", "v_stored", "qk_done", "high_done"))
        with nc.Block() as block:
            @block.sync
            def _(sp):
                sp.dma_start(wq[:, :], a["L0_ffn_Wq"]).then_inc(s_ld, 16)
                sp.dma_start(wc[:, 0, :], a["L0_ffn_Wk_c"]).then_inc(s_ld, 16)
                sp.dma_start(wc[:, 1, :], a["L0_ffn_Wv_c"]).then_inc(s_ld, 16)
                sp.dma_start(wkv[:, 0, :], a["L0_ffn_Wk"]).then_inc(s_ld, 16)
                sp.dma_start(wkv[:, 1, :], a["L0_ffn_Wv"]).then_inc(s_ld, 16)
                sp.dma_start(ROT[:, :, :], a["c_rope"].rearrange("t p s -> p t s")).then_inc(s_ld, 16)
                with sp.Fori(0, BATCH) as b:
                    for u in range(2):
                        n = 2 * b + u
                        sp.wait_ge(s_v, n + 1)
                        for gi in range(NG):
                            sp.dma_start(g["V"][NG * b + gi, u * BT:(u + 1) * BT, :].rearrange("(j p) c -> p j c", p=P),
                                         vs[:, u, :, gi * GH * DH:(gi + 1) * GH * DH]).then_inc(s_vst, 16)
                        sp.wait_ge(s_pt, n + 1)
                        for t in range(2):
                            for gi in range(NG):
                                sp.dma_start(
                                    g["QK"][t, NG * b + gi, :, :, u * BT:(u + 1) * BT].rearrange("w r s -> r w s"),
                                    parts[gi * GH * DH:(gi + 1) * GH * DH, u, :, t, :]).then_inc(s_st, 16)
                sp.wait_ge(s_vst, 16 * NG * NBLK)
                sp.wait_ge(s_st, 16 * 2 * NG * NBLK)

            @block.tensor
            def _(pe):
                pe.wait_ge(s_ld, 96)
                for t in range(2):
                    mm = pe.transpose(PS[0:DC, 7, t * P:(t + 1) * P], wc[:, t, :], IDN[:, :])
                mm.then_inc(s_wt, 1)
                pe.wait_ge(s_w, 1)
                for t in range(2):
                    mm = pe.matmul(PS[:, 6, t * P:(t + 1) * P], wcT[:, t, :], wkv[:, t, :], start=True, stop=True)
                mm.then_inc(s_wt, 1)
                pe.wait_ge(s_w, 6)
                with pe.Fori(0, BATCH) as b:
                    for u in range(2):
                        n = 2 * b + u
                        pe.wait_ge(s_xs, n + 1)
                        pe.wait_ge(s_rd, 2 * n)
                        for k in range(4):
                            mm = pe.matmul(PS[:, k, :], W[:, k, :], xs[:, u, :], start=True, stop=True)
                        mm.then_inc(s_pj, 1)
                        pe.wait_ge(s_v, n)
                        for j in range(TPB):
                            mm = pe.matmul(PS[:, 4, j * P:(j + 1) * P], xs[:, u, j * P:(j + 1) * P], W[:, 4, :],
                                           start=True, stop=True)
                        mm.then_inc(s_pj, 1)

            @block.vector
            def _(dve):
                dve.wait_ge(s_wt, 1)
                dve.tensor_copy(wcT[:, :, :], PS[0:DC, 7, 0:2 * P].rearrange("p (t m) -> p t m", t=2)).then_inc(s_w, 1)
                dve.wait_ge(s_wt, 2)
                dve.tensor_copy(W[:, 0, :], wq[:, :]).then_inc(s_w, 1)
                dve.tensor_copy(W[:, 1, :], PS[:, 6, 0:P]).then_inc(s_w, 1)
                dve.tensor_copy(W[:, 4, :], PS[:, 6, P:2 * P]).then_inc(s_w, 1)
                dve.wait_ge(s_w, 4)
                wv = W[:, 0:4, :].rearrange("p k (i two) -> p k i two", two=2)
                dve.tensor_scalar(wv[:, 2:4, :, 0], wv[:, 0:2, :, 1], -1.0, None, ALU.mult).then_inc(s_w, 1)
                dve.tensor_copy(wv[:, 2:4, :, 1], wv[:, 0:2, :, 0]).then_inc(s_w, 1)
                with dve.Fori(0, BATCH) as b:
                    for u in range(2):
                        n = 2 * b + u
                        cos = bc(ROT[:, 0, u * BT:(u + 1) * BT], [[0, 2], [1, BT]])
                        sin = bc(ROT[:, 1, u * BT:(u + 1) * BT], [[0, 2], [1, BT]])
                        dve.wait_ge(s_pj, 2 * n + 1)
                        dve.tensor_tensor(t1[:, :, :], PS[:, 0:2, :], cos, ALU.mult).then_inc(s_rd, 1)
                        dve.tensor_tensor(t2[:, :, :], PS[:, 2:4, :], sin, ALU.mult).then_inc(s_rd, 1)
                        dve.wait_ge(s_rd, 2 * n + 2)
                        dve.wait_ge(s_h, 2 * n)
                        dve.tensor_tensor(qk[:, :, :], t1[:, :, :], t2[:, :, :], ALU.add).then_inc(s_qk, 1)
                        dve.wait_ge(s_h, 2 * n + 1)
                        dve.tensor_tensor(res[:, :, :], qk[:, :, :], parts[:, u, 0, :, :],
                                          ALU.subtract).then_inc(s_qk, 1)
                        dve.wait_ge(s_h, 2 * n + 2)
                        dve.tensor_tensor(parts[:, u, 2, :, :], res[:, :, :], parts[:, u, 1, :, :],
                                          ALU.subtract).then_inc(s_pt, 1)

            @block.scalar
            def _(act):
                with act.Fori(0, BATCH) as b:
                    for u in range(2):
                        n = 2 * b + u
                        act.wait_ge(s_pj, 2 * n)
                        act.activation(xs[:, u, :], XNT[:, bass.ds(BT * n, BT)], ACT.Copy).then_inc(s_xs, 1)
                        act.wait_ge(s_pj, 2 * n + 2)
                        act.wait_ge(s_vst, 16 * NG * n)
                        act.activation(vs[:, u, :, :], PS[:, 4, :].rearrange("p (j c) -> p j c", j=TPB),
                                       ACT.Copy).then_inc(s_v, 1)
                        act.wait_ge(s_qk, 2 * n + 1)
                        act.wait_ge(s_st, 16 * 2 * NG * n)
                        act.activation(parts[:, u, 0, :, :], qk[:, :, :], ACT.Copy).then_inc(s_h, 1)
                        act.wait_ge(s_qk, 2 * n + 2)
                        act.activation(parts[:, u, 1, :, :], res[:, :, :], ACT.Copy).then_inc(s_h, 1)


def rope_attention(nc, a, g):
    IDN, PS, QK, V, O = (g[k] for k in ("IDN", "PS", "QK", "V", "O"))
    ITERS = BATCH * NG
    STEPS = HALVES * KT
    TILES = GH * KT * HALVES
    SPREAD = 14
    LOADS = 2 * PARTS * PARTS
    with ExitStack() as ctx:
        sb, sem = stage(nc, ctx)
        Q = sb("ra_q", [P, 2, GH, SEQ], BF16)
        K = sb("ra_k", [P, 2, GH, SEQ], BF16)
        vc = sb("ra_vc", [P, 2, KT, GH * DH])
        VA = sb("ra_va", [P, 2, KT, GH, VW])
        PR = sb("ra_p", [P, 2, GH, BT])
        ot = sb("ra_ot", [P, HALVES, BT])
        mh = sb("ra_mh", [P, GH * KT, HALVES])
        m = sb("ra_m", [P, GH * KT])
        nm = sb("ra_nm", [GH * KT, P])
        nr = sb("ra_nr", [GH * KT, P])
        mp = sb("ra_mp", [GH * KT, 2, PARTS, P], BF16)
        s_qk = [sem(f"ra_qk_loaded{u}") for u in range(2)]
        s_vl = [sem(f"ra_v_loaded{u}") for u in range(2)]
        s_mr = [sem(f"ra_max_rows{u}") for u in range(2)]
        s_va, s_set, s_tile, s_max, s_mx, s_mp, s_st, s_exp, s_pv, s_of, s_os, s_ch = (
            sem("ra_" + n) for n in ("v_ready", "set", "tile_ready", "tile_read", "m_ready", "m_parts", "scores_ready",
                                     "exp_done", "pv_done", "o_free", "o_stored", "chain"))
        with nc.Block() as block:
            @block.sync
            def _(sp):
                def load(n, u):
                    for i in range(PARTS):
                        for k in range(PARTS):
                            r = (i * PARTS + k) * DH
                            sp.dma_start(Q[r:r + DH, u, :, :], QK[0, n, i].rearrange("(j d) s -> d j s", d=DH)).then_inc(s_qk[u], 16)
                            sp.dma_start(K[r:r + DH, u, :, :], QK[1, n, k].rearrange("(j d) s -> d j s", d=DH)).then_inc(s_qk[u], 16)
                    sp.dma_start(vc[:, u, :, :], V[n].rearrange("(t p) c -> p t c", p=P)).then_inc(s_vl[u], 16)

                def max_rows(n1, u):
                    sp.wait_ge(s_mp, n1)
                    for i in range(PARTS):
                        sp.dma_start(Q[KMAX + i:KMAX + i + 1, u, :, :].rearrange("o j (t p) -> o (j t) p", p=P),
                                     mp[:, u, i, :]).then_inc(s_mr[u], 16)

                sp.wait_ge(s_set, 5)
                load(0, 0)
                max_rows(1, 0)
                with sp.Fori(0, ITERS // 2) as it:
                    for u in range(2):
                        n = 2 * it + u
                        sp.wait_ge(s_pv, 2 * STEPS * n + 3)
                        load(n + 1 if u == 0 else (n + 1) % ITERS, 1 - u)
                        for qc in range(HALVES):
                            if qc == 1:
                                max_rows(n + 2, 1 - u)
                            sp.wait_ge(s_of, HALVES * n + qc + 1)
                            sp.dma_start(O[n, :, qc * BT:(qc + 1) * BT], ot[:, qc, :]).then_inc(s_os, 16)
                sp.wait_ge(s_os, 16 * HALVES * ITERS)
                sp.wait_ge(s_mr[0], 16 * PARTS * (ITERS // 2 + 1))

            @block.tensor
            def _(pe):
                def max_tile(n1, c, u):
                    j, t, h = c // (KT * HALVES), c // HALVES % KT, c % HALVES
                    pe.wait_ge(s_max, (TILES + 1) * n1 + c + (1 if c < 2 else 0))
                    pe.matmul(PS[:, 5 + c % 3, :], Q[0:KMAX, u, j, t * P:(t + 1) * P],
                              K[0:KMAX, u, j, h * BT:(h + 1) * BT], start=True, stop=True).then_inc(s_tile, 1)

                def turn_max(n1):
                    pe.wait_ge(s_mx, n1 + 1)
                    pe.transpose(PS[0:GH * KT, 5 + TILES % 3, 0:P], m[:, :], IDN[:, :]).then_inc(s_tile, 1)

                def scores(n, s, pair, u):
                    e = 2 * STEPS * n + 2 * s + pair
                    pe.wait_ge(s_exp, e)
                    for j in (2 * pair, 2 * pair + 1):
                        mm = pe.matmul(PS[:, j, :], K[0:KROWS, u, j, (s % KT) * P:(s % KT + 1) * P],
                                       Q[0:KROWS, u, j, (s // KT) * BT:(s // KT + 1) * BT], start=True, stop=True)
                    mm.then_inc(s_st, 1)

                def weigh(n, s, pair, u):
                    e = 2 * STEPS * n + 2 * s + pair
                    if s % KT == 0 and pair == 0:
                        pe.wait_ge(s_of, HALVES * n + s // KT)
                    pe.wait_ge(s_exp, e + 2)
                    for j in (2 * pair, 2 * pair + 1):
                        mm = pe.matmul(PS[32 * j:32 * j + VW, 4, :], VA[:, u, s % KT, j, :], PR[:, s % 2, j, :],
                                       start=(s % KT == 0), stop=(s % KT == KT - 1))
                    mm.then_inc(s_pv, 1)

                pe.wait_ge(s_set, 5)
                pe.wait_ge(s_qk[0], 16 * LOADS)
                for c in range(TILES):
                    max_tile(0, c, 0)
                turn_max(0)
                with pe.Fori(0, ITERS // 2) as it:
                    for u in range(2):
                        n = 2 * it + u
                        pe.wait_ge(s_mr[u], 16 * PARTS * (it + 1))
                        pe.wait_ge(s_va, n + 1)
                        done = 0
                        for s in range(STEPS):
                            for pair in range(2):
                                scores(n, s, pair, u)
                                if s:
                                    weigh(n, s - 1, pair, u)
                                if s == 0 and pair == 1:
                                    pe.wait_ge(s_qk[1 - u], 16 * LOADS * (it + 1 + u))
                                upto = min(TILES, TILES * (2 * s + pair) // (2 * SPREAD - 1))
                                while done < upto:
                                    max_tile(n + 1, done, 1 - u)
                                    done += 1
                        turn_max(n + 1)
                        for pair in range(2):
                            weigh(n, STEPS - 1, pair, u)

            @block.scalar
            def _(act):
                act.drain().then_inc(s_exp, 1)

                def values(u, loads):
                    act.wait_ge(s_vl[u], loads)
                    act.activation(VA[:, u, :, :, 0:DH], vc[:, u, :, :].rearrange("p t (j d) -> p t j d", j=GH),
                                   ACT.Copy).then_inc(s_va, 1)

                act.wait_ge(s_set, 5)
                values(0, 16)
                with act.Fori(0, ITERS // 2) as it:
                    for u in range(2):
                        n = 2 * it + u

                        def output(qc):
                            act.wait_ge(s_pv, 2 * STEPS * n + 2 * KT * (qc + 1) + 3)
                            act.wait_ge(s_os, 16 * (HALVES * n + qc - 1) if qc else 16 * HALVES * n)
                            act.activation(ot[:, qc, :], PS[:, 4, :], ACT.Copy).then_inc(s_of, 1)

                        for s in range(STEPS):
                            if s == KT + 1:
                                output(0)
                            if s == KT + 4:
                                values(1 - u, 16 * (it + 1 + u))
                            for pair in range(2):
                                e = 2 * STEPS * n + 2 * s + pair
                                act.wait_ge(s_st, e + 1)
                                act.wait_ge(s_pv, e)
                                act.activation(PR[:, s % 2, 2 * pair:2 * pair + 2, :], PS[:, 2 * pair:2 * pair + 2, :],
                                               ACT.Exp, scale=float(DH) ** -0.5).then_inc(s_exp, 1)
                        output(1)

            @block.vector
            def _(dve):
                dve.memset(Q[64:128, :, :, :], 0.0).then_inc(s_set, 1)
                dve.memset(K[64:96, :, :, :], 0.0).then_inc(s_set, 1)
                dve.memset(K[96:128, :, :, :], 1.0).then_inc(s_set, 1)
                dve.memset(VA[:, :, :, :, :], 0.0).then_inc(s_set, 1)
                dve.wait_ge(s_set, 4)
                dve.memset(VA[:, :, :, :, DH:DH + 1], 1.0).then_inc(s_set, 1)
                dve.drain().then_inc(s_max, 2)
                dve.drain().then_inc(s_pv, 3)

                def maxima(n1, u, rows):
                    for c in range(TILES):
                        dve.wait_ge(s_tile, (TILES + 1) * n1 + c + 1)
                        dve.tensor_reduce(mh[:, c // HALVES, c % HALVES:c % HALVES + 1], PS[:, 5 + c % 3, :],
                                          AX.X, ALU.max).then_inc(s_max, 1)
                    dve.wait_ge(s_max, (TILES + 1) * n1 + TILES + 2)
                    dve.tensor_reduce(m[:, :], mh[:, :, :], AX.X, ALU.max).then_inc(s_mx, 1)
                    dve.wait_ge(s_tile, (TILES + 1) * (n1 + 1))
                    dve.tensor_scalar(nm[:, :], PS[0:GH * KT, 5 + TILES % 3, 0:P], -1.0, None, ALU.mult).then_inc(s_max, 1)
                    dve.wait_ge(s_max, (TILES + 1) * (n1 + 1) + 2)
                    dve.wait_ge(s_mr[u], rows)
                    ch = Chain(dve, s_ch, 3 * n1)
                    ch.link(dve.tensor_copy(mp[:, u, 0, :], nm[:, :]))
                    ch.link(dve.tensor_tensor(nr[:, :], nm[:, :], mp[:, u, 0, :], ALU.subtract))
                    ch.link(dve.tensor_copy(mp[:, u, 1, :], nr[:, :]))
                    dve.tensor_tensor(mp[:, u, 2, :], nr[:, :], mp[:, u, 1, :], ALU.subtract).then_inc(s_mp, 1)

                maxima(0, 0, 0)
                with dve.Fori(0, ITERS // 2) as it:
                    maxima(2 * it + 1, 1, 16 * PARTS * it)
                    maxima(2 * it + 2, 0, 16 * PARTS * (it + 1))


def broadcast_rows(ap, parts, n):
    return bass.AP(ap.tensor, ap.offset, [[0, parts], [1, n]])


def top2(dve, ch, p, w, lower, t1, t2, rank, n, e):
    def axes(ap, d):
        return bc(ap, [[e, n], d[0], d[1]])
    mine, other = axes(p, ([1, e], [0, e])), axes(p, ([0, e], [1, e]))
    ch.tick(dve.tensor_tensor(t1, other, mine, ALU.is_gt))
    ch.link(dve.tensor_tensor(t2, other, mine, ALU.is_equal))
    ch.link(dve.tensor_tensor(t2, t2, bc(lower, [[0, n], [e, e], [1, e]]), ALU.mult))
    ch.link(dve.tensor_tensor(t1, t1, t2, ALU.add))
    ch.link(dve.tensor_reduce(rank, t1, AX.X, ALU.add))
    ch.link(dve.scalar_tensor_tensor(w, rank, 1.5, p, ALU.is_lt, ALU.mult))


def ffn0(nc, a, g):
    with ExitStack() as ctx:
        sb, sem = stage(nc, ctx)
        LG = sb("f0_lg", [P, NT, GA + E0])
        W = sb("f0_w", [P, NT, E0])
        attention_output(nc, a, g, LG)
        route0(nc, a, LG, W)
        experts0(nc, a, g, W)


def attention_output(nc, a, g, LG):
    XN, XNT, IDN, PS, PW, O = (g[k] for k in ("XN", "XNT", "IDN", "PS", "PW", "O"))
    G = GA + E0
    with ExitStack() as ctx:
        sb, sem = stage(nc, ctx)
        wo = sb("ao_wo", [P, D])
        wg = sb("ao_wg", [P, G])
        gb = sb("ao_gb", [P, G])
        n1 = sb("ao_n1", [P, D])
        ot = sb("ao_ot", [P, 2, NG, BT])
        rc = sb("ao_rc", [P, TPB * H0])
        sa = sb("ao_sa", [P, TPB, D])
        saT = sb("ao_saT", [P, BT])
        y = sb("ao_y", [P, TPB, D])
        sq = sb("ao_sq", [P, TPB, D])
        ss = sb("ao_ss", [P, TPB])
        ms = sb("ao_ms", [P, TPB])
        r = sb("ao_r", [P, TPB])
        x1 = sb("ao_x1", [P, TPB, D])
        x1T = sb("ao_x1T", [P, BT])
        s_ot = [sem(f"ao_o_loaded{u}") for u in range(2)]
        s_w, s_o, s_rc, s_sa, s_saT, s_T, s_pr, s_y, s_ss, s_ms, s_r, s_x1, s_x1T, s_cp, s_lt, s_lg = (
            sem("ao_" + n) for n in ("weights", "o_turned", "recip", "normalised", "sa_turned", "saT_ready",
                                     "projected", "y_ready", "squares", "mean", "rms", "x1_ready", "x1_turned",
                                     "copied", "logits", "logits_read"))
        with nc.Block() as block:
            @block.sync
            def _(sp):
                sp.dma_start(wo[:, :], a["L0_ffn_Wo"]).then_inc(s_w, 16)
                sp.dma_start(wg[:, 0:GA], a["L0_ffn_Wg_gate"]).then_inc(s_w, 16)
                sp.dma_start(wg[:, GA:G], a["L0_ffn_We_gate"]).then_inc(s_w, 16)
                sp.dma_start(gb[:, 0:GA], broadcast_rows(a["L0_ffn_group_bias"], P, GA)).then_inc(s_w, 16)
                sp.dma_start(gb[:, GA:G], broadcast_rows(a["L0_ffn_expert_bias"], P, E0)).then_inc(s_w, 16)
                sp.dma_start(n1[:, :], broadcast_rows(a["L0_ffn_norm1_w"], P, D)).then_inc(s_w, 16)
                with sp.Fori(0, BATCH) as b:
                    for u in range(2):
                        sp.wait_ge(s_o, 2 * b)
                        sp.dma_start(ot[:, u, :, :], O[bass.ds(NG * b, NG), :, u * BT:(u + 1) * BT].rearrange(
                            "g p s -> p g s")).then_inc(s_ot[u], 16)

            @block.tensor
            def _(pe):
                pe.wait_ge(s_w, 96)
                with pe.Fori(0, BATCH) as b:
                    for u in range(2):
                        n = 2 * b + u
                        pe.wait_ge(s_ot[u], 16 * (b + 1))
                        pe.wait_ge(s_sa, n)
                        for j in range(TPB):
                            for gi in range(NG):
                                mm = pe.transpose(PS[:, j, gi * P:(gi + 1) * P], ot[:, u, gi, j * P:(j + 1) * P], IDN[:, :])
                        mm.then_inc(s_o, 1)
                        pe.wait_ge(s_sa, n + 1)
                        for j in range(TPB):
                            mm = pe.transpose(PS[:, 4, j * P:(j + 1) * P], sa[:, j, :], IDN[:, :])
                        mm.then_inc(s_saT, 1)
                        pe.wait_ge(s_T, n + 1)
                        for j in range(TPB):
                            mm = pe.matmul(PS[:, 5, j * P:(j + 1) * P], saT[:, j * P:(j + 1) * P], wo[:, :],
                                           start=True, stop=True)
                        mm.then_inc(s_pr, 1)
                        pe.wait_ge(s_x1, TPB * (n + 1))
                        for j in range(TPB):
                            mm = pe.transpose(PS[:, 6, j * P:(j + 1) * P], x1[:, j, :], IDN[:, :])
                        mm.then_inc(s_x1T, 1)
                        pe.wait_ge(s_cp, 3 * n + 2)
                        for j in range(TPB):
                            mm = pe.matmul(PS[:, 7, j * G:(j + 1) * G], x1T[:, j * P:(j + 1) * P], wg[:, :],
                                           start=True, stop=True)
                        mm.then_inc(s_lt, 1)

            @block.vector
            def _(dve):
                dve.wait_ge(s_w, 96)
                heads = PS[:, 0:TPB, :].rearrange("p j (h c) -> p (j h) c", c=VW)
                with dve.Fori(0, BATCH) as b:
                    for u in range(2):
                        n = 2 * b + u
                        dve.wait_ge(s_o, n + 1)
                        dve.reciprocal(rc[:, :], heads[:, :, DH]).then_inc(s_rc, 1)
                        dve.wait_ge(s_rc, n + 1)
                        dve.tensor_tensor(sa[:, :, :].rearrange("p j (h d) -> p (j h) d", d=DH), heads[:, :, 0:DH],
                                          bc(rc[:, :], [[1, TPB * H0], [0, DH]]), ALU.mult).then_inc(s_sa, 1)
                        dve.wait_ge(s_pr, n + 1)
                        dve.tensor_tensor(y[:, :, :], PS[:, 5, :].rearrange("p (j c) -> p j c", j=TPB),
                                          XN[:, bass.ds(TPB * n, TPB), :], ALU.add).then_inc(s_y, 1)
                        dve.wait_ge(s_ss, TPB * (n + 1))
                        dve.tensor_scalar(ms[:, :], ss[:, :], 1.0 / D, RMS_EPS, ALU.mult, ALU.add).then_inc(s_ms, 1)
                        dve.wait_ge(s_r, n + 1)
                        for j in range(TPB):
                            dve.scalar_tensor_tensor(x1[:, j, :], y[:, j, :], r[:, j:j + 1], n1[:, :],
                                                     ALU.mult, ALU.mult).then_inc(s_x1, 1)
                        dve.wait_ge(s_lt, n + 1)
                        dve.tensor_tensor(LG[:, bass.ds(TPB * n, TPB), :],
                                          PS[:, 7, 0:TPB * G].rearrange("p (j c) -> p j c", j=TPB),
                                          bc(gb[:, :], [[0, TPB], [1, G]]), ALU.add).then_inc(s_lg, 1)

            @block.gpsimd
            def _(pool):
                with pool.Fori(0, NBLK) as n:
                    pool.wait_ge(s_ms, n + 1)
                    pool.tensor_tensor(r[:, :], ms[:, :], PW[:, :], ALU.pow).then_inc(s_r, 1)

            @block.scalar
            def _(act):
                with act.Fori(0, NBLK) as n:
                    act.wait_ge(s_saT, n + 1)
                    act.activation(saT[:, :], PS[:, 4, :], ACT.Copy).then_inc(s_T, 1)
                    act.wait_ge(s_y, n + 1)
                    for j in range(TPB):
                        act.activation(sq[:, j, :], y[:, j, :], ACT.Square, accum_out=ss[:, j:j + 1]).then_inc(s_ss, 1)
                    act.wait_ge(s_x1, TPB * (n + 1))
                    act.activation(XN[:, bass.ds(TPB * n, TPB), :], x1[:, :, :], ACT.Copy).then_inc(s_cp, 1)
                    act.wait_ge(s_x1T, n + 1)
                    act.activation(x1T[:, :], PS[:, 6, :], ACT.Copy).then_inc(s_cp, 1)
                    act.wait_ge(s_cp, 3 * n + 2)
                    act.activation(XNT[:, bass.ds(BT * n, BT)], x1T[:, :], ACT.Copy).then_inc(s_cp, 1)


def route0(nc, a, LG, W):
    with ExitStack() as ctx:
        sb, sem = stage(nc, ctx)
        low = sb("r0_low", [P, E0 * E0])
        gm = sb("r0_gm", [P, NT])
        ge = sb("r0_ge", [P, NT, GA])
        gs = sb("r0_gs", [P, NT])
        gp = sb("r0_gp", [P, NT])
        em = sb("r0_em", [P, NT * GA])
        ee = sb("r0_ee", [P, NT * GA, EPG])
        es = sb("r0_es", [P, NT * GA])
        er = sb("r0_er", [P, NT, GA])
        mg = sb("r0_mg", [P, NT, GA])
        p = sb("r0_p", [P, NT, E0])
        t1 = sb("r0_t1", [P, NT, E0, E0])
        t2 = sb("r0_t2", [P, NT, E0, E0])
        rank = sb("r0_rank", [P, NT, E0])
        s_l, s_d, s_e, s_c = (sem("r0_" + n) for n in ("loaded", "differences", "exps", "chain"))
        with nc.Block() as block:
            @block.sync
            def _(sp):
                sp.dma_start(low[:, :], broadcast_rows(a["c_lower0"], P, E0 * E0)).then_inc(s_l, 16)
                sp.wait_ge(s_l, 16)

            @block.scalar
            def _(act):
                act.wait_ge(s_d, 2)
                act.activation(ge[:, :, :], ge[:, :, :], ACT.Exp).then_inc(s_e, 1)
                act.activation(ee[:, :, :], ee[:, :, :], ACT.Exp).then_inc(s_e, 1)

            @block.vector
            def _(dve):
                ch = Chain(dve, s_c)
                gl = LG[:, :, 0:GA]
                el = bc(LG[:, :, GA:GA + E0], [[GA + E0, NT], [EPG, GA], [1, EPG]])
                ch.tick(dve.tensor_reduce(gm[:, :], gl, AX.X, ALU.max))
                ch.link(dve.tensor_reduce(em[:, :].rearrange("p (n g) -> p n g", g=GA), el, AX.X, ALU.max))
                dve.tensor_tensor(ge[:, :, :], gl, bc(gm[:, :], [[1, NT], [0, GA]]), ALU.subtract).then_inc(s_d, 1)
                dve.tensor_tensor(ee[:, :, :].rearrange("p (n g) e -> p n g e", g=GA), el,
                                  bc(em[:, :], [[GA, NT], [1, GA], [0, EPG]]), ALU.subtract).then_inc(s_d, 1)
                dve.wait_ge(s_e, 2)
                ch.tick(dve.tensor_reduce(gs[:, :], ge[:, :, :], AX.X, ALU.add))
                ch.tick(dve.tensor_reduce(es[:, :], ee[:, :, :], AX.X, ALU.add))
                ch.link(dve.tensor_tensor(mg[:, :, 1], ge[:, :, 1], ge[:, :, 0], ALU.is_gt))
                ch.tick(dve.tensor_scalar(mg[:, :, 0], mg[:, :, 1], -1.0, 1.0, ALU.mult, ALU.add))
                ch.tick(dve.reciprocal(gp[:, :], gs[:, :]))
                ch.link(dve.reciprocal(er[:, :, :].rearrange("p n g -> p (n g)"), es[:, :]))
                ch.link(dve.tensor_tensor(er[:, :, :], er[:, :, :], mg[:, :, :], ALU.mult))
                ch.link(dve.tensor_tensor(p[:, :, :].rearrange("p n (g e) -> p (n g) e", g=GA), ee[:, :, :],
                                          bc(er[:, :, :], [[1, NT * GA], [0, EPG]]), ALU.mult))
                ch.link(dve.tensor_tensor(p[:, :, :], p[:, :, :], bc(gp[:, :], [[1, NT], [0, E0]]), ALU.mult))
                dve.wait_ge(s_l, 16)
                top2(dve, ch, p[:, :, :], W[:, :, :], low[:, :], t1[:, :, :, :], t2[:, :, :, :], rank[:, :, :], NT, E0)


def experts0(nc, a, g, W):
    X, XN, XNT, PS, PW = (g[k] for k in ("X", "XN", "XNT", "PS", "PW"))
    FT = HID // P
    EB = BT // D
    HB = E0 // EB
    with ExitStack() as ctx:
        sb, sem = stage(nc, ctx)
        wi = sb("e0_wi", [P, 2, 2 * HID])
        ws = sb("e0_ws", [P, FT, D])
        w2 = sb("e0_w2", [P, FT, E0, D])
        n2 = sb("e0_n2", [P, D])
        sg = sb("e0_sg", [P, 2, FT, BT])
        hT = sb("e0_hT", [P, 2, FT, BT])
        acc = sb("e0_acc", [P, TPB, D])
        y = sb("e0_y", [P, TPB, D])
        sq = sb("e0_sq", [P, TPB, D])
        ss = sb("e0_ss", [P, TPB])
        ms = sb("e0_ms", [P, TPB])
        r = sb("e0_r", [P, TPB])
        z = sb("e0_z", [P, TPB, D])
        s_w, s_up, s_sg, s_h, s_dn, s_sh, s_ac, s_y, s_ss, s_ms, s_r, s_z, s_n2 = (
            sem("e0_" + n) for n in ("weights", "up_done", "silu_done", "hidden", "down_done", "shared_done", "combined",
                                     "y_ready", "squares", "mean", "rms", "z_ready", "norm_halved"))
        with nc.Block() as block:
            @block.sync
            def _(sp):
                sp.dma_start(wi[:, 0, :], a["L0_ffn_W_shared_in"]).then_inc(s_w, 16)
                sp.dma_start(wi[:, 1, :], a["L0_ffn_W1_shared"]).then_inc(s_w, 16)
                sp.dma_start(ws[:, :, :], a["L0_ffn_W_shared_out"].rearrange("(f p) d -> p f d", p=P)).then_inc(s_w, 16)
                for f in range(FT):
                    sp.dma_start(w2[:, f, :, :], a["L0_ffn_W2_experts"][:, f * P:(f + 1) * P, :].rearrange(
                        "e p d -> p e d")).then_inc(s_w, 16)
                sp.dma_start(n2[:, :], broadcast_rows(a["L0_ffn_norm2_w"], P, D)).then_inc(s_w, 16)
                sp.wait_ge(s_w, 96)

            @block.tensor
            def _(pe):
                pe.wait_ge(s_w, 96)
                with pe.Fori(0, NBLK) as n:
                    pe.wait_ge(s_ac, TPB * E0 * n)
                    pe.wait_ge(s_y, n)
                    for k in range(2):
                        for c in range(2 * FT):
                            mm = pe.matmul(PS[:, 2 * FT * k + c, :], wi[:, k, c * P:(c + 1) * P],
                                           XNT[:, bass.ds(BT * n, BT)], start=True, stop=True)
                        mm.then_inc(s_up, 1)
                    pe.wait_ge(s_h, 2 * n + 1)
                    for j in range(TPB):
                        for f in range(FT):
                            mm = pe.matmul(PS[:, 2, j * P:(j + 1) * P], hT[:, 0, f, j * P:(j + 1) * P], ws[:, f, :],
                                           start=(f == 0), stop=(f == FT - 1))
                    mm.then_inc(s_sh, 1)
                    pe.wait_ge(s_h, 2 * n + 2)
                    for j in range(TPB):
                        for h in range(HB):
                            if j:
                                pe.wait_ge(s_ac, E0 * (TPB * n + j - 1) + EB * (h + 1))
                            for f in range(FT):
                                mm = pe.matmul(PS[:, h, :], hT[:, 1, f, j * P:(j + 1) * P],
                                               w2[:, f, h * EB:(h + 1) * EB, :], start=(f == 0), stop=(f == FT - 1))
                            mm.then_inc(s_dn, 1)

            @block.scalar
            def _(act):
                with act.Fori(0, NBLK) as n:
                    for k in range(2):
                        act.wait_ge(s_up, 2 * n + k + 1)
                        act.wait_ge(s_h, 2 * n)
                        act.activation(sg[:, k, :, :], PS[:, 2 * FT * k:2 * FT * k + FT, :], ACT.Silu).then_inc(s_sg, 1)
                    act.wait_ge(s_y, n + 1)
                    for j in range(TPB):
                        act.activation(sq[:, j, :], y[:, j, :], ACT.Square, accum_out=ss[:, j:j + 1]).then_inc(s_ss, 1)

            @block.gpsimd
            def _(pool):
                with pool.Fori(0, NBLK) as n:
                    pool.wait_ge(s_ms, n + 1)
                    pool.tensor_tensor(r[:, :], ms[:, :], PW[:, :], ALU.pow).then_inc(s_r, 1)

            @block.vector
            def _(dve):
                dve.wait_ge(s_w, 96)
                dve.tensor_scalar(n2[:, :], n2[:, :], 0.5, None, ALU.mult).then_inc(s_n2, 1)
                dve.wait_ge(s_n2, 1)
                with dve.Fori(0, NBLK) as n:
                    for k in range(2):
                        dve.wait_ge(s_sg, 2 * n + k + 1)
                        dve.wait_ge(s_dn, TPB * HB * n)
                        dve.tensor_tensor(hT[:, k, :, :], sg[:, k, :, :],
                                          PS[:, 2 * FT * k + FT:2 * FT * (k + 1), :], ALU.mult).then_inc(s_h, 1)
                    for j in range(TPB):
                        for x in range(E0):
                            if x % EB == 0:
                                dve.wait_ge(s_dn, HB * (TPB * n + j) + x // EB + 1)
                            if x:
                                dve.wait_ge(s_ac, E0 * (TPB * n + j) + x)
                            dve.scalar_tensor_tensor(
                                acc[:, j, :], PS[:, x // EB, x % EB * D:(x % EB + 1) * D], W[:, TPB * n + j, x:x + 1],
                                acc[:, j, :] if x else XN[:, TPB * n + j, :], ALU.mult, ALU.add).then_inc(s_ac, 1)
                    dve.wait_ge(s_ac, E0 * TPB * (n + 1))
                    dve.wait_ge(s_sh, n + 1)
                    dve.tensor_tensor(y[:, :, :], PS[:, 2, :].rearrange("p (j c) -> p j c", j=TPB), acc[:, :, :],
                                      ALU.add).then_inc(s_y, 1)
                    dve.wait_ge(s_ss, TPB * (n + 1))
                    dve.tensor_scalar(ms[:, :], ss[:, :], 1.0 / D, RMS_EPS, ALU.mult, ALU.add).then_inc(s_ms, 1)
                    dve.wait_ge(s_r, n + 1)
                    for j in range(TPB):
                        dve.scalar_tensor_tensor(z[:, j, :], y[:, j, :], r[:, j:j + 1], n2[:, :],
                                                 ALU.mult, ALU.mult).then_inc(s_z, 1)
                    dve.wait_ge(s_z, TPB * (n + 1))
                    dve.tensor_tensor(X[:, bass.ds(TPB * n, TPB), :], X[:, bass.ds(TPB * n, TPB), :], z[:, :, :],
                                      ALU.add)


def linear_attention(nc, a, g):
    X, XNT, IDN, PS = (g[k] for k in ("X", "XNT", "IDN", "PS"))
    C = H1 * HD
    CB = C // BT
    PB = BT // P
    with ExitStack() as ctx:
        sb, sem = stage(nc, ctx)
        wq, wk, wv = (sb("la_w" + c, [P, C]) for c in "qkv")
        wo = sb("la_wo", [P, NP, D])
        bq = sb("la_bq", [P, NP])
        bo = sb("la_bo", [P, 1])
        bkv = sb("la_bkv", [P, 2, C])
        ones = sb("la_ones", [P, VW])
        sel = sb("la_sel", [P, NP, P])
        rows = sb("la_rows", [P, NP // PB, VW])
        blocks = sb("la_blocks", [P, P])
        xs = sb("la_xs", [P, SEQ])
        tk = sb("la_tk", [P, 2, C])
        ek = sb("la_ek", [P, 2, C])
        km = sb("la_km", [P, 2, C])
        vt = sb("la_vt", [P, 2, C])
        kvs = sb("la_kvs", [P, NP, P])
        ksr = sb("la_ksr", [VW, C])
        ksm = sb("la_ksm", [P, NP, VW])
        G = sb("la_g", [P, NP, D])
        eq = sb("la_eq", [P, 2, BT])
        rq = sb("la_rq", [P, 2, BT])
        qm = sb("la_qm", [P, NP, BT])
        de = sb("la_de", [P, BT])
        z = sb("la_z", [P, BT])
        oT = sb("la_oT", [P, BT])
        (s_w, s_one, s_x, s_pj, s_rd, s_ex, s_re, s_km, s_kv, s_ks, s_kst, s_ksm, s_gm, s_g, s_q, s_eq, s_qm, s_dn, s_de,
         s_z, s_zb, s_zq, s_o, s_oT, s_t, s_add) = (sem("la_" + n) for n in (
             "weights", "ones", "x_ready", "projected", "psum_read", "exp_k", "relu_k", "k_ready", "kv_done", "kv_masked",
             "sums_turned", "sums_masked", "g_done", "g_copied", "q_done", "exp_relu_q", "q_ready", "denominators",
             "eps_added", "z_ready", "z_spread", "q_scaled", "output", "output_copied", "output_turned", "added"))
        with nc.Block() as block:
            @block.sync
            def _(sp):
                for w, name in ((wq, "wq"), (wk, "wk"), (wv, "wv")):
                    sp.dma_start(w[:, :], a["L0_attn_" + name].rearrange("f h d -> f (h d)")).then_inc(s_w, 16)
                sp.dma_start(wo[:, :, :], a["L0_attn_wo"].rearrange("(p h) m f -> (h m) p f", h=2)).then_inc(s_w, 16)
                sp.dma_start(bq[:, :], a["L0_attn_bq"].rearrange("(p h) d -> (h d) p", h=2),
                             allow_slow_non_contiguous=True).then_inc(s_w, 16)
                sp.dma_start(bo[:, :], a["L0_attn_bo"].rearrange("(f o) -> f o", o=1),
                             allow_slow_non_contiguous=True).then_inc(s_w, 16)
                sp.dma_start(bkv[:, 0, :], broadcast_rows(a["L0_attn_bk"], P, C)).then_inc(s_w, 16)
                sp.dma_start(bkv[:, 1, :], broadcast_rows(a["L0_attn_bv"], P, C)).then_inc(s_w, 16)
                sp.dma_start(sel[:, :, :], a["c_spread"]).then_inc(s_w, 16)
                sp.dma_start(rows[:, :, :], a["c_rows"]).then_inc(s_w, 16)
                sp.dma_start(blocks[:, :], a["c_blocks"]).then_inc(s_w, 16)
                sp.wait_ge(s_w, 11 * 16)

            @block.tensor
            def _(pe):
                pe.wait_ge(s_w, 11 * 16)
                pe.wait_ge(s_one, 1)
                with pe.Fori(0, BATCH) as b:
                    pe.wait_ge(s_x, b + 1)

                    def project(t):
                        pe.wait_ge(s_rd, 2 * (KT * b + t))
                        for k, w in enumerate((wk, wv)):
                            for c in range(CB):
                                mm = pe.matmul(PS[:, CB * k + c, :], xs[:, t * P:(t + 1) * P], w[:, c * BT:(c + 1) * BT],
                                               start=True, stop=True)
                            mm.then_inc(s_pj, 1)

                    def gather(t):
                        pe.wait_ge(s_km, KT * b + t + 1)
                        for p in range(NP):
                            pe.matmul(PS[:, 4 + p // PB, p % PB * P:(p % PB + 1) * P], vt[:, t % 2, p * P:(p + 1) * P],
                                      km[:, t % 2, p * P:(p + 1) * P], start=(t == 0 and p % PB == 0),
                                      stop=(t == KT - 1), skip_group_check=True)
                        for c in range(CB):
                            mm = pe.matmul(PS[0:VW, 6 + c, :], ones[:, :], km[:, t % 2, c * BT:(c + 1) * BT],
                                           start=(t == 0), stop=(t == KT - 1))
                        mm.then_inc(s_kv, 1)

                    project(0)
                    for t in range(KT):
                        if t + 1 < KT:
                            project(t + 1)
                        gather(t)
                    pe.wait_ge(s_ks, 2 * b + 2)
                    for p in range(NP):
                        mm = pe.matmul(PS[:, 1 + p // PB, p % PB * P:(p % PB + 1) * P], kvs[:, p, :], wo[:, p, :],
                                       start=True, stop=True)
                    mm.then_inc(s_gm, 1)
                    for p in range(NP):
                        mm = pe.transpose(PS[:, 0, p * VW:(p + 1) * VW], ksr[:, p * P:(p + 1) * P], IDN[0:VW, 0:VW])
                    mm.then_inc(s_kst, 1)
                    pe.wait_ge(s_g, b + 1)
                    pe.wait_ge(s_ksm, b + 1)
                    for c in range(HALVES):
                        n = HALVES * b + c
                        for p in range(NP):
                            if p >= 2 or c:
                                pe.wait_ge(s_qm, NP * n + p - 1)
                            pe.matmul(PS[:, p % 2, :], wq[:, p * P:(p + 1) * P], xs[:, c * BT:(c + 1) * BT],
                                      start=True, stop=True).then_inc(s_q, 1)
                        pe.wait_ge(s_qm, NP * (n + 1))
                        for p in range(NP):
                            r = 32 * (p % PB)
                            mm = pe.matmul(PS[r:r + VW, 4, :], ksm[:, p, :], qm[:, p, :], start=(p < PB), stop=(p >= PB))
                        mm.then_inc(s_dn, 1)
                        pe.wait_ge(s_z, n + 1)
                        for p in range(NP + 1):
                            if p < NP:
                                if p >= 2:
                                    pe.wait_ge(s_zq, NP * n + p - 1)
                                pe.matmul(PS[:, 5 + p % 2, :], sel[:, p, :], z[:, :], start=True, stop=True).then_inc(s_zb, 1)
                            if p:
                                pe.wait_ge(s_zq, NP * n + p)
                                mm = pe.matmul(PS[:, 7, :], G[:, p - 1, :], qm[:, p - 1, :], start=(p == 1), stop=(p == NP))
                        mm.then_inc(s_o, 1)
                        pe.wait_ge(s_oT, n + 1)
                        for j in range(TPB):
                            mm = pe.transpose(PS[:, 3, j * P:(j + 1) * P], oT[:, j * P:(j + 1) * P], IDN[:, :])
                        mm.then_inc(s_t, 1)
                    pe.wait_ge(s_add, HALVES * (b + 1))

            @block.scalar
            def _(act):
                act.wait_ge(s_w, 11 * 16)
                with act.Fori(0, BATCH) as b:
                    act.wait_ge(s_o, HALVES * b)
                    act.activation(xs[:, :], XNT[:, bass.ds(SEQ * b, SEQ)], ACT.Copy).then_inc(s_x, 1)
                    for t in range(KT):
                        i = KT * b + t
                        act.wait_ge(s_rd, 2 * i + 1)
                        act.activation(ek[:, t % 2, :], tk[:, t % 2, :], ACT.Exp).then_inc(s_ex, 1)
                        act.wait_ge(s_ex, i + 1)
                        act.wait_ge(s_kv, i - 1) if t >= 2 else act.wait_ge(s_kv, KT * b)
                        act.activation(km[:, t % 2, :], tk[:, t % 2, :], ACT.Relu).then_inc(s_re, 1)
                    act.wait_ge(s_gm, b + 1)
                    act.activation(G[:, :, :], PS[:, 1:3, :].rearrange("p k (q f) -> p (k q) f", f=D), ACT.Copy).then_inc(s_g, 1)
                    for c in range(HALVES):
                        n = HALVES * b + c
                        for p in range(NP):
                            act.wait_ge(s_q, NP * n + p + 1)
                            if p >= 2 or c:
                                act.wait_ge(s_qm, NP * n + p - 1)
                            act.activation(eq[:, p % 2, :], PS[:, p % 2, :], ACT.Exp, bias=bq[:, p:p + 1]).then_inc(s_eq, 1)
                            act.activation(rq[:, p % 2, :], PS[:, p % 2, :], ACT.Relu, bias=bq[:, p:p + 1]).then_inc(s_eq, 1)
                        act.wait_ge(s_o, n + 1)
                        act.activation(oT[:, :], PS[:, 7, :], ACT.Identity, bias=bo[:, 0:1]).then_inc(s_oT, 1)

            @block.vector
            def _(dve):
                dve.memset(ones[:, :], 1.0).then_inc(s_one, 1)
                dve.wait_ge(s_w, 11 * 16)
                with dve.Fori(0, BATCH) as b:
                    for t in range(KT + 1):
                        i = KT * b + t
                        if t < KT:
                            dve.wait_ge(s_pj, 2 * i + 1)
                            dve.tensor_tensor(tk[:, t % 2, :].rearrange("p (k c) -> p k c", k=CB), PS[:, 0:CB, :],
                                              bkv[:, 0, :].rearrange("p (k c) -> p k c", k=CB), ALU.add).then_inc(s_rd, 1)
                            dve.wait_ge(s_pj, 2 * i + 2)
                            dve.wait_ge(s_kv, i - 1) if t >= 2 else dve.wait_ge(s_kv, KT * b)
                            dve.tensor_tensor(vt[:, t % 2, :].rearrange("p (k c) -> p k c", k=CB), PS[:, CB:2 * CB, :],
                                              bkv[:, 1, :].rearrange("p (k c) -> p k c", k=CB), ALU.add).then_inc(s_rd, 1)
                        if t:
                            dve.wait_ge(s_rd, 2 * i)
                            dve.wait_ge(s_re, i)
                            dve.scalar_tensor_tensor(km[:, (t - 1) % 2, :], ek[:, (t - 1) % 2, :], 1.0,
                                                     km[:, (t - 1) % 2, :], ALU.min, ALU.add).then_inc(s_km, 1)
                    dve.wait_ge(s_kv, KT * (b + 1))
                    dve.tensor_copy(ksr[:, :].rearrange("p (k c) -> p k c", k=CB), PS[0:VW, 6:8, :]).then_inc(s_ks, 1)
                    dve.tensor_tensor(kvs[:, :, :], PS[:, 4:6, :].rearrange("p k (q d) -> p (k q) d", d=P),
                                      bc(blocks[:, :], [[0, NP], [1, P]]), ALU.mult).then_inc(s_ks, 1)
                    dve.wait_ge(s_kst, b + 1)
                    dve.tensor_tensor(ksm[:, :, :].rearrange("p (k q) c -> p k q c", q=PB),
                                      PS[:, 0, 0:NP * VW].rearrange("p (k q c) -> p k q c", q=PB, c=VW),
                                      bc(rows[:, :, :], [[VW, NP // PB], [0, PB], [1, VW]]), ALU.mult).then_inc(s_ksm, 1)
                    for c in range(HALVES):
                        n = HALVES * b + c
                        for p in range(NP):
                            dve.wait_ge(s_eq, 2 * (NP * n + p + 1))
                            if p == 0 and c:
                                dve.wait_ge(s_o, n)
                            dve.scalar_tensor_tensor(qm[:, p, :], eq[:, p % 2, :], 1.0, rq[:, p % 2, :],
                                                     ALU.min, ALU.add).then_inc(s_qm, 1)
                        dve.wait_ge(s_dn, n + 1)
                        dve.tensor_scalar(de[:, :], PS[:, 4, :], LIN_EPS, None, ALU.add).then_inc(s_de, 1)
                        dve.wait_ge(s_de, n + 1)
                        dve.reciprocal(z[:, :], de[:, :]).then_inc(s_z, 1)
                        for p in range(NP):
                            dve.wait_ge(s_zb, NP * n + p + 1)
                            dve.tensor_tensor(qm[:, p, :], qm[:, p, :], PS[:, 5 + p % 2, :], ALU.mult).then_inc(s_zq, 1)
                        dve.wait_ge(s_t, n + 1)
                        dve.tensor_tensor(X[:, bass.ds(TPB * n, TPB), :], X[:, bass.ds(TPB * n, TPB), :],
                                          PS[:, 3, :].rearrange("p (j c) -> p j c", j=TPB), ALU.add).then_inc(s_add, 1)


def ffn1(nc, a, g):
    with ExitStack() as ctx:
        sb, sem = stage(nc, ctx)
        LG = sb("f1_lg", [P, NT, E1])
        W = sb("f1_w", [P, NT, E1])
        gates1(nc, a, g, LG)
        route1(nc, a, LG, W)
        experts1(nc, a, g, W)


def gates1(nc, a, g, LG):
    XNT, IDN, PS = (g[k] for k in ("XNT", "IDN", "PS"))
    with ExitStack() as ctx:
        sb, sem = stage(nc, ctx)
        gw = sb("g1_gw", [E1, P])
        gT = sb("g1_gT", [P, E1])
        xs = sb("g1_xs", [P, 2, BT])
        s_w, s_t, s_g, s_x, s_l, s_r = (sem("g1_" + n) for n in ("weights", "turned", "gates", "x_ready", "logits", "read"))
        with nc.Block() as block:
            @block.sync
            def _(sp):
                sp.dma_start(gw[:, :], a["L1_ffn_gate_w"]).then_inc(s_w, 16)
                sp.wait_ge(s_w, 16)

            @block.tensor
            def _(pe):
                pe.wait_ge(s_w, 16)
                pe.transpose(PS[:, 7, 0:E1], gw[:, :], IDN[0:E1, 0:E1]).then_inc(s_t, 1)
                pe.wait_ge(s_g, 1)
                with pe.Fori(0, NBLK // 2) as it:
                    for u in range(2):
                        n = 2 * it + u
                        pe.wait_ge(s_x, n + 1)
                        pe.wait_ge(s_r, n)
                        for j in range(TPB):
                            mm = pe.matmul(PS[:, u, j * E1:(j + 1) * E1], xs[:, u, j * P:(j + 1) * P], gT[:, :],
                                           start=True, stop=True)
                        mm.then_inc(s_l, 1)

            @block.scalar
            def _(act):
                act.wait_ge(s_t, 1)
                act.activation(gT[:, :], PS[:, 7, 0:E1], ACT.Copy).then_inc(s_g, 1)
                with act.Fori(0, NBLK // 2) as it:
                    for u in range(2):
                        n = 2 * it + u
                        act.wait_ge(s_r, n)
                        act.activation(xs[:, u, :], XNT[:, bass.ds(BT * n, BT)], ACT.Copy).then_inc(s_x, 1)

            @block.vector
            def _(dve):
                dve.drain().then_inc(s_r, 1)
                with dve.Fori(0, NBLK // 2) as it:
                    for u in range(2):
                        n = 2 * it + u
                        dve.wait_ge(s_l, n + 1)
                        dve.tensor_copy(LG[:, bass.ds(TPB * n, TPB), :],
                                        PS[:, u, 0:TPB * E1].rearrange("p (j c) -> p j c", j=TPB)).then_inc(s_r, 1)


def route1(nc, a, LG, W):
    with ExitStack() as ctx:
        sb, sem = stage(nc, ctx)
        low = sb("r1_low", [P, E1 * E1])
        gm = sb("r1_gm", [P, NT])
        gs = sb("r1_gs", [P, NT])
        gr = sb("r1_gr", [P, NT])
        p = sb("r1_p", [P, NT, E1])
        t1 = sb("r1_t1", [P, NT, E1, E1])
        t2 = sb("r1_t2", [P, NT, E1, E1])
        rank = sb("r1_rank", [P, NT, E1])
        s_l, s_d, s_e, s_c = (sem("r1_" + n) for n in ("loaded", "differences", "exps", "chain"))
        with nc.Block() as block:
            @block.sync
            def _(sp):
                sp.dma_start(low[:, :], broadcast_rows(a["c_lower1"], P, E1 * E1)).then_inc(s_l, 16)
                sp.wait_ge(s_l, 16)

            @block.scalar
            def _(act):
                act.wait_ge(s_d, 1)
                act.activation(p[:, :, :], p[:, :, :], ACT.Exp).then_inc(s_e, 1)

            @block.vector
            def _(dve):
                ch = Chain(dve, s_c)
                per = [[1, NT], [0, E1]]
                ch.link(dve.tensor_reduce(gm[:, :], LG[:, :, :], AX.X, ALU.max))
                dve.tensor_tensor(p[:, :, :], LG[:, :, :], bc(gm[:, :], per), ALU.subtract).then_inc(s_d, 1)
                dve.wait_ge(s_e, 1)
                ch.link(dve.tensor_reduce(gs[:, :], p[:, :, :], AX.X, ALU.add))
                ch.link(dve.reciprocal(gr[:, :], gs[:, :]))
                ch.link(dve.tensor_tensor(p[:, :, :], p[:, :, :], bc(gr[:, :], per), ALU.mult))
                dve.wait_ge(s_l, 16)
                top2(dve, ch, p[:, :, :], W[:, :, :], low[:, :], t1[:, :, :, :], t2[:, :, :, :], rank[:, :, :], NT, E1)
                ch.link(dve.tensor_reduce(gs[:, :], W[:, :, :], AX.X, ALU.add))
                ch.link(dve.tensor_scalar(gm[:, :], gs[:, :], 1e-10, None, ALU.max))
                ch.link(dve.reciprocal(gr[:, :], gm[:, :]))
                ch.link(dve.tensor_tensor(W[:, :, :], W[:, :, :], bc(gr[:, :], per), ALU.mult))


def experts1(nc, a, g, W):
    X, XN, XNT, PS = (g[k] for k in ("X", "XN", "XNT", "PS"))
    FT = F1 // P
    with ExitStack() as ctx:
        sb, sem = stage(nc, ctx)
        w1 = sb("e1_w1", [P, E1, F1])
        w2 = sb("e1_w2", [P, E1, FT, D])
        b1 = sb("e1_b1", [P, E1, FT])
        b2 = sb("e1_b2", [P, E1, D])
        hh = sb("e1_hh", [P, 2, FT, BT])
        acc = sb("e1_acc", [P, TPB, D])
        s_w, s_up, s_h, s_dn, s_ac, s_cl, s_x = (sem("e1_" + n) for n in (
            "weights", "up_done", "hidden", "down_done", "combined", "clipped", "x_added"))
        adds = 2 * E1 * TPB
        with nc.Block() as block:
            @block.sync
            def _(sp):
                sp.dma_start(w1[:, :, :], a["L1_ffn_w1"].rearrange("e d f -> d e f")).then_inc(s_w, 16)
                for f in range(FT):
                    sp.dma_start(w2[:, :, f, :], a["L1_ffn_w2"][:, f * P:(f + 1) * P, :].rearrange(
                        "e p d -> p e d")).then_inc(s_w, 16)
                sp.dma_start(b1[:, :, :], a["L1_ffn_b1"].rearrange("e (f p) -> p e f", p=P),
                             allow_slow_non_contiguous=True).then_inc(s_w, 16)
                sp.dma_start(b2[:, :, :], broadcast_rows(a["L1_ffn_b2"], P, E1 * D).rearrange(
                    "p (e d) -> p e d", d=D)).then_inc(s_w, 16)
                sp.wait_ge(s_w, 80)

            @block.tensor
            def _(pe):
                pe.wait_ge(s_w, 80)
                with pe.Fori(0, NBLK) as n:
                    def up(e):
                        i = E1 * n + e
                        if e >= 2:
                            pe.wait_ge(s_h, FT * (i - 1))
                        else:
                            pe.wait_ge(s_h, FT * E1 * n)
                        for f in range(FT):
                            pe.matmul(PS[:, FT * (e % 2) + f, :], w1[:, e, f * P:(f + 1) * P],
                                      XNT[:, bass.ds(BT * n, BT)], start=True, stop=True).then_inc(s_up, 1)

                    def down(e):
                        i = E1 * n + e
                        pe.wait_ge(s_h, FT * (i + 1))
                        pe.wait_ge(s_ac, adds * n + 2 * TPB * max(e - 1, 0))
                        for j in range(TPB):
                            for f in range(FT):
                                mm = pe.matmul(PS[:, 4 + e % 2, j * P:(j + 1) * P], hh[:, e % 2, f, j * P:(j + 1) * P],
                                               w2[:, e, f, :], start=(f == 0), stop=(f == FT - 1))
                        mm.then_inc(s_dn, 1)

                    up(0)
                    for e in range(E1):
                        if e + 1 < E1:
                            up(e + 1)
                        down(e)

            @block.scalar
            def _(act):
                act.wait_ge(s_w, 80)
                with act.Fori(0, NBLK) as n:
                    for e in range(E1):
                        i = E1 * n + e
                        act.wait_ge(s_dn, i - 1 if e >= 2 else E1 * n)
                        for f in range(FT):
                            act.wait_ge(s_up, FT * i + f + 1)
                            act.activation(hh[:, e % 2, f, :], PS[:, FT * (e % 2) + f, :], ACT.Gelu,
                                           bias=b1[:, e, f:f + 1]).then_inc(s_h, 1)

            @block.vector
            def _(dve):
                dve.wait_ge(s_w, 80)
                with dve.Fori(0, NBLK) as n:
                    for e in range(E1):
                        for k in range(2):
                            if k:
                                dve.wait_ge(s_dn, E1 * n + e + 1)
                            for j in range(TPB):
                                if e or k:
                                    dve.wait_ge(s_ac, adds * n + TPB * (2 * e + k - 1) + j + 1)
                                dve.scalar_tensor_tensor(
                                    acc[:, j, :], PS[:, 4 + e % 2, j * P:(j + 1) * P] if k else b2[:, e, :],
                                    W[:, TPB * n + j, e:e + 1], acc[:, j, :] if e or k else XN[:, TPB * n + j, :],
                                    ALU.mult, ALU.add).then_inc(s_ac, 1)
                    dve.wait_ge(s_ac, adds * (n + 1))
                    dve.tensor_scalar(acc[:, :, :], acc[:, :, :], 100.0, -100.0, ALU.min, ALU.max).then_inc(s_cl, 1)
                    dve.wait_ge(s_cl, n + 1)
                    xb = X[:, bass.ds(TPB * n, TPB), :]
                    dve.scalar_tensor_tensor(xb, acc[:, :, :], 0.5, xb, ALU.mult, ALU.add).then_inc(s_x, 1)
                    dve.wait_ge(s_x, n + 1)


def causal(nc, a, g):
    with ExitStack() as ctx:
        sb, sem = stage(nc, ctx)
        YT = sb("ca_yt", [P, BATCH + 1, SEQ])
        causal_attention(nc, a, g, YT)
        causal_output(nc, a, g, YT)


def causal_attention(nc, a, g, YT):
    XNT, IDN, PS = (g[k] for k in ("XNT", "IDN", "PS"))
    ITERS = BATCH * NP
    C = H1 * HD
    STEPS = [(qc, kt) for qc in range(HALVES) for kt in range(TPB * (qc + 1))]
    NS = len(STEPS)
    TILES = [(h, t, c) for h in range(2) for t in range(KT) for c in range(t // TPB + 1)]
    PREP = [("q", 0), ("q", 1), ("k", 0), ("k", 1), ("v", 0), ("v", 1)] + [("t", i) for i in range(len(TILES))] + [("m", 0)]
    OUT = {2: ("z", 1), 3: ("y", 1), TPB + 3: ("z", 0), TPB + 4: ("y", 0)}
    RING, at = [], 0
    for s in range(NS):
        upto = min(len(PREP) * (s + 1) // (NS - 2), len(PREP))
        RING.append(([OUT[s]] if s in OUT else []) + PREP[at:upto])
        at = upto
    USES = sum(map(len, RING))
    PRO = len(PREP)
    PLACE = {use: i for i, use in enumerate(x for uses in RING for x in uses)}
    assert USES % 2 == 1 and PRO % 2 == 1
    with ExitStack() as ctx:
        sb, sem = stage(nc, ctx)
        w = sb("ca_w", [P, 2, 3, P])
        bqk = sb("ca_bqk", [P, 2, 2])
        bv = sb("ca_bv", [P, 2, P])
        wo = sb("ca_wo", [P, 2, D])
        tri = sb("ca_tri", [P, 3, P])
        trb = sb("ca_trb", [P, 3, P], BF16)
        sel = sb("ca_sel", [P, P])
        ones = sb("ca_ones", [P, VW])
        xs = sb("ca_xs", [P, 2, SEQ])
        Q = sb("ca_q", [P, 2, 2, SEQ])
        K = sb("ca_k", [P, 2, 2, SEQ])
        qb = sb("ca_qb", [P, 2, SEQ], BF16)
        kb = sb("ca_kb", [P, SEQ], BF16)
        VA = sb("ca_v", [P, 2, KT, P])
        PR = sb("ca_p", [P, 2, 2, BT])
        ot = sb("ca_ot", [P, BT])
        su = sb("ca_su", [2 * VW, BT])
        z = sb("ca_z", [P, BT])
        on = sb("ca_on", [P, BT])
        mh = sb("ca_mh", [P, 2 * KT, HALVES])
        m = sb("ca_m", [P, 2 * KT])
        nm = sb("ca_nm", [2 * KT, P])
        s_wl = [sem(f"ca_w_loaded{u}") for u in range(2)]
        s_mr = [sem(f"ca_max_rows{u}") for u in range(2)]
        s_wo = [sem(f"ca_wo_loaded{u}") for u in range(2)]
        (s_c, s_set, s_x, s_ring, s_rd, s_mx, s_st, s_exp, s_pv, s_ot, s_z) = (
            sem("ca_" + n) for n in (
                "constants", "set", "x_ready", "ring_filled", "ring_read", "m_ready", "scores_ready",
                "exp_done", "pv_done", "sums_copied", "z_ready"))
        SETS = 14

        def number(n, use):
            return PRO + USES * n + PLACE[use]

        def behind(n, qc):
            return HALVES * n - 1 if qc else HALVES * n

        with nc.Block() as block:
            @block.sync
            def _(sp):
                sp.dma_start(tri[:, :, :], a["c_masks"]).then_inc(s_c, 16)
                sp.dma_start(sel[:, :], a["c_pair"]).then_inc(s_c, 16)
                wout = a["L1_attn_W_out"].rearrange("(p c) f -> p c f", p=NP)
                wqkv = a["L1_attn_W_qkv"].rearrange("f (t p c) -> p f t c", t=3, p=NP)
                bias = a["L1_attn_b_qkv"].rearrange("(t p c) -> p c t", t=3, p=NP)

                def load(n, u):
                    sp.dma_start(w[:, u, :, :], wqkv[n]).then_inc(s_wl[u], 16)
                    sp.dma_start(bqk[:, u, :], bias[n, :, 0:2], allow_slow_non_contiguous=True).then_inc(s_wl[u], 16)
                    row = bias[n, :, 2:3]
                    sp.dma_start(bv[:, u, :], bass.AP(row.tensor, row.offset, [[0, P], [1, P]])).then_inc(s_wl[u], 16)

                def max_rows(reads, u):
                    sp.wait_ge(s_rd, reads)
                    for h in range(2):
                        sp.dma_start(Q[HD * (1 - h):HD * (1 - h) + 1, u, h, :].rearrange("o (t p) -> o t p", p=P),
                                     nm[KT * h:KT * (h + 1), :]).then_inc(s_mr[u], 16)

                load(0, 0)
                load(1, 1)
                max_rows(PRO + 1, 0)
                with sp.Fori(0, ITERS // 2) as it:
                    for u in range(2):
                        n = 2 * it + u
                        sp.wait_ge(s_rd, PRO + USES * n + 1)
                        load((n + 2) % NP, u)
                        sp.dma_start(wo[:, u, :], wout[n % NP]).then_inc(s_wo[u], 16)
                        max_rows(number(n, ("m", 0)) + 2, 1 - u)
                for u in range(2):
                    sp.wait_ge(s_wl[u], 48 * (ITERS // 2 + 1))
                    sp.wait_ge(s_mr[u], 32 * (ITERS // 2 + 1 - u))

            @block.tensor
            def _(pe):
                def turn(num, place, use, u, rd_k):
                    kind, i = use
                    bank = 6 + place % 2
                    pe.wait_ge(s_rd, num + (1 if place == 0 else 0))
                    if kind in "qk":
                        mm = pe.matmul(PS[:, bank, :], w[:, u, "qk".index(kind), :], xs[:, u, i * BT:(i + 1) * BT],
                                       start=True, stop=True)
                    elif kind == "v":
                        for j in range(TPB):
                            r = (i * TPB + j) * P
                            mm = pe.matmul(PS[:, bank, j * P:(j + 1) * P], xs[:, u, r:r + P], w[:, u, 2, :],
                                           start=True, stop=True)
                    elif kind == "t":
                        if i == 0:
                            pe.wait_ge(s_rd, rd_k)
                        h, t, c = TILES[i]
                        width = min(BT, (t + 1) * P - c * BT)
                        diagonal = c == t // TPB
                        mm = pe.matmul(PS[:, bank, 0:width], qb[:, h, t * P:(t + 1) * P], kb[:, c * BT:c * BT + width],
                                       start=True, stop=not diagonal)
                        if diagonal:
                            mm = pe.matmul(PS[:, bank, width - P:width], trb[:, 0, :], trb[:, 1, :], start=False, stop=True)
                    elif kind == "m":
                        mm = pe.transpose(PS[0:2 * KT, bank, 0:P], m[:, :], IDN[:, :])
                    elif kind == "z":
                        mm = pe.matmul(PS[:, bank, :], sel[:, :], z[:, :], start=True, stop=True)
                    else:
                        mm = pe.matmul(PS[:, bank, :], wo[:, u, :], on[:, :], start=True, stop=True)
                    mm.then_inc(s_ring, 1)

                def span(s):
                    qc, kt = STEPS[s]
                    return max(0, kt * P - qc * BT)

                def scores(n, s, u):
                    qc, kt = STEPS[s]
                    off, diagonal = span(s), kt >= qc * TPB
                    pe.wait_ge(s_exp, NS * n + s)
                    for h in range(2):
                        bank = 2 * (s % 2) + h
                        mm = pe.matmul(PS[:, bank, off:BT], K[:, u, h, kt * P:(kt + 1) * P],
                                       Q[:, u, h, qc * BT + off:(qc + 1) * BT], start=True, stop=not diagonal)
                        if diagonal:
                            mm = pe.matmul(PS[:, bank, off:off + P], trb[:, 0, :], trb[:, 2, :], start=False, stop=True)
                    mm.then_inc(s_st, 1)

                def weigh(n, s, u):
                    qc, kt = STEPS[s]
                    off, last = span(s), s + 1 == NS or STEPS[s + 1][0] != qc
                    if kt == 0:
                        pe.wait_ge(s_ot, 2 * (HALVES * n + qc))
                    pe.wait_ge(s_exp, NS * n + s + 2)
                    for h in range(2):
                        pe.matmul(PS[HD * h:HD * (h + 1), 4, off:BT], VA[:, u, kt, HD * h:HD * (h + 1)],
                                  PR[:, s % 2, h, off:BT], start=(kt == 0), stop=last, skip_group_check=True)
                    for h in range(2):
                        mm = pe.matmul(PS[VW * h:VW * (h + 1), 5, off:BT], ones[:, :], PR[:, s % 2, h, off:BT],
                                       start=(kt == 0), stop=last, skip_group_check=True)
                    mm.then_inc(s_pv, 1)

                pe.wait_ge(s_c, 32)
                pe.wait_ge(s_set, SETS)
                pe.wait_ge(s_wl[0], 48)
                pe.wait_ge(s_x, 1)
                for i, use in enumerate(PREP):
                    if use[0] == "m":
                        pe.wait_ge(s_mx, 1)
                    turn(i, i, use, 0, PREP.index(("k", 1)) + 2)
                with pe.Fori(0, ITERS // 2) as it:
                    for u in range(2):
                        n = 2 * it + u
                        for s in range(NS):
                            if s == 0:
                                pe.wait_ge(s_mr[u], 32 * (it + 1))
                            scores(n, s, u)
                            for i, use in enumerate(RING[s] + [None]):
                                if s and i == len(RING[s]) // 2:
                                    weigh(n, s - 1, u)
                                if use is None:
                                    continue
                                kind, half = use
                                if use == ("q", 0):
                                    pe.wait_ge(s_wl[1 - u], 48 * (it + 1 + u))
                                    pe.wait_ge(s_x, n + 2)
                                elif kind == "m":
                                    pe.wait_ge(s_mx, n + 2)
                                elif kind == "z":
                                    pe.wait_ge(s_z, behind(n, half) + 2)
                                elif kind == "y":
                                    pe.wait_ge(s_rd, number(n, ("z", half)) + 2)
                                    pe.wait_ge(s_wo[(u - half) % 2], 16 * (it + 1 - (half if u == 0 else 0)))
                                of_last = kind in "zy" and half == 1
                                buffers = u if kind in "zy" and half == 0 else 1 - u
                                assert of_last or kind not in "zy" or buffers == u
                                turn(number(n, use), PLACE[use], use, buffers, number(n, ("k", 1)) + 2)
                        weigh(n, NS - 1, u)
                pe.wait_ge(s_z, HALVES * ITERS + 1)
                turn(PRO + USES * ITERS, 0, ("z", 1), 1, 0)
                pe.wait_ge(s_rd, PRO + USES * ITERS + 2)
                turn(PRO + USES * ITERS + 1, 1, ("y", 1), 1, 0)

            @block.scalar
            def _(act):
                act.drain().then_inc(s_exp, 1)
                act.wait_ge(s_c, 32)
                for n1 in range(2):
                    act.activation(xs[:, n1, :], XNT[:, 0:SEQ], ACT.Copy).then_inc(s_x, 1)

                def sums(n, qc, steps):
                    act.wait_ge(s_pv, NS * n + steps + 1)
                    act.wait_ge(s_rd, number(n, ("z", 1 - qc)) + 2)
                    act.activation(ot[:, :], PS[:, 4, :], ACT.Copy).then_inc(s_ot, 1)
                    act.activation(su[:, :], PS[0:2 * VW, 5, :], ACT.Copy).then_inc(s_ot, 1)

                act.wait_ge(s_set, SETS)
                with act.Fori(0, ITERS // 2) as it:
                    for u in range(2):
                        n = 2 * it + u
                        for s in range(NS):
                            qc, kt = STEPS[s]
                            off = max(0, kt * P - qc * BT)
                            act.wait_ge(s_st, NS * n + s + 1)
                            act.wait_ge(s_pv, NS * n + s)
                            act.activation(PR[:, s % 2, :, off:BT], PS[:, 2 * (s % 2):2 * (s % 2) + 2, off:BT],
                                           ACT.Exp, scale=float(HD) ** -0.5).then_inc(s_exp, 1)
                            if s == TPB:
                                sums(n, 0, TPB)
                            if s == NS - 2:
                                act.wait_ge(s_ring, PRO + USES * n)
                                act.activation(xs[:, u, :], XNT[:, bass.ds(SEQ * ((n + 2) % ITERS // NP), SEQ)],
                                               ACT.Copy).then_inc(s_x, 1)
                        sums(n, 1, NS)

            @block.vector
            def _(dve):
                def half(q, u, h, i, rows):
                    return q[rows, u, h, i * BT:(i + 1) * BT]

                lower, upper = slice(0, HD), slice(HD, P)
                for u in range(2):
                    dve.memset(Q[upper, u, 0, :], 0.0).then_inc(s_set, 1)
                    dve.memset(Q[lower, u, 1, :], 0.0).then_inc(s_set, 1)
                    dve.memset(K[upper, u, 0, :], 1.0).then_inc(s_set, 1)
                    dve.memset(K[lower, u, 1, :], 1.0).then_inc(s_set, 1)
                dve.memset(qb[upper, 0, :], 0.0).then_inc(s_set, 1)
                dve.memset(qb[lower, 1, :], 0.0).then_inc(s_set, 1)
                dve.memset(ones[:, :], 1.0).then_inc(s_set, 1)
                dve.memset(z[:, :], 0.0).then_inc(s_set, 1)
                dve.memset(mh[:, :, :], -3e38)
                dve.memset(ot[:, :], 0.0)
                dve.memset(su[:, :], 1.0)
                dve.memset(wo[:, 1, :], 0.0)
                dve.memset(YT[:, :, :], 0.0).then_inc(s_set, 1)
                dve.wait_ge(s_c, 32)
                dve.tensor_copy(trb[:, :, :], tri[:, :, :]).then_inc(s_set, 1)
                dve.wait_ge(s_set, SETS)
                dve.drain().then_inc(s_rd, 1)
                dve.drain().then_inc(s_pv, 1)

                def read(num, place, use, u, n, rows=None):
                    kind, i = use
                    bank = 6 + place % 2
                    dve.wait_ge(s_ring, num + 1)
                    if kind in "qk":
                        t = "qk".index(kind)
                        full = (Q, K)[t]
                        for h, r in enumerate((lower, upper)):
                            dve.tensor_scalar(half(full, u, h, i, r), PS[r, bank, :], bqk[r, u, t:t + 1], None, ALU.add)
                            if kind == "q":
                                ins = dve.tensor_scalar(qb[r, h, i * BT:(i + 1) * BT], PS[r, bank, :], bqk[r, u, t:t + 1],
                                                        None, ALU.add)
                        if kind == "k":
                            ins = dve.tensor_scalar(kb[:, i * BT:(i + 1) * BT], PS[:, bank, :], bqk[:, u, t:t + 1],
                                                    None, ALU.add)
                    elif kind == "v":
                        ins = dve.tensor_tensor(VA[:, u, i * TPB:(i + 1) * TPB, :],
                                                PS[:, bank, :].rearrange("p (j c) -> p j c", j=TPB),
                                                bc(bv[:, u, :], [[0, TPB], [1, P]]), ALU.add)
                    elif kind == "t":
                        h, t, c = TILES[i]
                        width = min(BT, (t + 1) * P - c * BT)
                        ins = dve.tensor_reduce(mh[:, h * KT + t, c:c + 1], PS[:, bank, 0:width], AX.X, ALU.max)
                    elif kind == "m":
                        dve.wait_ge(*rows)
                        ins = dve.tensor_scalar(nm[:, :], PS[0:2 * KT, bank, 0:P], -1.0, None, ALU.mult)
                    elif kind == "z":
                        ins = dve.tensor_tensor(on[:, :], ot[:, :], PS[:, bank, :], ALU.mult)
                    else:
                        dve.wait_ge(s_rd, num + 1)
                        y = YT[:, (n + NP - 1) // NP if i else n // NP + 1, i * BT:(i + 1) * BT]
                        ins = dve.tensor_tensor(y, y, PS[:, bank, :], ALU.add)
                    ins.then_inc(s_rd, 1)

                def maxima(num):
                    dve.wait_ge(s_rd, num + 1)
                    dve.tensor_reduce(m[:, :], mh[:, :, :], AX.X, ALU.max).then_inc(s_mx, 1)

                dve.wait_ge(s_wl[0], 48)
                for i, use in enumerate(PREP):
                    if use[0] == "m":
                        maxima(i)
                    read(i, i, use, 0, 0, (s_set, SETS))
                with dve.Fori(0, ITERS // 2) as it:
                    for u in range(2):
                        n = 2 * it + u
                        for s in range(NS):
                            if s in (1, TPB + 1):
                                past = behind(n, s == 1)
                                dve.wait_ge(s_ot, 2 * past + 2)
                                dve.reciprocal(z[0:2 * VW, :], su[:, :]).then_inc(s_z, 1)
                            for use in RING[s]:
                                if use == ("q", 0):
                                    dve.wait_ge(s_wl[1 - u], 48 * (it + 1 + u))
                                if use[0] == "m":
                                    maxima(number(n, use))
                                read(number(n, use), PLACE[use], use, 1 - u, n, (s_mr[u], 32 * (it + 1)))
                dve.wait_ge(s_ot, 2 * HALVES * ITERS)
                dve.reciprocal(z[0:2 * VW, :], su[:, :]).then_inc(s_z, 1)
                read(PRO + USES * ITERS, 0, ("z", 1), 1, ITERS)
                read(PRO + USES * ITERS + 1, 1, ("y", 1), 1, ITERS)


def causal_output(nc, a, g, YT):
    X, IDN, PS = (g[k] for k in ("X", "IDN", "PS"))
    with ExitStack() as ctx:
        sb, sem = stage(nc, ctx)
        bo = sb("co_bo", [P, 1])
        yb = sb("co_yb", [P, 2, BT])
        s_c, s_y, s_t, s_a = (sem("co_" + n) for n in ("bias", "y_biased", "y_turned", "added"))
        with nc.Block() as block:
            @block.sync
            def _(sp):
                sp.dma_start(bo[:, :], a["L1_attn_b_out"].rearrange("(f o) -> f o", o=1),
                             allow_slow_non_contiguous=True).then_inc(s_c, 16)
                sp.wait_ge(s_c, 16)

            @block.scalar
            def _(act):
                act.wait_ge(s_c, 16)
                with act.Fori(0, BATCH) as b:
                    for u in range(2):
                        act.wait_ge(s_t, 2 * b)
                        act.activation(yb[:, u, :], YT[:, b + 1, u * BT:(u + 1) * BT], ACT.Identity,
                                       bias=bo[:, 0:1]).then_inc(s_y, 1)

            @block.tensor
            def _(pe):
                with pe.Fori(0, BATCH) as b:
                    for u in range(2):
                        n = 2 * b + u
                        pe.wait_ge(s_y, n + 1)
                        pe.wait_ge(s_a, 2 * b)
                        for j in range(TPB):
                            mm = pe.transpose(PS[:, u, j * P:(j + 1) * P], yb[:, u, j * P:(j + 1) * P], IDN[:, :])
                        mm.then_inc(s_t, 1)

            @block.vector
            def _(dve):
                with dve.Fori(0, BATCH) as b:
                    for u in range(2):
                        n = 2 * b + u
                        dve.wait_ge(s_t, n + 1)
                        xb = X[:, bass.ds(TPB * n, TPB), :]
                        dve.tensor_tensor(xb, xb, PS[:, u, :].rearrange("p (j c) -> p j c", j=TPB),
                                          ALU.add).then_inc(s_a, 1)


def constants():
    dim = np.arange(P) % DH
    inv = np.float32(1.0) / np.float32(10000.0) ** (np.arange(0, DH, 2, dtype=np.float32) / np.float32(DH))
    angle = (np.arange(SEQ, dtype=np.float32)[None, :] * inv.astype(np.float32)[dim // 2][:, None]).astype(np.float32)
    pb = BT // P
    spread = np.zeros((P, NP, P), np.float32)
    rows = np.zeros((P, NP // pb, VW), np.float32)
    for h in range(2):
        for p in range(NP):
            spread[32 * (p % pb) + 2 * (p // pb) + h, p, h * HD:(h + 1) * HD] = 1.0
        for k in range(NP // pb):
            rows[h * HD:(h + 1) * HD, k, 2 * k + h] = 1.0
    pair = np.zeros((P, P), np.float32)
    for h in range(2):
        pair[VW * h, h * HD:(h + 1) * HD] = 1.0
    return {
        "c_ident": np.eye(P, dtype=np.float32),
        "c_rope": np.stack([np.cos(angle), np.sin(angle)]).astype(np.float32),
        "c_lower0": np.tril(np.ones((E0, E0), np.float32), -1),
        "c_spread": spread,
        "c_rows": rows,
        "c_blocks": np.kron(np.eye(2, dtype=np.float32), np.ones((HD, HD), np.float32)),
        "c_masks": np.stack([np.eye(P) * MASK_ROW, np.triu(np.ones((P, P)), 1) * MASK_COL,
                             np.tril(np.ones((P, P)), -1) * MASK_COL], axis=1).astype(np.float32),
        "c_pair": pair,
        "c_lower1": np.tril(np.ones((E1, E1), np.float32), -1),
    }


_INS = ["L0_attn_x", "L0_attn_wq", "L0_attn_bq", "L0_attn_wk", "L0_attn_bk", "L0_attn_wv", "L0_attn_bv", "L0_attn_wo",
        "L0_attn_bo", "L0_ffn_Wq", "L0_ffn_Wk_c", "L0_ffn_Wv_c", "L0_ffn_Wk", "L0_ffn_Wv", "L0_ffn_Wo",
        "L0_ffn_W_shared_in", "L0_ffn_W_shared_out", "L0_ffn_W1_shared", "L0_ffn_W2_experts", "L0_ffn_Wg_gate",
        "L0_ffn_We_gate", "L0_ffn_group_bias", "L0_ffn_expert_bias", "L0_ffn_norm1_w", "L0_ffn_norm2_w",
        "L1_attn_W_qkv", "L1_attn_b_qkv", "L1_attn_W_out", "L1_attn_b_out", "L1_ffn_gate_w", "L1_ffn_w1", "L1_ffn_b1",
        "L1_ffn_w2", "L1_ffn_b2"]


def kernel(**inputs):
    import concourse.bacc as bacc
    from concourse.bass_utils import run_bass_kernel_spmd

    nc = bacc.Bacc("TRN2", target_bir_lowering=False, num_devices=1)
    arrays, args = {}, {}
    for name, value in [(n, inputs[n]) for n in _INS] + list(constants().items()):
        array = np.ascontiguousarray(value)
        arrays[f"in_{name}"] = array
        args[name] = nc.dram_tensor(f"in_{name}", array.shape, mybir.dt.from_np(array.dtype), kind="ExternalInput").ap()
    out = nc.dram_tensor("out_0_dram", [BATCH, SEQ, D], F32, kind="ExternalOutput").ap()
    build(nc, args, out)
    results = run_bass_kernel_spmd(nc, [arrays], core_ids=[0])
    return results.results[0]["out_0_dram"]
```

```python
from contextlib import ExitStack
from itertools import count

import numpy as np

import concourse.bass as bass
from concourse import mybir

F32 = mybir.dt.float32
BF16 = mybir.dt.bfloat16
ALU = mybir.AluOpType
ACT = mybir.ActivationFunctionType
AX = mybir.AxisListType

P = 128
BATCH, SEQ, D = 4, 1024, 128
TOKENS = BATCH * SEQ
BT = 512
TPB = BT // P
NBLK = TOKENS // BT
NT = TOKENS // P
HALVES = SEQ // BT

H0, DH = 16, 8
GH = 4
NG = H0 // GH
PARTS = 3
STK = PARTS * PARTS * DH
KMAX = 96
KROWS = KMAX + PARTS
VW = 32
KT = SEQ // P

HID, E0, EPG = 256, 8, 4
GA = 2
H1, HD = 16, 64
NP = H1 // 2
E1, F1 = 14, 256

LN_EPS, RMS_EPS, LIN_EPS = 1e-5, 1e-6, 1e-6
MASK_ROW, MASK_COL = 250.0, -320.0


class Chain:

    def __init__(self, engine, sem, start=0):
        self.engine, self.sem, self.start, self.n = engine, sem, start, 0

    def tick(self, ins):
        ins.then_inc(self.sem, 1)
        self.n += 1

    def wait(self):
        self.engine.wait_ge(self.sem, self.start + self.n)

    def link(self, ins):
        self.tick(ins)
        self.wait()


def bc(ap, dims):
    return bass.AP(ap.tensor, ap.offset, [list(ap.ap[0])] + [list(d) for d in dims])


def build(nc, a, out, upto=99):
    with ExitStack() as ctx:
        X = ctx.enter_context(nc.sbuf_tensor("X", [P, NT + TPB, D], F32))
        XN = ctx.enter_context(nc.sbuf_tensor("XN", [P, NT, D], F32))
        XNT = ctx.enter_context(nc.sbuf_tensor("XNT", [P, TOKENS], F32))
        IDN = ctx.enter_context(nc.sbuf_tensor("IDN", [P, P], F32))
        PS = ctx.enter_context(nc.psum_tensor("PS", [P, 8, BT], F32))
        PW = ctx.enter_context(nc.sbuf_tensor("PW", [P, TPB], F32))
        scratch = dict(
            QK=nc.dram_tensor("qk_parts", [2, BATCH * H0, PARTS, DH, SEQ], BF16, kind="Internal").ap(),
            V=nc.dram_tensor("v_heads", [BATCH * NG, SEQ, GH * DH], F32, kind="Internal").ap(),
            O=nc.dram_tensor("o_heads", [BATCH * NG + 1, P, SEQ], F32, kind="Internal").ap(),
        )
        g = dict(X=X, XN=XN, XNT=XNT, IDN=IDN, PS=PS, PW=PW, **scratch)
        start(nc, a, g)
        stages = [
            lambda: layernorm(nc, g), lambda: rope_project(nc, a, g), lambda: rope_attention(nc, a, g),
            lambda: ffn0(nc, a, g),
            lambda: layernorm(nc, g), lambda: linear_attention(nc, a, g),
            lambda: layernorm(nc, g), lambda: rope_project(nc, a, g), lambda: rope_attention(nc, a, g),
            lambda: ffn0(nc, a, g),
            lambda: layernorm(nc, g), lambda: ffn1(nc, a, g),
            lambda: layernorm(nc, g), lambda: causal(nc, a, g),
            lambda: layernorm(nc, g), lambda: ffn1(nc, a, g),
        ]
        for s in stages[:upto]:
            s()
        finish(nc, g, out)


STAGES = count()


def stage(nc, ctx):
    number = next(STAGES)
    sems = []

    def sb(name, shape, dt=F32):
        return ctx.enter_context(nc.sbuf_tensor(f"{name}_{number}", shape, dt))

    def sem(name):
        if not sems:
            ctx.callback(clear)
        sems.append(nc.alloc_semaphore(f"{name}_{number}"))
        return sems[-1]

    def clear():
        nc.clear_and_free_semaphores(sems)
        nc.all_engine_barrier()
    return sb, sem


def start(nc, a, g):
    X, IDN, PW = g["X"], g["IDN"], g["PW"]
    with ExitStack() as ctx:
        sb, sem = stage(nc, ctx)
        loaded = sem("loaded")
        with nc.Block() as block:
            @block.sync
            def _(sp):
                sp.dma_start(X[:, 0:NT, :], a["L0_attn_x"].rearrange("b (t p) d -> p (b t) d", p=P)).then_inc(loaded, 16)
                sp.dma_start(IDN[:, :], a["c_ident"]).then_inc(loaded, 16)
                sp.wait_ge(loaded, 32)

            @block.gpsimd
            def _(pool):
                pool.memset(X[:, NT:NT + TPB, :], 0.0)
                pool.memset(PW[:, :], -0.5)


def finish(nc, g, out):
    X = g["X"]
    with ExitStack() as ctx:
        sb, sem = stage(nc, ctx)
        stored = sem("stored")
        with nc.Block() as block:
            @block.sync
            def _(sp):
                sp.dma_start(out.rearrange("b (t p) d -> p (b t) d", p=P), X[:, 0:NT, :]).then_inc(stored, 16)
                sp.wait_ge(stored, 16)


def layernorm(nc, g):
    X, XN, XNT, IDN, PS, PW = (g[k] for k in ("X", "XN", "XNT", "IDN", "PS", "PW"))
    with ExitStack() as ctx:
        sb, sem = stage(nc, ctx)
        st = sb("ln_st", [P, 2, TPB, 6])
        mv = sb("ln_mv", [P, 2, TPB, 2])
        ve = sb("ln_ve", [P, 2, TPB])
        rs = sb("ln_rs", [P, 2, TPB])
        xn = sb("ln_xn", [P, 2, TPB, D])
        eps = sb("ln_eps", [P, TPB])
        mark = sb("ln_mark", [P, 1])
        s_st, s_mv, s_ve, s_rs, s_xn, s_t, s_c = (sem("ln_" + n) for n in
                                                  ("stats", "meanvar", "vareps", "rstd", "normed", "turned", "copied"))
        with nc.Block() as block:
            @block.vector
            def _(dve):
                def stats(n, u):
                    for j in range(TPB):
                        dve.bn_stats(st[:, u, j, :], X[:, TPB * n + j, :]).then_inc(s_st, 1)
                    dve.wait_ge(s_st, (TPB + 1) * n + TPB)
                    dve.memset(mark[:, :], 0.0).then_inc(s_st, 1)
                    for j in range(TPB):
                        dve.bn_aggr(mv[:, u, j, :], st[:, u, j, :]).then_inc(s_mv, 1)

                dve.memset(eps[:, :], LN_EPS)
                stats(0, 0)
                with dve.Fori(0, NBLK // 2) as it:
                    for u in range(2):
                        n = 2 * it + u
                        stats(n + 1, 1 - u)
                        dve.wait_ge(s_rs, n + 1)
                        dve.wait_ge(s_c, 2 * n)
                        for j in range(TPB):
                            dve.tensor_scalar(xn[:, u, j, :], X[:, TPB * n + j, :], mv[:, u, j, 0:1],
                                              rs[:, u, j:j + 1], ALU.subtract, ALU.mult).then_inc(s_xn, 1)

            @block.gpsimd
            def _(pool):
                with pool.Fori(0, NBLK // 2) as it:
                    for u in range(2):
                        n = 2 * it + u
                        pool.wait_ge(s_mv, TPB * n + TPB)
                        pool.tensor_tensor(ve[:, u, :], mv[:, u, :, 1], eps[:, :], ALU.add).then_inc(s_ve, 1)
                        pool.wait_ge(s_ve, n + 1)
                        pool.wait_ge(s_xn, TPB * n)
                        pool.tensor_tensor(rs[:, u, :], ve[:, u, :], PW[:, :], ALU.pow).then_inc(s_rs, 1)

            @block.tensor
            def _(pe):
                with pe.Fori(0, NBLK // 2) as it:
                    for u in range(2):
                        n = 2 * it + u
                        pe.wait_ge(s_xn, TPB * n + TPB)
                        pe.wait_ge(s_c, 2 * n)
                        for j in range(TPB):
                            mm = pe.transpose(PS[:, u, j * P:(j + 1) * P], xn[:, u, j, :], IDN[:, :])
                        mm.then_inc(s_t, 1)

            @block.scalar
            def _(act):
                act.drain().then_inc(s_c, 2)
                with act.Fori(0, NBLK // 2) as it:
                    for u in range(2):
                        n = 2 * it + u
                        act.wait_ge(s_xn, TPB * n + TPB)
                        act.activation(XN[:, bass.ds(TPB * n, TPB), :], xn[:, u, :, :], ACT.Copy).then_inc(s_c, 1)
                        act.wait_ge(s_t, n + 1)
                        act.activation(XNT[:, bass.ds(BT * n, BT)], PS[:, u, :], ACT.Copy).then_inc(s_c, 1)


def rope_project(nc, a, g):
    XNT, IDN, PS = g["XNT"], g["IDN"], g["PS"]
    DC = a["L0_ffn_Wk_c"].shape[1]
    with ExitStack() as ctx:
        sb, sem = stage(nc, ctx)
        wq = sb("rp_wq", [P, D])
        wc = sb("rp_wc", [P, 2, DC])
        wkv = sb("rp_wkv", [DC, 2, D])
        wcT = sb("rp_wcT", [DC, 2, P])
        W = sb("rp_W", [P, 5, D])
        ROT = sb("rp_rot", [P, 2, SEQ])
        xs = sb("rp_xs", [P, 2, BT])
        t1 = sb("rp_t1", [P, 2, BT])
        t2 = sb("rp_t2", [P, 2, BT])
        qk = sb("rp_qk", [P, 2, BT])
        res = sb("rp_res", [P, 2, BT])
        parts = sb("rp_parts", [P, 2, PARTS, 2, BT], BF16)
        vs = sb("rp_vs", [P, 2, TPB, D])
        s_ld, s_w, s_wt, s_xs, s_pj, s_rd, s_v, s_chain, s_pt, s_st, s_vst, s_qk, s_h = (sem("rp_" + n) for n in (
            "loaded", "weights", "wturned", "x_ready", "projected", "psum_read", "v_copied", "chain", "parts_done",
            "qk_stored", "v_stored", "qk_done", "high_done"))
        with nc.Block() as block:
            @block.sync
            def _(sp):
                sp.dma_start(wq[:, :], a["L0_ffn_Wq"]).then_inc(s_ld, 16)
                sp.dma_start(wc[:, 0, :], a["L0_ffn_Wk_c"]).then_inc(s_ld, 16)
                sp.dma_start(wc[:, 1, :], a["L0_ffn_Wv_c"]).then_inc(s_ld, 16)
                sp.dma_start(wkv[:, 0, :], a["L0_ffn_Wk"]).then_inc(s_ld, 16)
                sp.dma_start(wkv[:, 1, :], a["L0_ffn_Wv"]).then_inc(s_ld, 16)
                sp.dma_start(ROT[:, :, :], a["c_rope"].rearrange("t p s -> p t s")).then_inc(s_ld, 16)
                with sp.Fori(0, BATCH) as b:
                    for u in range(2):
                        n = 2 * b + u
                        sp.wait_ge(s_v, n + 1)
                        for gi in range(NG):
                            sp.dma_start(g["V"][NG * b + gi, u * BT:(u + 1) * BT, :].rearrange("(j p) c -> p j c", p=P),
                                         vs[:, u, :, gi * GH * DH:(gi + 1) * GH * DH]).then_inc(s_vst, 16)
                        sp.wait_ge(s_pt, n + 1)
                        for t in range(2):
                            for w in range(PARTS):
                                sp.dma_start(g["QK"][t, bass.ds(H0 * b, H0), w, :, u * BT:(u + 1) * BT],
                                             parts[:, u, w, t, :]).then_inc(s_st, 16)
                sp.wait_ge(s_vst, 16 * NG * NBLK)
                sp.wait_ge(s_st, 16 * 2 * PARTS * NBLK)

            @block.tensor
            def _(pe):
                pe.wait_ge(s_ld, 96)
                for t in range(2):
                    mm = pe.transpose(PS[0:DC, 7, t * P:(t + 1) * P], wc[:, t, :], IDN[:, :])
                mm.then_inc(s_wt, 1)
                pe.wait_ge(s_w, 1)
                for t in range(2):
                    mm = pe.matmul(PS[:, 6, t * P:(t + 1) * P], wcT[:, t, :], wkv[:, t, :], start=True, stop=True)
                mm.then_inc(s_wt, 1)
                pe.wait_ge(s_w, 6)
                with pe.Fori(0, BATCH) as b:
                    for u in range(2):
                        n = 2 * b + u
                        pe.wait_ge(s_xs, n + 1)
                        pe.wait_ge(s_rd, 2 * n)
                        for k in range(4):
                            mm = pe.matmul(PS[:, k, :], W[:, k, :], xs[:, u, :], start=True, stop=True)
                        mm.then_inc(s_pj, 1)
                        pe.wait_ge(s_v, n)
                        for j in range(TPB):
                            mm = pe.matmul(PS[:, 4, j * P:(j + 1) * P], xs[:, u, j * P:(j + 1) * P], W[:, 4, :],
                                           start=True, stop=True)
                        mm.then_inc(s_pj, 1)

            @block.vector
            def _(dve):
                dve.wait_ge(s_wt, 1)
                dve.tensor_copy(wcT[:, :, :], PS[0:DC, 7, 0:2 * P].rearrange("p (t m) -> p t m", t=2)).then_inc(s_w, 1)
                dve.wait_ge(s_wt, 2)
                dve.tensor_copy(W[:, 0, :], wq[:, :]).then_inc(s_w, 1)
                dve.tensor_copy(W[:, 1, :], PS[:, 6, 0:P]).then_inc(s_w, 1)
                dve.tensor_copy(W[:, 4, :], PS[:, 6, P:2 * P]).then_inc(s_w, 1)
                dve.wait_ge(s_w, 4)
                wv = W[:, 0:4, :].rearrange("p k (i two) -> p k i two", two=2)
                dve.tensor_scalar(wv[:, 2:4, :, 0], wv[:, 0:2, :, 1], -1.0, None, ALU.mult).then_inc(s_w, 1)
                dve.tensor_copy(wv[:, 2:4, :, 1], wv[:, 0:2, :, 0]).then_inc(s_w, 1)
                with dve.Fori(0, BATCH) as b:
                    for u in range(2):
                        n = 2 * b + u
                        cos = bc(ROT[:, 0, u * BT:(u + 1) * BT], [[0, 2], [1, BT]])
                        sin = bc(ROT[:, 1, u * BT:(u + 1) * BT], [[0, 2], [1, BT]])
                        dve.wait_ge(s_pj, 2 * n + 1)
                        dve.tensor_tensor(t1[:, :, :], PS[:, 0:2, :], cos, ALU.mult).then_inc(s_rd, 1)
                        dve.tensor_tensor(t2[:, :, :], PS[:, 2:4, :], sin, ALU.mult).then_inc(s_rd, 1)
                        dve.wait_ge(s_rd, 2 * n + 2)
                        dve.wait_ge(s_h, 2 * n)
                        dve.tensor_tensor(qk[:, :, :], t1[:, :, :], t2[:, :, :], ALU.add).then_inc(s_qk, 1)
                        dve.wait_ge(s_h, 2 * n + 1)
                        dve.tensor_tensor(res[:, :, :], qk[:, :, :], parts[:, u, 0, :, :],
                                          ALU.subtract).then_inc(s_qk, 1)
                        dve.wait_ge(s_h, 2 * n + 2)
                        dve.tensor_tensor(parts[:, u, 2, :, :], res[:, :, :], parts[:, u, 1, :, :],
                                          ALU.subtract).then_inc(s_pt, 1)

            @block.scalar
            def _(act):
                with act.Fori(0, BATCH) as b:
                    for u in range(2):
                        n = 2 * b + u
                        act.wait_ge(s_pj, 2 * n)
                        act.activation(xs[:, u, :], XNT[:, bass.ds(BT * n, BT)], ACT.Copy).then_inc(s_xs, 1)
                        act.wait_ge(s_pj, 2 * n + 2)
                        act.wait_ge(s_vst, 16 * NG * n)
                        act.activation(vs[:, u, :, :], PS[:, 4, :].rearrange("p (j c) -> p j c", j=TPB),
                                       ACT.Copy).then_inc(s_v, 1)
                        act.wait_ge(s_qk, 2 * n + 1)
                        act.wait_ge(s_st, 16 * 2 * PARTS * n)
                        act.activation(parts[:, u, 0, :, :], qk[:, :, :], ACT.Copy).then_inc(s_h, 1)
                        act.wait_ge(s_qk, 2 * n + 2)
                        act.activation(parts[:, u, 1, :, :], res[:, :, :], ACT.Copy).then_inc(s_h, 1)


def rope_attention(nc, a, g):
    IDN, PS, QK, V, O = (g[k] for k in ("IDN", "PS", "QK", "V", "O"))
    ITERS = BATCH * NG
    STEPS = HALVES * KT
    PH = GH // 2
    TILES = PH * KT * HALVES
    LOADS = PH * (PARTS + 1)
    LATE = 3
    REST = [(1, c) for c in range(TILES // 2, TILES)]
    FIRST = [(0, c) for c in range(TILES)]
    BEGIN = [(1, c) for c in range(TILES // 2)]
    PRO = FIRST + BEGIN[:LATE] + [("turn", 0)] + BEGIN[LATE:]
    RING = REST + FIRST[:LATE] + [("turn", 1)] + FIRST[LATE:] + BEGIN[:LATE] + [("turn", 0)] + BEGIN[LATE:]
    assert len(RING) % 3 == 0
    with ExitStack() as ctx:
        sb, sem = stage(nc, ctx)
        Q = sb("ra_q", [P, 2, GH, SEQ], BF16)
        K = sb("ra_k", [P, 2, GH, SEQ], BF16)
        vc = sb("ra_vc", [P, 2, KT, GH * DH])
        VA = sb("ra_va", [P, 2, KT, GH, VW])
        PR = sb("ra_p", [P, 2, GH, BT])
        ot = sb("ra_ot", [P, 2, BT])
        mh = sb("ra_mh", [P, 2, PH * KT, HALVES])
        m = sb("ra_m", [P, 2, PH * KT])
        nm = sb("ra_nm", [PH * KT, P])
        nr = sb("ra_nr", [PH * KT, P])
        mp = sb("ra_mp", [PH * KT, 2, 2, PARTS, P], BF16)
        s_qk = [[sem(f"ra_qk{p}_loaded{u}") for u in range(2)] for p in range(2)]
        s_mr = [[sem(f"ra_max_rows{p}_{u}") for u in range(2)] for p in range(2)]
        s_vl = [sem(f"ra_v_loaded{u}") for u in range(2)]
        s_st = [sem(f"ra_scores_ready{p}") for p in range(2)]
        s_exp = [sem(f"ra_exp_done{p}") for p in range(2)]
        s_os = [sem(f"ra_o_stored{h}") for h in range(2)]
        s_va, s_set, s_tile, s_max, s_mx, s_mp, s_pv, s_of, s_ch = (
            sem("ra_" + n) for n in ("v_ready", "set", "tile_ready", "tile_read", "m_ready", "m_parts", "pv_done",
                                     "o_free", "chain"))
        SETS = 9

        def behind(s, pair, u):
            if pair == 0:
                return u, s
            return (u if s >= KT else 1 - u), (s - KT) % STEPS

        with nc.Block() as block:
            @block.sync
            def _(sp):
                def load(n, pair, u):
                    for j in range(PH * pair, PH * (pair + 1)):
                        k = QK[1, GH * n + j, 0, :, :]
                        sp.dma_start(K[0:STK, u, j, :], bass.AP(k.tensor, k.offset, [
                            [0, PARTS], [SEQ, PARTS * DH], [1, SEQ]])).then_inc(s_qk[pair][u], 16)
                        for i in range(PARTS):
                            q = QK[0, GH * n + j, i, :, :]
                            sp.dma_start(Q[i * PARTS * DH:(i + 1) * PARTS * DH, u, j, :], bass.AP(q.tensor, q.offset, [
                                [0, PARTS], [SEQ, DH], [1, SEQ]])).then_inc(s_qk[pair][u], 16)

                def values(n, u):
                    sp.dma_start(vc[:, u, :, :], V[n].rearrange("(t p) c -> p t c", p=P)).then_inc(s_vl[u], 16)

                def max_rows(ready, pair, u):
                    sp.wait_ge(s_mp, ready)
                    for i in range(PARTS):
                        sp.dma_start(Q[KMAX + i:KMAX + i + 1, u, PH * pair:PH * (pair + 1), :].rearrange(
                            "o j (t p) -> o (j t) p", p=P), mp[:, pair, u, i, :]).then_inc(s_mr[pair][u], 16)

                sp.wait_ge(s_set, SETS)
                load(0, 0, 0)
                load(0, 1, 0)
                values(0, 0)
                max_rows(1, 0, 0)
                with sp.Fori(0, ITERS // 2) as it:
                    for u in range(2):
                        n = 2 * it + u
                        after = n + 1 if u == 0 else (n + 1) % ITERS
                        sp.wait_ge(s_st[0], STEPS * n)
                        load(after, 0, 1 - u)
                        max_rows(2 * n + 2, 1, u)
                        sp.wait_ge(s_st[1], STEPS * n + KT)
                        load(after, 1, 1 - u)
                        sp.wait_ge(s_va, n + 1)
                        values(after, 1 - u)
                        max_rows(2 * n + 3, 0, 1 - u)
                sp.wait_ge(s_mr[0][0], 16 * PARTS * (ITERS // 2 + 1))

            @block.gpsimd
            def _(pool):
                def store(n, h, pairs=(0, 1)):
                    pool.wait_ge(s_of, 2 * n + h + 1)
                    for pair in pairs:
                        rows, half = slice(VW * PH * pair, VW * PH * (pair + 1)), (pair + h + 1) % 2
                        pool.dma_start(O[n + (1 if pair < h else 0), rows, half * BT:(half + 1) * BT],
                                       ot[rows, h, :]).then_inc(s_os[h], 16)

                with pool.Fori(0, ITERS) as n:
                    for h in range(2):
                        store(n, h)
                store(ITERS, 0)
                store(ITERS, 1, (1,))
                pool.wait_ge(s_os[0], 32 * (ITERS + 1))
                pool.wait_ge(s_os[1], 32 * ITERS + 16)

            @block.tensor
            def _(pe):
                def ring(number, place, use, n2, u):
                    if not isinstance(number, int) or number >= 3:
                        pe.wait_ge(s_max, number - 2)
                    if use[0] == "turn":
                        pe.wait_ge(s_mx, n2)
                        pe.transpose(PS[0:PH * KT, 5 + place % 3, 0:P], m[:, use[1], :], IDN[:, :]).then_inc(s_tile, 1)
                    else:
                        pair, c = use
                        j, t, h = PH * pair + c // (KT * HALVES), c // HALVES % KT, c % HALVES
                        pe.matmul(PS[:, 5 + place % 3, :], Q[0:KMAX, u, j, t * P:(t + 1) * P],
                                  K[0:KMAX, u, j, h * BT:(h + 1) * BT], start=True, stop=True).then_inc(s_tile, 1)

                def scores(n, s, pair, u):
                    ub, sb_ = behind(s, pair, u)
                    pe.wait_ge(s_exp[pair], STEPS * n + s)
                    for j in (PH * pair, PH * pair + 1):
                        mm = pe.matmul(PS[:, j, :], K[0:KROWS, ub, j, (sb_ % KT) * P:(sb_ % KT + 1) * P],
                                       Q[0:KROWS, ub, j, (sb_ // KT) * BT:(sb_ // KT + 1) * BT], start=True, stop=True)
                    mm.then_inc(s_st[pair], 1)

                def weigh(s, u, pairs=(0, 1), start=None):
                    for pair in pairs:
                        ub, sb_ = behind(s, pair, u)
                        for j in (PH * pair, PH * pair + 1):
                            mm = pe.matmul(PS[VW * j:VW * (j + 1), 4, :], VA[:, ub, sb_ % KT, j, :], PR[:, s % 2, j, :],
                                           start=(s % KT == 0) if start is None else start, stop=(s % KT == KT - 1),
                                           skip_group_check=True)
                    mm.then_inc(s_pv, 1)

                pe.wait_ge(s_set, SETS)
                pe.wait_ge(s_va, 1)
                weigh(0, 1, start=True)
                pe.wait_ge(s_qk[0][0], 16 * LOADS)
                for i, use in enumerate(PRO):
                    if use == BEGIN[0]:
                        pe.wait_ge(s_qk[1][0], 16 * LOADS)
                    ring(i, i, use, 1, 0)
                with pe.Fori(0, ITERS // 2) as it:
                    for u in range(2):
                        n = 2 * it + u
                        done = 0
                        for s in range(STEPS):
                            for pair in range(2):
                                if s == KT * pair:
                                    pe.wait_ge(s_mr[pair][u], 16 * PARTS * (it + 1))
                                scores(n, s, pair, u)
                                upto = len(RING) * (2 * s + pair + 1) // (2 * STEPS)
                                while done < upto:
                                    use = RING[done]
                                    if use in (FIRST[0], BEGIN[0]):
                                        pe.wait_ge(s_qk[use[0]][1 - u], 16 * LOADS * (it + 1 + u))
                                    ring(len(PRO) + len(RING) * n + done, len(PRO) + done, use,
                                         2 * n + 2 if use[1] == 1 else 2 * n + 3, u if use in REST else 1 - u)
                                    done += 1
                            if s % KT == 1:
                                pe.wait_ge(s_of, 2 * n + s // KT + 1)
                            if s == 1:
                                pe.wait_ge(s_va, n + 1)
                            weigh((s - 1) % STEPS, u if s else 1 - u)
                for s in range(KT):
                    scores(ITERS, s, 1, 0)
                    if s == 1:
                        pe.wait_ge(s_of, 2 * ITERS + 1)
                    weigh((s - 1) % STEPS, 0 if s else 1, (1,) if s else (0, 1))
                pe.wait_ge(s_exp[1], STEPS * ITERS + KT)
                weigh(KT - 1, 0, (1,))

            @block.scalar
            def _(act):
                def values(u, loads):
                    act.wait_ge(s_vl[u], loads)
                    act.activation(VA[:, u, :, :, 0:DH], vc[:, u, :, :].rearrange("p t (j d) -> p t j d", j=GH),
                                   ACT.Copy).then_inc(s_va, 1)

                def exps(n, s, pair):
                    e = STEPS * n + s + 1
                    act.wait_ge(s_st[pair], e)
                    act.wait_ge(s_pv, e)
                    act.activation(PR[:, s % 2, PH * pair:PH * (pair + 1), :], PS[:, PH * pair:PH * (pair + 1), :],
                                   ACT.Exp, scale=float(DH) ** -0.5).then_inc(s_exp[pair], 1)

                def output(n, h, rows=slice(0, P)):
                    act.wait_ge(s_pv, STEPS * n + KT * h + 2)
                    act.wait_ge(s_os[h], 32 * n)
                    act.activation(ot[rows, h, :], PS[rows, 4, :], ACT.Copy).then_inc(s_of, 1)

                act.wait_ge(s_set, SETS)
                values(0, 16)
                with act.Fori(0, ITERS // 2) as it:
                    for u in range(2):
                        n = 2 * it + u
                        for s in range(STEPS):
                            for pair in range(2):
                                exps(n, s, pair)
                            if s % KT == 0:
                                output(n, s // KT)
                            if s == KT + 4:
                                values(1 - u, 16 * (it + 1 + u))
                for s in range(KT):
                    exps(ITERS, s, 1)
                    if s == 0:
                        output(ITERS, 0)
                output(ITERS, 1, slice(VW * PH, P))

            @block.vector
            def _(dve):
                dve.memset(Q[64:128, :, :, :], 0.0).then_inc(s_set, 1)
                dve.memset(K[64:96, :, :, :], 0.0).then_inc(s_set, 1)
                dve.memset(K[96:128, :, :, :], 1.0).then_inc(s_set, 1)
                dve.memset(Q[0:64, 1, PH:GH, :], 0.0).then_inc(s_set, 1)
                dve.memset(K[0:64, 1, PH:GH, :], 0.0).then_inc(s_set, 1)
                dve.memset(PR[:, 0, :, :], 0.0).then_inc(s_set, 1)
                dve.memset(PR[:, 1, :, :], 0.0).then_inc(s_set, 1)
                dve.memset(VA[:, :, :, :, :], 0.0).then_inc(s_set, 1)
                dve.wait_ge(s_set, SETS - 1)
                dve.memset(VA[:, :, :, :, DH:DH + 1], 1.0).then_inc(s_set, 1)

                def read(number, place, use, passes, u, rows):
                    bank = 5 + place % 3
                    dve.wait_ge(s_tile, number + 1)
                    if use[0] == "turn":
                        pair = use[1]
                        dve.tensor_scalar(nm[:, :], PS[0:PH * KT, bank, 0:P], -1.0, None, ALU.mult).then_inc(s_max, 1)
                        dve.wait_ge(s_max, number + 1)
                        dve.wait_ge(s_mr[pair][u], rows)
                        ch = Chain(dve, s_ch, 3 * passes)
                        ch.link(dve.tensor_copy(mp[:, pair, u, 0, :], nm[:, :]))
                        ch.link(dve.tensor_tensor(nr[:, :], nm[:, :], mp[:, pair, u, 0, :], ALU.subtract))
                        ch.link(dve.tensor_copy(mp[:, pair, u, 1, :], nr[:, :]))
                        dve.tensor_tensor(mp[:, pair, u, 2, :], nr[:, :], mp[:, pair, u, 1, :],
                                          ALU.subtract).then_inc(s_mp, 1)
                    else:
                        pair, c = use
                        dve.tensor_reduce(mh[:, pair, c // HALVES, c % HALVES:c % HALVES + 1], PS[:, bank, :],
                                          AX.X, ALU.max).then_inc(s_max, 1)
                        if c == TILES - 1:
                            dve.wait_ge(s_max, number + 1)
                            dve.tensor_reduce(m[:, pair, :], mh[:, pair, :, :], AX.X, ALU.max).then_inc(s_mx, 1)

                for i, use in enumerate(PRO):
                    read(i, i, use, 0, 0, 0)
                with dve.Fori(0, ITERS // 2) as it:
                    for u in range(2):
                        n = 2 * it + u
                        for i, use in enumerate(RING):
                            second = use == ("turn", 1)
                            read(len(PRO) + len(RING) * n + i, len(PRO) + i, use, 2 * n + (1 if second else 2),
                                 u if second else 1 - u, 16 * PARTS * (it if second else it + u))


def broadcast_rows(ap, parts, n):
    return bass.AP(ap.tensor, ap.offset, [[0, parts], [1, n]])


def top2(dve, ch, p, w, lower, t1, t2, rank, n, e):
    def axes(ap, d):
        return bc(ap, [[e, n], d[0], d[1]])
    mine, other = axes(p, ([1, e], [0, e])), axes(p, ([0, e], [1, e]))
    ch.tick(dve.tensor_tensor(t1, other, mine, ALU.is_gt))
    ch.link(dve.tensor_tensor(t2, other, mine, ALU.is_equal))
    ch.link(dve.tensor_tensor(t2, t2, bc(lower, [[0, n], [e, e], [1, e]]), ALU.mult))
    ch.link(dve.tensor_tensor(t1, t1, t2, ALU.add))
    ch.link(dve.tensor_reduce(rank, t1, AX.X, ALU.add))
    ch.link(dve.scalar_tensor_tensor(w, rank, 1.5, p, ALU.is_lt, ALU.mult))


def ffn0(nc, a, g):
    with ExitStack() as ctx:
        sb, sem = stage(nc, ctx)
        LG = sb("f0_lg", [P, NT, GA + E0])
        W = sb("f0_w", [P, NT, E0])
        attention_output(nc, a, g, LG)
        route0(nc, a, LG, W)
        experts0(nc, a, g, W)


def attention_output(nc, a, g, LG):
    XN, XNT, IDN, PS, PW, O = (g[k] for k in ("XN", "XNT", "IDN", "PS", "PW", "O"))
    G = GA + E0
    with ExitStack() as ctx:
        sb, sem = stage(nc, ctx)
        wo = sb("ao_wo", [P, D])
        wg = sb("ao_wg", [P, G])
        gb = sb("ao_gb", [P, G])
        n1 = sb("ao_n1", [P, D])
        ot = sb("ao_ot", [P, 2, NG, BT])
        rc = sb("ao_rc", [P, TPB * H0])
        sa = sb("ao_sa", [P, TPB, D])
        saT = sb("ao_saT", [P, BT])
        y = sb("ao_y", [P, TPB, D])
        sq = sb("ao_sq", [P, TPB, D])
        ss = sb("ao_ss", [P, TPB])
        ms = sb("ao_ms", [P, TPB])
        r = sb("ao_r", [P, TPB])
        x1 = sb("ao_x1", [P, TPB, D])
        x1T = sb("ao_x1T", [P, BT])
        s_ot = [sem(f"ao_o_loaded{u}") for u in range(2)]
        s_w, s_o, s_rc, s_sa, s_saT, s_T, s_pr, s_y, s_ss, s_ms, s_r, s_x1, s_x1T, s_cp, s_lt, s_lg = (
            sem("ao_" + n) for n in ("weights", "o_turned", "recip", "normalised", "sa_turned", "saT_ready",
                                     "projected", "y_ready", "squares", "mean", "rms", "x1_ready", "x1_turned",
                                     "copied", "logits", "logits_read"))
        with nc.Block() as block:
            @block.sync
            def _(sp):
                sp.dma_start(wo[:, :], a["L0_ffn_Wo"]).then_inc(s_w, 16)
                sp.dma_start(wg[:, 0:GA], a["L0_ffn_Wg_gate"]).then_inc(s_w, 16)
                sp.dma_start(wg[:, GA:G], a["L0_ffn_We_gate"]).then_inc(s_w, 16)
                sp.dma_start(gb[:, 0:GA], broadcast_rows(a["L0_ffn_group_bias"], P, GA)).then_inc(s_w, 16)
                sp.dma_start(gb[:, GA:G], broadcast_rows(a["L0_ffn_expert_bias"], P, E0)).then_inc(s_w, 16)
                sp.dma_start(n1[:, :], broadcast_rows(a["L0_ffn_norm1_w"], P, D)).then_inc(s_w, 16)
                with sp.Fori(0, BATCH) as b:
                    for u in range(2):
                        sp.wait_ge(s_o, 2 * b)
                        sp.dma_start(ot[:, u, :, :], O[bass.ds(NG * b + 1, NG), :, u * BT:(u + 1) * BT].rearrange(
                            "g p s -> p g s")).then_inc(s_ot[u], 16)

            @block.tensor
            def _(pe):
                pe.wait_ge(s_w, 96)
                with pe.Fori(0, BATCH) as b:
                    for u in range(2):
                        n = 2 * b + u
                        pe.wait_ge(s_ot[u], 16 * (b + 1))
                        pe.wait_ge(s_sa, n)
                        for j in range(TPB):
                            for gi in range(NG):
                                mm = pe.transpose(PS[:, j, gi * P:(gi + 1) * P], ot[:, u, gi, j * P:(j + 1) * P], IDN[:, :])
                        mm.then_inc(s_o, 1)
                        pe.wait_ge(s_sa, n + 1)
                        for j in range(TPB):
                            mm = pe.transpose(PS[:, 4, j * P:(j + 1) * P], sa[:, j, :], IDN[:, :])
                        mm.then_inc(s_saT, 1)
                        pe.wait_ge(s_T, n + 1)
                        for j in range(TPB):
                            mm = pe.matmul(PS[:, 5, j * P:(j + 1) * P], saT[:, j * P:(j + 1) * P], wo[:, :],
                                           start=True, stop=True)
                        mm.then_inc(s_pr, 1)
                        pe.wait_ge(s_x1, TPB * (n + 1))
                        for j in range(TPB):
                            mm = pe.transpose(PS[:, 6, j * P:(j + 1) * P], x1[:, j, :], IDN[:, :])
                        mm.then_inc(s_x1T, 1)
                        pe.wait_ge(s_cp, 3 * n + 2)
                        for j in range(TPB):
                            mm = pe.matmul(PS[:, 7, j * G:(j + 1) * G], x1T[:, j * P:(j + 1) * P], wg[:, :],
                                           start=True, stop=True)
                        mm.then_inc(s_lt, 1)

            @block.vector
            def _(dve):
                dve.wait_ge(s_w, 96)
                heads = PS[:, 0:TPB, :].rearrange("p j (h c) -> p (j h) c", c=VW)
                with dve.Fori(0, BATCH) as b:
                    for u in range(2):
                        n = 2 * b + u
                        dve.wait_ge(s_o, n + 1)
                        dve.reciprocal(rc[:, :], heads[:, :, DH]).then_inc(s_rc, 1)
                        dve.wait_ge(s_rc, n + 1)
                        dve.tensor_tensor(sa[:, :, :].rearrange("p j (h d) -> p (j h) d", d=DH), heads[:, :, 0:DH],
                                          bc(rc[:, :], [[1, TPB * H0], [0, DH]]), ALU.mult).then_inc(s_sa, 1)
                        dve.wait_ge(s_pr, n + 1)
                        dve.tensor_tensor(y[:, :, :], PS[:, 5, :].rearrange("p (j c) -> p j c", j=TPB),
                                          XN[:, bass.ds(TPB * n, TPB), :], ALU.add).then_inc(s_y, 1)
                        dve.wait_ge(s_ss, TPB * (n + 1))
                        dve.tensor_scalar(ms[:, :], ss[:, :], 1.0 / D, RMS_EPS, ALU.mult, ALU.add).then_inc(s_ms, 1)
                        dve.wait_ge(s_r, n + 1)
                        for j in range(TPB):
                            dve.scalar_tensor_tensor(x1[:, j, :], y[:, j, :], r[:, j:j + 1], n1[:, :],
                                                     ALU.mult, ALU.mult).then_inc(s_x1, 1)
                        dve.wait_ge(s_lt, n + 1)
                        dve.tensor_tensor(LG[:, bass.ds(TPB * n, TPB), :],
                                          PS[:, 7, 0:TPB * G].rearrange("p (j c) -> p j c", j=TPB),
                                          bc(gb[:, :], [[0, TPB], [1, G]]), ALU.add).then_inc(s_lg, 1)

            @block.gpsimd
            def _(pool):
                with pool.Fori(0, NBLK) as n:
                    pool.wait_ge(s_ms, n + 1)
                    pool.tensor_tensor(r[:, :], ms[:, :], PW[:, :], ALU.pow).then_inc(s_r, 1)

            @block.scalar
            def _(act):
                with act.Fori(0, NBLK) as n:
                    act.wait_ge(s_saT, n + 1)
                    act.activation(saT[:, :], PS[:, 4, :], ACT.Copy).then_inc(s_T, 1)
                    act.wait_ge(s_y, n + 1)
                    for j in range(TPB):
                        act.activation(sq[:, j, :], y[:, j, :], ACT.Square, accum_out=ss[:, j:j + 1]).then_inc(s_ss, 1)
                    act.wait_ge(s_x1, TPB * (n + 1))
                    act.activation(XN[:, bass.ds(TPB * n, TPB), :], x1[:, :, :], ACT.Copy).then_inc(s_cp, 1)
                    act.wait_ge(s_x1T, n + 1)
                    act.activation(x1T[:, :], PS[:, 6, :], ACT.Copy).then_inc(s_cp, 1)
                    act.wait_ge(s_cp, 3 * n + 2)
                    act.activation(XNT[:, bass.ds(BT * n, BT)], x1T[:, :], ACT.Copy).then_inc(s_cp, 1)


def route0(nc, a, LG, W):
    with ExitStack() as ctx:
        sb, sem = stage(nc, ctx)
        low = sb("r0_low", [P, E0 * E0])
        gm = sb("r0_gm", [P, NT])
        ge = sb("r0_ge", [P, NT, GA])
        gs = sb("r0_gs", [P, NT])
        gp = sb("r0_gp", [P, NT])
        em = sb("r0_em", [P, NT * GA])
        ee = sb("r0_ee", [P, NT * GA, EPG])
        es = sb("r0_es", [P, NT * GA])
        er = sb("r0_er", [P, NT, GA])
        mg = sb("r0_mg", [P, NT, GA])
        p = sb("r0_p", [P, NT, E0])
        t1 = sb("r0_t1", [P, NT, E0, E0])
        t2 = sb("r0_t2", [P, NT, E0, E0])
        rank = sb("r0_rank", [P, NT, E0])
        s_l, s_d, s_e, s_c = (sem("r0_" + n) for n in ("loaded", "differences", "exps", "chain"))
        with nc.Block() as block:
            @block.sync
            def _(sp):
                sp.dma_start(low[:, :], broadcast_rows(a["c_lower0"], P, E0 * E0)).then_inc(s_l, 16)
                sp.wait_ge(s_l, 16)

            @block.scalar
            def _(act):
                act.wait_ge(s_d, 2)
                act.activation(ge[:, :, :], ge[:, :, :], ACT.Exp).then_inc(s_e, 1)
                act.activation(ee[:, :, :], ee[:, :, :], ACT.Exp).then_inc(s_e, 1)

            @block.vector
            def _(dve):
                ch = Chain(dve, s_c)
                gl = LG[:, :, 0:GA]
                el = bc(LG[:, :, GA:GA + E0], [[GA + E0, NT], [EPG, GA], [1, EPG]])
                ch.tick(dve.tensor_reduce(gm[:, :], gl, AX.X, ALU.max))
                ch.link(dve.tensor_reduce(em[:, :].rearrange("p (n g) -> p n g", g=GA), el, AX.X, ALU.max))
                dve.tensor_tensor(ge[:, :, :], gl, bc(gm[:, :], [[1, NT], [0, GA]]), ALU.subtract).then_inc(s_d, 1)
                dve.tensor_tensor(ee[:, :, :].rearrange("p (n g) e -> p n g e", g=GA), el,
                                  bc(em[:, :], [[GA, NT], [1, GA], [0, EPG]]), ALU.subtract).then_inc(s_d, 1)
                dve.wait_ge(s_e, 2)
                ch.tick(dve.tensor_reduce(gs[:, :], ge[:, :, :], AX.X, ALU.add))
                ch.tick(dve.tensor_reduce(es[:, :], ee[:, :, :], AX.X, ALU.add))
                ch.link(dve.tensor_tensor(mg[:, :, 1], ge[:, :, 1], ge[:, :, 0], ALU.is_gt))
                ch.tick(dve.tensor_scalar(mg[:, :, 0], mg[:, :, 1], -1.0, 1.0, ALU.mult, ALU.add))
                ch.tick(dve.reciprocal(gp[:, :], gs[:, :]))
                ch.link(dve.reciprocal(er[:, :, :].rearrange("p n g -> p (n g)"), es[:, :]))
                ch.link(dve.tensor_tensor(er[:, :, :], er[:, :, :], mg[:, :, :], ALU.mult))
                ch.link(dve.tensor_tensor(p[:, :, :].rearrange("p n (g e) -> p (n g) e", g=GA), ee[:, :, :],
                                          bc(er[:, :, :], [[1, NT * GA], [0, EPG]]), ALU.mult))
                ch.link(dve.tensor_tensor(p[:, :, :], p[:, :, :], bc(gp[:, :], [[1, NT], [0, E0]]), ALU.mult))
                dve.wait_ge(s_l, 16)
                top2(dve, ch, p[:, :, :], W[:, :, :], low[:, :], t1[:, :, :, :], t2[:, :, :, :], rank[:, :, :], NT, E0)


def experts0(nc, a, g, W):
    X, XN, XNT, PS, PW = (g[k] for k in ("X", "XN", "XNT", "PS", "PW"))
    FT = HID // P
    EB = BT // D
    HB = E0 // EB
    with ExitStack() as ctx:
        sb, sem = stage(nc, ctx)
        wi = sb("e0_wi", [P, 2, 2 * HID])
        ws = sb("e0_ws", [P, FT, D])
        w2 = sb("e0_w2", [P, FT, E0, D])
        n2 = sb("e0_n2", [P, D])
        sg = sb("e0_sg", [P, 2, FT, BT])
        hT = sb("e0_hT", [P, 2, FT, BT])
        acc = sb("e0_acc", [P, TPB, D])
        y = sb("e0_y", [P, TPB, D])
        sq = sb("e0_sq", [P, TPB, D])
        ss = sb("e0_ss", [P, TPB])
        ms = sb("e0_ms", [P, TPB])
        r = sb("e0_r", [P, TPB])
        z = sb("e0_z", [P, TPB, D])
        s_w, s_up, s_sg, s_h, s_dn, s_sh, s_ac, s_y, s_ss, s_ms, s_r, s_z, s_n2 = (
            sem("e0_" + n) for n in ("weights", "up_done", "silu_done", "hidden", "down_done", "shared_done", "combined",
                                     "y_ready", "squares", "mean", "rms", "z_ready", "norm_halved"))
        with nc.Block() as block:
            @block.sync
            def _(sp):
                sp.dma_start(wi[:, 0, :], a["L0_ffn_W_shared_in"]).then_inc(s_w, 16)
                sp.dma_start(wi[:, 1, :], a["L0_ffn_W1_shared"]).then_inc(s_w, 16)
                sp.dma_start(ws[:, :, :], a["L0_ffn_W_shared_out"].rearrange("(f p) d -> p f d", p=P)).then_inc(s_w, 16)
                for f in range(FT):
                    sp.dma_start(w2[:, f, :, :], a["L0_ffn_W2_experts"][:, f * P:(f + 1) * P, :].rearrange(
                        "e p d -> p e d")).then_inc(s_w, 16)
                sp.dma_start(n2[:, :], broadcast_rows(a["L0_ffn_norm2_w"], P, D)).then_inc(s_w, 16)
                sp.wait_ge(s_w, 96)

            @block.tensor
            def _(pe):
                pe.wait_ge(s_w, 96)
                with pe.Fori(0, NBLK) as n:
                    pe.wait_ge(s_ac, TPB * E0 * n)
                    pe.wait_ge(s_y, n)
                    for k in range(2):
                        for c in range(2 * FT):
                            mm = pe.matmul(PS[:, 2 * FT * k + c, :], wi[:, k, c * P:(c + 1) * P],
                                           XNT[:, bass.ds(BT * n, BT)], start=True, stop=True)
                        mm.then_inc(s_up, 1)
                    pe.wait_ge(s_h, 2 * n + 1)
                    for j in range(TPB):
                        for f in range(FT):
                            mm = pe.matmul(PS[:, 2, j * P:(j + 1) * P], hT[:, 0, f, j * P:(j + 1) * P], ws[:, f, :],
                                           start=(f == 0), stop=(f == FT - 1))
                    mm.then_inc(s_sh, 1)
                    pe.wait_ge(s_h, 2 * n + 2)
                    for j in range(TPB):
                        for h in range(HB):
                            if j:
                                pe.wait_ge(s_ac, E0 * (TPB * n + j - 1) + EB * (h + 1))
                            for f in range(FT):
                                mm = pe.matmul(PS[:, h, :], hT[:, 1, f, j * P:(j + 1) * P],
                                               w2[:, f, h * EB:(h + 1) * EB, :], start=(f == 0), stop=(f == FT - 1))
                            mm.then_inc(s_dn, 1)

            @block.scalar
            def _(act):
                with act.Fori(0, NBLK) as n:
                    for k in range(2):
                        act.wait_ge(s_up, 2 * n + k + 1)
                        act.wait_ge(s_h, 2 * n)
                        act.activation(sg[:, k, :, :], PS[:, 2 * FT * k:2 * FT * k + FT, :], ACT.Silu).then_inc(s_sg, 1)
                    act.wait_ge(s_y, n + 1)
                    for j in range(TPB):
                        act.activation(sq[:, j, :], y[:, j, :], ACT.Square, accum_out=ss[:, j:j + 1]).then_inc(s_ss, 1)

            @block.gpsimd
            def _(pool):
                with pool.Fori(0, NBLK) as n:
                    pool.wait_ge(s_ms, n + 1)
                    pool.tensor_tensor(r[:, :], ms[:, :], PW[:, :], ALU.pow).then_inc(s_r, 1)

            @block.vector
            def _(dve):
                dve.wait_ge(s_w, 96)
                dve.tensor_scalar(n2[:, :], n2[:, :], 0.5, None, ALU.mult).then_inc(s_n2, 1)
                dve.wait_ge(s_n2, 1)
                with dve.Fori(0, NBLK) as n:
                    for k in range(2):
                        dve.wait_ge(s_sg, 2 * n + k + 1)
                        dve.wait_ge(s_dn, TPB * HB * n)
                        dve.tensor_tensor(hT[:, k, :, :], sg[:, k, :, :],
                                          PS[:, 2 * FT * k + FT:2 * FT * (k + 1), :], ALU.mult).then_inc(s_h, 1)
                    for j in range(TPB):
                        for x in range(E0):
                            if x % EB == 0:
                                dve.wait_ge(s_dn, HB * (TPB * n + j) + x // EB + 1)
                            if x:
                                dve.wait_ge(s_ac, E0 * (TPB * n + j) + x)
                            dve.scalar_tensor_tensor(
                                acc[:, j, :], PS[:, x // EB, x % EB * D:(x % EB + 1) * D], W[:, TPB * n + j, x:x + 1],
                                acc[:, j, :] if x else XN[:, TPB * n + j, :], ALU.mult, ALU.add).then_inc(s_ac, 1)
                    dve.wait_ge(s_ac, E0 * TPB * (n + 1))
                    dve.wait_ge(s_sh, n + 1)
                    dve.tensor_tensor(y[:, :, :], PS[:, 2, :].rearrange("p (j c) -> p j c", j=TPB), acc[:, :, :],
                                      ALU.add).then_inc(s_y, 1)
                    dve.wait_ge(s_ss, TPB * (n + 1))
                    dve.tensor_scalar(ms[:, :], ss[:, :], 1.0 / D, RMS_EPS, ALU.mult, ALU.add).then_inc(s_ms, 1)
                    dve.wait_ge(s_r, n + 1)
                    for j in range(TPB):
                        dve.scalar_tensor_tensor(z[:, j, :], y[:, j, :], r[:, j:j + 1], n2[:, :],
                                                 ALU.mult, ALU.mult).then_inc(s_z, 1)
                    dve.wait_ge(s_z, TPB * (n + 1))
                    dve.tensor_tensor(X[:, bass.ds(TPB * n, TPB), :], X[:, bass.ds(TPB * n, TPB), :], z[:, :, :],
                                      ALU.add)


def linear_attention(nc, a, g):
    X, XNT, IDN, PS = (g[k] for k in ("X", "XNT", "IDN", "PS"))
    C = H1 * HD
    CB = C // BT
    PB = BT // P
    with ExitStack() as ctx:
        sb, sem = stage(nc, ctx)
        wq, wk, wv = (sb("la_w" + c, [P, C]) for c in "qkv")
        wo = sb("la_wo", [P, NP, D])
        bq = sb("la_bq", [P, NP])
        bo = sb("la_bo", [P, 1])
        bkv = sb("la_bkv", [P, 2, C])
        ones = sb("la_ones", [P, VW])
        sel = sb("la_sel", [P, NP, P])
        rows = sb("la_rows", [P, NP // PB, VW])
        blocks = sb("la_blocks", [P, P])
        xs = sb("la_xs", [P, SEQ])
        tk = sb("la_tk", [P, 2, C])
        ek = sb("la_ek", [P, 2, C])
        km = sb("la_km", [P, 2, C])
        vt = sb("la_vt", [P, 2, C])
        kvs = sb("la_kvs", [P, NP, P])
        ksr = sb("la_ksr", [VW, C])
        ksm = sb("la_ksm", [P, NP, VW])
        G = sb("la_g", [P, NP, D])
        eq = sb("la_eq", [P, 2, BT])
        rq = sb("la_rq", [P, 2, BT])
        qm = sb("la_qm", [P, NP, BT])
        de = sb("la_de", [P, BT])
        z = sb("la_z", [P, BT])
        oT = sb("la_oT", [P, BT])
        (s_w, s_one, s_x, s_pj, s_rd, s_ex, s_re, s_km, s_kv, s_ks, s_kst, s_ksm, s_gm, s_g, s_q, s_eq, s_qm, s_dn, s_de,
         s_z, s_zb, s_zq, s_o, s_oT, s_t, s_add) = (sem("la_" + n) for n in (
             "weights", "ones", "x_ready", "projected", "psum_read", "exp_k", "relu_k", "k_ready", "kv_done", "kv_masked",
             "sums_turned", "sums_masked", "g_done", "g_copied", "q_done", "exp_relu_q", "q_ready", "denominators",
             "eps_added", "z_ready", "z_spread", "q_scaled", "output", "output_copied", "output_turned", "added"))
        with nc.Block() as block:
            @block.sync
            def _(sp):
                for w, name in ((wq, "wq"), (wk, "wk"), (wv, "wv")):
                    sp.dma_start(w[:, :], a["L0_attn_" + name].rearrange("f h d -> f (h d)")).then_inc(s_w, 16)
                sp.dma_start(wo[:, :, :], a["L0_attn_wo"].rearrange("(p h) m f -> (h m) p f", h=2)).then_inc(s_w, 16)
                sp.dma_start(bq[:, :], a["L0_attn_bq"].rearrange("(p h) d -> (h d) p", h=2),
                             allow_slow_non_contiguous=True).then_inc(s_w, 16)
                sp.dma_start(bo[:, :], a["L0_attn_bo"].rearrange("(f o) -> f o", o=1),
                             allow_slow_non_contiguous=True).then_inc(s_w, 16)
                sp.dma_start(bkv[:, 0, :], broadcast_rows(a["L0_attn_bk"], P, C)).then_inc(s_w, 16)
                sp.dma_start(bkv[:, 1, :], broadcast_rows(a["L0_attn_bv"], P, C)).then_inc(s_w, 16)
                sp.dma_start(sel[:, :, :], a["c_spread"]).then_inc(s_w, 16)
                sp.dma_start(rows[:, :, :], a["c_rows"]).then_inc(s_w, 16)
                sp.dma_start(blocks[:, :], a["c_blocks"]).then_inc(s_w, 16)
                sp.wait_ge(s_w, 11 * 16)

            @block.tensor
            def _(pe):
                pe.wait_ge(s_w, 11 * 16)
                pe.wait_ge(s_one, 1)
                with pe.Fori(0, BATCH) as b:
                    pe.wait_ge(s_x, b + 1)

                    def project(t):
                        pe.wait_ge(s_rd, 2 * (KT * b + t))
                        for k, w in enumerate((wk, wv)):
                            for c in range(CB):
                                mm = pe.matmul(PS[:, CB * k + c, :], xs[:, t * P:(t + 1) * P], w[:, c * BT:(c + 1) * BT],
                                               start=True, stop=True)
                            mm.then_inc(s_pj, 1)

                    def gather(t):
                        pe.wait_ge(s_km, KT * b + t + 1)
                        for p in range(NP):
                            pe.matmul(PS[:, 4 + p // PB, p % PB * P:(p % PB + 1) * P], vt[:, t % 2, p * P:(p + 1) * P],
                                      km[:, t % 2, p * P:(p + 1) * P], start=(t == 0 and p % PB == 0),
                                      stop=(t == KT - 1), skip_group_check=True)
                        for c in range(CB):
                            mm = pe.matmul(PS[0:VW, 6 + c, :], ones[:, :], km[:, t % 2, c * BT:(c + 1) * BT],
                                           start=(t == 0), stop=(t == KT - 1))
                        mm.then_inc(s_kv, 1)

                    project(0)
                    for t in range(KT):
                        if t + 1 < KT:
                            project(t + 1)
                        gather(t)
                    pe.wait_ge(s_ks, 2 * b + 2)
                    for p in range(NP):
                        mm = pe.matmul(PS[:, 1 + p // PB, p % PB * P:(p % PB + 1) * P], kvs[:, p, :], wo[:, p, :],
                                       start=True, stop=True)
                    mm.then_inc(s_gm, 1)
                    for p in range(NP):
                        mm = pe.transpose(PS[:, 0, p * VW:(p + 1) * VW], ksr[:, p * P:(p + 1) * P], IDN[0:VW, 0:VW])
                    mm.then_inc(s_kst, 1)
                    pe.wait_ge(s_g, b + 1)
                    pe.wait_ge(s_ksm, b + 1)
                    for c in range(HALVES):
                        n = HALVES * b + c
                        for p in range(NP):
                            if p >= 2 or c:
                                pe.wait_ge(s_qm, NP * n + p - 1)
                            pe.matmul(PS[:, p % 2, :], wq[:, p * P:(p + 1) * P], xs[:, c * BT:(c + 1) * BT],
                                      start=True, stop=True).then_inc(s_q, 1)
                        pe.wait_ge(s_qm, NP * (n + 1))
                        for p in range(NP):
                            r = 32 * (p % PB)
                            mm = pe.matmul(PS[r:r + VW, 4, :], ksm[:, p, :], qm[:, p, :], start=(p < PB), stop=(p >= PB))
                        mm.then_inc(s_dn, 1)
                        pe.wait_ge(s_z, n + 1)
                        for p in range(NP + 1):
                            if p < NP:
                                if p >= 2:
                                    pe.wait_ge(s_zq, NP * n + p - 1)
                                pe.matmul(PS[:, 5 + p % 2, :], sel[:, p, :], z[:, :], start=True, stop=True).then_inc(s_zb, 1)
                            if p:
                                pe.wait_ge(s_zq, NP * n + p)
                                mm = pe.matmul(PS[:, 7, :], G[:, p - 1, :], qm[:, p - 1, :], start=(p == 1), stop=(p == NP))
                        mm.then_inc(s_o, 1)
                        pe.wait_ge(s_oT, n + 1)
                        for j in range(TPB):
                            mm = pe.transpose(PS[:, 3, j * P:(j + 1) * P], oT[:, j * P:(j + 1) * P], IDN[:, :])
                        mm.then_inc(s_t, 1)
                    pe.wait_ge(s_add, HALVES * (b + 1))

            @block.scalar
            def _(act):
                act.wait_ge(s_w, 11 * 16)
                with act.Fori(0, BATCH) as b:
                    act.wait_ge(s_o, HALVES * b)
                    act.activation(xs[:, :], XNT[:, bass.ds(SEQ * b, SEQ)], ACT.Copy).then_inc(s_x, 1)
                    for t in range(KT):
                        i = KT * b + t
                        act.wait_ge(s_rd, 2 * i + 1)
                        act.activation(ek[:, t % 2, :], tk[:, t % 2, :], ACT.Exp).then_inc(s_ex, 1)
                        act.wait_ge(s_ex, i + 1)
                        act.wait_ge(s_kv, i - 1) if t >= 2 else act.wait_ge(s_kv, KT * b)
                        act.activation(km[:, t % 2, :], tk[:, t % 2, :], ACT.Relu).then_inc(s_re, 1)
                    act.wait_ge(s_gm, b + 1)
                    act.activation(G[:, :, :], PS[:, 1:3, :].rearrange("p k (q f) -> p (k q) f", f=D), ACT.Copy).then_inc(s_g, 1)
                    for c in range(HALVES):
                        n = HALVES * b + c
                        for p in range(NP):
                            act.wait_ge(s_q, NP * n + p + 1)
                            if p >= 2 or c:
                                act.wait_ge(s_qm, NP * n + p - 1)
                            act.activation(eq[:, p % 2, :], PS[:, p % 2, :], ACT.Exp, bias=bq[:, p:p + 1]).then_inc(s_eq, 1)
                            act.activation(rq[:, p % 2, :], PS[:, p % 2, :], ACT.Relu, bias=bq[:, p:p + 1]).then_inc(s_eq, 1)
                        act.wait_ge(s_o, n + 1)
                        act.activation(oT[:, :], PS[:, 7, :], ACT.Identity, bias=bo[:, 0:1]).then_inc(s_oT, 1)

            @block.vector
            def _(dve):
                dve.memset(ones[:, :], 1.0).then_inc(s_one, 1)
                dve.wait_ge(s_w, 11 * 16)
                with dve.Fori(0, BATCH) as b:
                    for t in range(KT + 1):
                        i = KT * b + t
                        if t < KT:
                            dve.wait_ge(s_pj, 2 * i + 1)
                            dve.tensor_tensor(tk[:, t % 2, :].rearrange("p (k c) -> p k c", k=CB), PS[:, 0:CB, :],
                                              bkv[:, 0, :].rearrange("p (k c) -> p k c", k=CB), ALU.add).then_inc(s_rd, 1)
                            dve.wait_ge(s_pj, 2 * i + 2)
                            dve.wait_ge(s_kv, i - 1) if t >= 2 else dve.wait_ge(s_kv, KT * b)
                            dve.tensor_tensor(vt[:, t % 2, :].rearrange("p (k c) -> p k c", k=CB), PS[:, CB:2 * CB, :],
                                              bkv[:, 1, :].rearrange("p (k c) -> p k c", k=CB), ALU.add).then_inc(s_rd, 1)
                        if t:
                            dve.wait_ge(s_rd, 2 * i)
                            dve.wait_ge(s_re, i)
                            dve.scalar_tensor_tensor(km[:, (t - 1) % 2, :], ek[:, (t - 1) % 2, :], 1.0,
                                                     km[:, (t - 1) % 2, :], ALU.min, ALU.add).then_inc(s_km, 1)
                    dve.wait_ge(s_kv, KT * (b + 1))
                    dve.tensor_copy(ksr[:, :].rearrange("p (k c) -> p k c", k=CB), PS[0:VW, 6:8, :]).then_inc(s_ks, 1)
                    dve.tensor_tensor(kvs[:, :, :], PS[:, 4:6, :].rearrange("p k (q d) -> p (k q) d", d=P),
                                      bc(blocks[:, :], [[0, NP], [1, P]]), ALU.mult).then_inc(s_ks, 1)
                    dve.wait_ge(s_kst, b + 1)
                    dve.tensor_tensor(ksm[:, :, :].rearrange("p (k q) c -> p k q c", q=PB),
                                      PS[:, 0, 0:NP * VW].rearrange("p (k q c) -> p k q c", q=PB, c=VW),
                                      bc(rows[:, :, :], [[VW, NP // PB], [0, PB], [1, VW]]), ALU.mult).then_inc(s_ksm, 1)
                    for c in range(HALVES):
                        n = HALVES * b + c
                        for p in range(NP):
                            dve.wait_ge(s_eq, 2 * (NP * n + p + 1))
                            if p == 0 and c:
                                dve.wait_ge(s_o, n)
                            dve.scalar_tensor_tensor(qm[:, p, :], eq[:, p % 2, :], 1.0, rq[:, p % 2, :],
                                                     ALU.min, ALU.add).then_inc(s_qm, 1)
                        dve.wait_ge(s_dn, n + 1)
                        dve.tensor_scalar(de[:, :], PS[:, 4, :], LIN_EPS, None, ALU.add).then_inc(s_de, 1)
                        dve.wait_ge(s_de, n + 1)
                        dve.reciprocal(z[:, :], de[:, :]).then_inc(s_z, 1)
                        for p in range(NP):
                            dve.wait_ge(s_zb, NP * n + p + 1)
                            dve.tensor_tensor(qm[:, p, :], qm[:, p, :], PS[:, 5 + p % 2, :], ALU.mult).then_inc(s_zq, 1)
                        dve.wait_ge(s_t, n + 1)
                        dve.tensor_tensor(X[:, bass.ds(TPB * n, TPB), :], X[:, bass.ds(TPB * n, TPB), :],
                                          PS[:, 3, :].rearrange("p (j c) -> p j c", j=TPB), ALU.add).then_inc(s_add, 1)


def ffn1(nc, a, g):
    with ExitStack() as ctx:
        sb, sem = stage(nc, ctx)
        LG = sb("f1_lg", [P, NT, E1])
        W = sb("f1_w", [P, NT, E1])
        gates1(nc, a, g, LG)
        route1(nc, a, LG, W)
        experts1(nc, a, g, W)


def gates1(nc, a, g, LG):
    XNT, IDN, PS = (g[k] for k in ("XNT", "IDN", "PS"))
    with ExitStack() as ctx:
        sb, sem = stage(nc, ctx)
        gw = sb("g1_gw", [E1, P])
        gT = sb("g1_gT", [P, E1])
        xs = sb("g1_xs", [P, 2, BT])
        s_w, s_t, s_g, s_x, s_l, s_r = (sem("g1_" + n) for n in ("weights", "turned", "gates", "x_ready", "logits", "read"))
        with nc.Block() as block:
            @block.sync
            def _(sp):
                sp.dma_start(gw[:, :], a["L1_ffn_gate_w"]).then_inc(s_w, 16)
                sp.wait_ge(s_w, 16)

            @block.tensor
            def _(pe):
                pe.wait_ge(s_w, 16)
                pe.transpose(PS[:, 7, 0:E1], gw[:, :], IDN[0:E1, 0:E1]).then_inc(s_t, 1)
                pe.wait_ge(s_g, 1)
                with pe.Fori(0, NBLK // 2) as it:
                    for u in range(2):
                        n = 2 * it + u
                        pe.wait_ge(s_x, n + 1)
                        pe.wait_ge(s_r, n)
                        for j in range(TPB):
                            mm = pe.matmul(PS[:, u, j * E1:(j + 1) * E1], xs[:, u, j * P:(j + 1) * P], gT[:, :],
                                           start=True, stop=True)
                        mm.then_inc(s_l, 1)

            @block.scalar
            def _(act):
                act.wait_ge(s_t, 1)
                act.activation(gT[:, :], PS[:, 7, 0:E1], ACT.Copy).then_inc(s_g, 1)
                with act.Fori(0, NBLK // 2) as it:
                    for u in range(2):
                        n = 2 * it + u
                        act.wait_ge(s_r, n)
                        act.activation(xs[:, u, :], XNT[:, bass.ds(BT * n, BT)], ACT.Copy).then_inc(s_x, 1)

            @block.vector
            def _(dve):
                dve.drain().then_inc(s_r, 1)
                with dve.Fori(0, NBLK // 2) as it:
                    for u in range(2):
                        n = 2 * it + u
                        dve.wait_ge(s_l, n + 1)
                        dve.tensor_copy(LG[:, bass.ds(TPB * n, TPB), :],
                                        PS[:, u, 0:TPB * E1].rearrange("p (j c) -> p j c", j=TPB)).then_inc(s_r, 1)


def route1(nc, a, LG, W):
    with ExitStack() as ctx:
        sb, sem = stage(nc, ctx)
        low = sb("r1_low", [P, E1 * E1])
        gm = sb("r1_gm", [P, NT])
        gs = sb("r1_gs", [P, NT])
        gr = sb("r1_gr", [P, NT])
        p = sb("r1_p", [P, NT, E1])
        t1 = sb("r1_t1", [P, NT, E1, E1])
        t2 = sb("r1_t2", [P, NT, E1, E1])
        rank = sb("r1_rank", [P, NT, E1])
        s_l, s_d, s_e, s_c = (sem("r1_" + n) for n in ("loaded", "differences", "exps", "chain"))
        with nc.Block() as block:
            @block.sync
            def _(sp):
                sp.dma_start(low[:, :], broadcast_rows(a["c_lower1"], P, E1 * E1)).then_inc(s_l, 16)
                sp.wait_ge(s_l, 16)

            @block.scalar
            def _(act):
                act.wait_ge(s_d, 1)
                act.activation(p[:, :, :], p[:, :, :], ACT.Exp).then_inc(s_e, 1)

            @block.vector
            def _(dve):
                ch = Chain(dve, s_c)
                per = [[1, NT], [0, E1]]
                ch.link(dve.tensor_reduce(gm[:, :], LG[:, :, :], AX.X, ALU.max))
                dve.tensor_tensor(p[:, :, :], LG[:, :, :], bc(gm[:, :], per), ALU.subtract).then_inc(s_d, 1)
                dve.wait_ge(s_e, 1)
                ch.link(dve.tensor_reduce(gs[:, :], p[:, :, :], AX.X, ALU.add))
                ch.link(dve.reciprocal(gr[:, :], gs[:, :]))
                ch.link(dve.tensor_tensor(p[:, :, :], p[:, :, :], bc(gr[:, :], per), ALU.mult))
                dve.wait_ge(s_l, 16)
                top2(dve, ch, p[:, :, :], W[:, :, :], low[:, :], t1[:, :, :, :], t2[:, :, :, :], rank[:, :, :], NT, E1)
                ch.link(dve.tensor_reduce(gs[:, :], W[:, :, :], AX.X, ALU.add))
                ch.link(dve.tensor_scalar(gm[:, :], gs[:, :], 1e-10, None, ALU.max))
                ch.link(dve.reciprocal(gr[:, :], gm[:, :]))
                ch.link(dve.tensor_tensor(W[:, :, :], W[:, :, :], bc(gr[:, :], per), ALU.mult))


def experts1(nc, a, g, W):
    X, XN, XNT, PS = (g[k] for k in ("X", "XN", "XNT", "PS"))
    FT = F1 // P
    with ExitStack() as ctx:
        sb, sem = stage(nc, ctx)
        w1 = sb("e1_w1", [P, E1, F1])
        w2 = sb("e1_w2", [P, E1, FT, D])
        b1 = sb("e1_b1", [P, E1, FT])
        b2 = sb("e1_b2", [P, E1, D])
        hh = sb("e1_hh", [P, 2, FT, BT])
        acc = sb("e1_acc", [P, TPB, D])
        s_w, s_up, s_h, s_dn, s_ac, s_cl, s_x = (sem("e1_" + n) for n in (
            "weights", "up_done", "hidden", "down_done", "combined", "clipped", "x_added"))
        adds = 2 * E1 * TPB
        with nc.Block() as block:
            @block.sync
            def _(sp):
                sp.dma_start(w1[:, :, :], a["L1_ffn_w1"].rearrange("e d f -> d e f")).then_inc(s_w, 16)
                for f in range(FT):
                    sp.dma_start(w2[:, :, f, :], a["L1_ffn_w2"][:, f * P:(f + 1) * P, :].rearrange(
                        "e p d -> p e d")).then_inc(s_w, 16)
                sp.dma_start(b1[:, :, :], a["L1_ffn_b1"].rearrange("e (f p) -> p e f", p=P),
                             allow_slow_non_contiguous=True).then_inc(s_w, 16)
                sp.dma_start(b2[:, :, :], broadcast_rows(a["L1_ffn_b2"], P, E1 * D).rearrange(
                    "p (e d) -> p e d", d=D)).then_inc(s_w, 16)
                sp.wait_ge(s_w, 80)

            @block.tensor
            def _(pe):
                pe.wait_ge(s_w, 80)
                with pe.Fori(0, NBLK) as n:
                    def up(e):
                        i = E1 * n + e
                        if e >= 2:
                            pe.wait_ge(s_h, FT * (i - 1))
                        else:
                            pe.wait_ge(s_h, FT * E1 * n)
                        for f in range(FT):
                            pe.matmul(PS[:, FT * (e % 2) + f, :], w1[:, e, f * P:(f + 1) * P],
                                      XNT[:, bass.ds(BT * n, BT)], start=True, stop=True).then_inc(s_up, 1)

                    def down(e):
                        i = E1 * n + e
                        pe.wait_ge(s_h, FT * (i + 1))
                        pe.wait_ge(s_ac, adds * n + 2 * TPB * max(e - 1, 0))
                        for j in range(TPB):
                            for f in range(FT):
                                mm = pe.matmul(PS[:, 4 + e % 2, j * P:(j + 1) * P], hh[:, e % 2, f, j * P:(j + 1) * P],
                                               w2[:, e, f, :], start=(f == 0), stop=(f == FT - 1))
                        mm.then_inc(s_dn, 1)

                    up(0)
                    for e in range(E1):
                        if e + 1 < E1:
                            up(e + 1)
                        down(e)

            @block.scalar
            def _(act):
                act.wait_ge(s_w, 80)
                with act.Fori(0, NBLK) as n:
                    for e in range(E1):
                        i = E1 * n + e
                        act.wait_ge(s_dn, i - 1 if e >= 2 else E1 * n)
                        for f in range(FT):
                            act.wait_ge(s_up, FT * i + f + 1)
                            act.activation(hh[:, e % 2, f, :], PS[:, FT * (e % 2) + f, :], ACT.Gelu,
                                           bias=b1[:, e, f:f + 1]).then_inc(s_h, 1)

            @block.vector
            def _(dve):
                dve.wait_ge(s_w, 80)
                with dve.Fori(0, NBLK) as n:
                    for e in range(E1):
                        for k in range(2):
                            if k:
                                dve.wait_ge(s_dn, E1 * n + e + 1)
                            for j in range(TPB):
                                if e or k:
                                    dve.wait_ge(s_ac, adds * n + TPB * (2 * e + k - 1) + j + 1)
                                dve.scalar_tensor_tensor(
                                    acc[:, j, :], PS[:, 4 + e % 2, j * P:(j + 1) * P] if k else b2[:, e, :],
                                    W[:, TPB * n + j, e:e + 1], acc[:, j, :] if e or k else XN[:, TPB * n + j, :],
                                    ALU.mult, ALU.add).then_inc(s_ac, 1)
                    dve.wait_ge(s_ac, adds * (n + 1))
                    dve.tensor_scalar(acc[:, :, :], acc[:, :, :], 100.0, -100.0, ALU.min, ALU.max).then_inc(s_cl, 1)
                    dve.wait_ge(s_cl, n + 1)
                    xb = X[:, bass.ds(TPB * n, TPB), :]
                    dve.scalar_tensor_tensor(xb, acc[:, :, :], 0.5, xb, ALU.mult, ALU.add).then_inc(s_x, 1)
                    dve.wait_ge(s_x, n + 1)


def causal(nc, a, g):
    with ExitStack() as ctx:
        sb, sem = stage(nc, ctx)
        YT = sb("ca_yt", [P, BATCH + 1, SEQ])
        causal_attention(nc, a, g, YT)
        causal_output(nc, a, g, YT)


def causal_attention(nc, a, g, YT):
    XNT, IDN, PS = (g[k] for k in ("XNT", "IDN", "PS"))
    ITERS = BATCH * NP
    C = H1 * HD
    STEPS = [(qc, kt) for qc in range(HALVES) for kt in range(TPB * (qc + 1))]
    NS = len(STEPS)
    TILES = [(h, t, c) for h in range(2) for t in range(KT) for c in range(t // TPB + 1)]
    VTILES = [range(0, 3), range(3, 6), range(6, KT)]
    PREP = ([("q", 0), ("q", 1), ("k", 0), ("k", 1)] + [("v", i) for i in range(len(VTILES))]
            + [("t", i) for i in range(len(TILES))] + [("m", 0)])
    OUT = {2: ("z", 1), 4: ("y", 1), TPB + 2: ("z", 0), TPB + 4: ("y", 0)}
    CHUNKS = 4
    ADDS = [sum(kt > 0 for _, kt in STEPS[:s]) for s in range(NS + 1)]
    LEAD = 2
    RING, at = [], 0
    for s in range(NS):
        upto = min(len(PREP) * (s + 1) // (NS - LEAD), len(PREP))
        RING.append(([OUT[s]] if s in OUT else []) + PREP[at:upto])
        at = upto
    USES = sum(map(len, RING))
    PRO = len(PREP)
    PLACE = {use: i for i, use in enumerate(x for uses in RING for x in uses)}
    AT = {i: use for use, i in PLACE.items()}
    assert USES % 3 == 0
    assert all(PLACE["y", i] - PLACE["z", i] > CHUNKS + 1 for i in range(2))
    with ExitStack() as ctx:
        sb, sem = stage(nc, ctx)
        w = sb("ca_w", [P, 2, 3, P])
        bqk = sb("ca_bqk", [P, 2, 2])
        bv = sb("ca_bv", [P, 2, P])
        wo = sb("ca_wo", [P, 2, D])
        tri = sb("ca_tri", [P, 3, P])
        trb = sb("ca_trb", [P, 3, P], BF16)
        ones = sb("ca_ones", [P, HD])
        xs = sb("ca_xs", [P, 2, SEQ])
        Q = sb("ca_q", [P, 2, 2, SEQ])
        K = sb("ca_k", [P, 2, 2, SEQ])
        qb = sb("ca_qb", [P, 2, SEQ], BF16)
        kb = sb("ca_kb", [P, SEQ], BF16)
        VA = sb("ca_v", [P, 2, KT, P])
        PR = sb("ca_p", [P, 3, 2, BT])
        S = sb("ca_s", [P, 2, 2, BT])
        ot = sb("ca_ot", [P, BT])
        su = sb("ca_su", [P, BT])
        z = sb("ca_z", [P, BT])
        on = sb("ca_on", [P, BT])
        mh = sb("ca_mh", [P, 2 * KT, HALVES])
        m = sb("ca_m", [P, 2 * KT])
        nm = sb("ca_nm", [2 * KT, P])
        s_wl = [sem(f"ca_w_loaded{u}") for u in range(2)]
        s_mr = [sem(f"ca_max_rows{u}") for u in range(2)]
        s_wo = [sem(f"ca_wo_loaded{u}") for u in range(2)]
        (s_c, s_set, s_x, s_ring, s_rd, s_mx, s_st, s_exp, s_pv, s_ot,
         s_first, s_sum, s_z, s_on) = (
            sem("ca_" + n) for n in (
                "constants", "set", "x_ready", "ring_filled", "ring_read", "m_ready", "scores_ready",
                "exp_done", "pv_done", "o_copied",
                "first_exps", "exps_added", "z_ready", "o_divided"))
        SETS = 14

        def number(n, use):
            return PRO + USES * n + PLACE[use]

        def behind(n, qc):
            return HALVES * n if qc else HALVES * n + 1

        def added(n, qc):
            return ADDS[NS] * n + (0 if qc else ADDS[TPB]) + 2

        with nc.Block() as block:
            @block.sync
            def _(sp):
                sp.dma_start(tri[:, :, :], a["c_masks"]).then_inc(s_c, 16)
                wout = a["L1_attn_W_out"].rearrange("(p c) f -> p c f", p=NP)
                wqkv = a["L1_attn_W_qkv"].rearrange("f (t p c) -> p f t c", t=3, p=NP)
                bias = a["L1_attn_b_qkv"].rearrange("(t p c) -> p c t", t=3, p=NP)

                def load(n, u):
                    sp.dma_start(w[:, u, :, :], wqkv[n]).then_inc(s_wl[u], 16)
                    sp.dma_start(bqk[:, u, :], bias[n, :, 0:2], allow_slow_non_contiguous=True).then_inc(s_wl[u], 16)
                    row = bias[n, :, 2:3]
                    sp.dma_start(bv[:, u, :], bass.AP(row.tensor, row.offset, [[0, P], [1, P]])).then_inc(s_wl[u], 16)

                def max_rows(reads, u):
                    sp.wait_ge(s_rd, reads)
                    for h in range(2):
                        sp.dma_start(Q[HD * (1 - h):HD * (1 - h) + 1, u, h, :].rearrange("o (t p) -> o t p", p=P),
                                     nm[KT * h:KT * (h + 1), :]).then_inc(s_mr[u], 16)

                load(0, 0)
                load(1, 1)
                max_rows(PRO, 0)
                with sp.Fori(0, ITERS // 2) as it:
                    for u in range(2):
                        n = 2 * it + u
                        sp.wait_ge(s_rd, PRO + USES * n)
                        load((n + 2) % NP, u)
                        sp.dma_start(wo[:, u, :], wout[n % NP]).then_inc(s_wo[u], 16)
                        max_rows(number(n, ("m", 0)) + 1, 1 - u)
                for u in range(2):
                    sp.wait_ge(s_wl[u], 48 * (ITERS // 2 + 1))
                    sp.wait_ge(s_mr[u], 32 * (ITERS // 2 + 1 - u))

            @block.tensor
            def _(pe):
                def turn(num, place, use, u, rd_k):
                    kind, i = use
                    bank = 5 + place % 3
                    if not isinstance(num, int) or num >= 3:
                        pe.wait_ge(s_rd, num - 2)
                    if kind in "qk":
                        mm = pe.matmul(PS[:, bank, :], w[:, u, "qk".index(kind), :], xs[:, u, i * BT:(i + 1) * BT],
                                       start=True, stop=True)
                    elif kind == "v":
                        for j, t in enumerate(VTILES[i]):
                            mm = pe.matmul(PS[:, bank, j * P:(j + 1) * P], xs[:, u, t * P:(t + 1) * P], w[:, u, 2, :],
                                           start=True, stop=True)
                    elif kind == "t":
                        if i == 0:
                            pe.wait_ge(s_rd, rd_k)
                        h, t, c = TILES[i]
                        width = min(BT, (t + 1) * P - c * BT)
                        diagonal = c == t // TPB
                        mm = pe.matmul(PS[:, bank, 0:width], qb[:, h, t * P:(t + 1) * P], kb[:, c * BT:c * BT + width],
                                       start=True, stop=not diagonal)
                        if diagonal:
                            mm = pe.matmul(PS[:, bank, width - P:width], trb[:, 0, :], trb[:, 1, :], start=False, stop=True)
                    elif kind == "m":
                        mm = pe.transpose(PS[0:2 * KT, bank, 0:P], m[:, :], IDN[:, :])
                    elif kind == "z":
                        for h in range(2):
                            mm = pe.matmul(PS[HD * h:HD * (h + 1), bank, :], ones[:, :], S[:, i, h, :], start=True,
                                           stop=True, skip_group_check=True)
                    else:
                        mm = pe.matmul(PS[:, bank, :], wo[:, u, :], on[:, :], start=True, stop=True)
                    mm.then_inc(s_ring, 1)

                def span(s):
                    qc, kt = STEPS[s]
                    return max(0, kt * P - qc * BT)

                def scores(n, s, u):
                    qc, kt = STEPS[s]
                    off, diagonal = span(s), kt >= qc * TPB
                    pe.wait_ge(s_exp, NS * n + s)
                    for h in range(2):
                        bank = 2 * (s % 2) + h
                        mm = pe.matmul(PS[:, bank, off:BT], K[:, u, h, kt * P:(kt + 1) * P],
                                       Q[:, u, h, qc * BT + off:(qc + 1) * BT], start=True, stop=not diagonal)
                        if diagonal:
                            mm = pe.matmul(PS[:, bank, off:off + P], trb[:, 0, :], trb[:, 2, :], start=False, stop=True)
                    mm.then_inc(s_st, 1)

                def weigh(n, s, u):
                    qc, kt = STEPS[s]
                    off, last = span(s), s + 1 == NS or STEPS[s + 1][0] != qc
                    if kt == 0:
                        pe.wait_ge(s_ot, HALVES * n + qc)
                    pe.wait_ge(s_exp, NS * n + s + 2)
                    for h in range(2):
                        mm = pe.matmul(PS[HD * h:HD * (h + 1), 4, off:BT], VA[:, u, kt, HD * h:HD * (h + 1)],
                                       PR[:, s % 3, h, off:BT], start=(kt == 0), stop=last, skip_group_check=True)
                    mm.then_inc(s_pv, 1)

                pe.wait_ge(s_c, 16)
                pe.wait_ge(s_set, SETS)
                pe.wait_ge(s_wl[0], 48)
                pe.wait_ge(s_x, 1)
                for i, use in enumerate(PREP):
                    if use[0] == "m":
                        pe.wait_ge(s_mx, 1)
                    turn(i, i, use, 0, PREP.index(("k", 1)) + 1)
                with pe.Fori(0, ITERS // 2) as it:
                    for u in range(2):
                        n = 2 * it + u
                        for s in range(NS):
                            if s == 0:
                                pe.wait_ge(s_mr[u], 32 * (it + 1))
                            scores(n, s, u)
                            for i, use in enumerate(RING[s] + [None]):
                                if s and i == len(RING[s]) // 2:
                                    weigh(n, s - 1, u)
                                if use is None:
                                    continue
                                kind, half = use
                                if use == ("q", 0):
                                    pe.wait_ge(s_wl[1 - u], 48 * (it + 1 + u))
                                    pe.wait_ge(s_x, n + 2)
                                elif kind == "m":
                                    pe.wait_ge(s_mx, n + 2)
                                elif kind == "z":
                                    pe.wait_ge(s_sum, added(n, half))
                                elif kind == "y":
                                    pe.wait_ge(s_on, behind(n, half) + 1)
                                    pe.wait_ge(s_wo[(u - half) % 2], 16 * (it + 1 - (half if u == 0 else 0)))
                                of_last = kind in "zy" and half == 1
                                buffers = u if kind in "zy" and half == 0 else 1 - u
                                assert of_last or kind not in "zy" or buffers == u
                                turn(number(n, use), PRO + PLACE[use], use, buffers, number(n, ("k", 1)) + 1)
                        weigh(n, NS - 1, u)
                pe.wait_ge(s_sum, added(ITERS, 1))
                turn(PRO + USES * ITERS, PRO, ("z", 1), 1, 0)
                pe.wait_ge(s_on, behind(ITERS, 1) + 1)
                turn(PRO + USES * ITERS + 1, PRO + 1, ("y", 1), 1, 0)

            @block.scalar
            def _(act):
                act.drain().then_inc(s_exp, 1)
                act.wait_ge(s_c, 16)
                for n1 in range(2):
                    act.activation(xs[:, n1, :], XNT[:, 0:SEQ], ACT.Copy).then_inc(s_x, 1)

                def output(n, qc, steps):
                    act.wait_ge(s_pv, NS * n + steps + 2)
                    act.wait_ge(s_on, HALVES * n + qc + 1)
                    act.activation(ot[:, :], PS[:, 4, :], ACT.Copy).then_inc(s_ot, 1)

                act.wait_ge(s_set, SETS)
                with act.Fori(0, ITERS // 2) as it:
                    for u in range(2):
                        n = 2 * it + u
                        for s in range(NS):
                            qc, kt = STEPS[s]
                            off = max(0, kt * P - qc * BT)
                            act.wait_ge(s_st, NS * n + s + 1)
                            act.wait_ge(s_pv, NS * n + s)
                            act.wait_ge(s_sum, ADDS[NS] * n + (ADDS[s - 2] + 2 if s >= 2 else 2 - (2 - s)))
                            act.activation(PR[:, s % 3, :, off:BT], PS[:, 2 * (s % 2):2 * (s % 2) + 2, off:BT],
                                           ACT.Exp, scale=float(HD) ** -0.5).then_inc(s_exp, 1)
                            if kt == 0:
                                act.wait_ge(s_ring, number(n, ("z", qc)) + 1 - (0 if qc else USES))
                                act.wait_ge(s_exp, NS * n + s + 2)
                                act.activation(S[:, qc, :, :], PR[:, s % 3, :, :], ACT.Copy).then_inc(s_first, 1)
                            if s == TPB:
                                output(n, 0, TPB)
                            if s == NS - 2:
                                act.wait_ge(s_ring, PRO + USES * n)
                                act.activation(xs[:, u, :], XNT[:, bass.ds(SEQ * ((n + 2) % ITERS // NP), SEQ)],
                                               ACT.Copy).then_inc(s_x, 1)
                        output(n, 1, NS)

            @block.gpsimd
            def _(pool):
                pool.wait_ge(s_set, SETS)
                pool.drain().then_inc(s_sum, 2)
                with pool.Fori(0, ITERS) as n:
                    for s, (qc, kt) in enumerate(STEPS):
                        off = max(0, kt * P - qc * BT)
                        if kt == 0:
                            continue
                        pool.wait_ge(s_exp, NS * n + s + 2)
                        if kt == 1:
                            pool.wait_ge(s_first, HALVES * n + qc + 1)
                        else:
                            pool.wait_ge(s_sum, ADDS[NS] * n + ADDS[s] + 2)
                        pool.tensor_tensor(S[:, qc, :, off:BT], S[:, qc, :, off:BT], PR[:, s % 3, :, off:BT],
                                           ALU.add).then_inc(s_sum, 1)

            @block.vector
            def _(dve):
                def half(q, u, h, i, rows):
                    return q[rows, u, h, i * BT:(i + 1) * BT]

                lower, upper = slice(0, HD), slice(HD, P)
                for u in range(2):
                    dve.memset(Q[upper, u, 0, :], 0.0).then_inc(s_set, 1)
                    dve.memset(Q[lower, u, 1, :], 0.0).then_inc(s_set, 1)
                    dve.memset(K[upper, u, 0, :], 1.0).then_inc(s_set, 1)
                    dve.memset(K[lower, u, 1, :], 1.0).then_inc(s_set, 1)
                dve.memset(qb[upper, 0, :], 0.0).then_inc(s_set, 1)
                dve.memset(qb[lower, 1, :], 0.0).then_inc(s_set, 1)
                dve.memset(ones[:, :], 1.0).then_inc(s_set, 1)
                dve.memset(S[:, 1, :, :], 1.0).then_inc(s_set, 1)
                dve.memset(mh[:, :, :], -3e38)
                dve.memset(ot[:, :], 0.0)
                dve.memset(wo[:, 1, :], 0.0)
                dve.memset(YT[:, :, :], 0.0).then_inc(s_set, 1)
                dve.wait_ge(s_c, 16)
                dve.tensor_copy(trb[:, :, :], tri[:, :, :]).then_inc(s_set, 1)
                dve.wait_ge(s_set, SETS)
                dve.drain().then_inc(s_pv, 2)

                def read(num, place, use, u, n, rows=None):
                    kind, i = use
                    bank = 5 + place % 3
                    dve.wait_ge(s_ring, num + 1)
                    if kind in "qk":
                        t = "qk".index(kind)
                        full = (Q, K)[t]
                        for h, r in enumerate((lower, upper)):
                            dve.tensor_scalar(half(full, u, h, i, r), PS[r, bank, :], bqk[r, u, t:t + 1], None, ALU.add)
                            if kind == "q":
                                ins = dve.tensor_scalar(qb[r, h, i * BT:(i + 1) * BT], PS[r, bank, :], bqk[r, u, t:t + 1],
                                                        None, ALU.add)
                        if kind == "k":
                            ins = dve.tensor_scalar(kb[:, i * BT:(i + 1) * BT], PS[:, bank, :], bqk[:, u, t:t + 1],
                                                    None, ALU.add)
                    elif kind == "v":
                        t = VTILES[i]
                        ins = dve.tensor_tensor(VA[:, u, t[0]:t[-1] + 1, :],
                                                PS[:, bank, 0:len(t) * P].rearrange("p (j c) -> p j c", j=len(t)),
                                                bc(bv[:, u, :], [[0, len(t)], [1, P]]), ALU.add)
                    elif kind == "t":
                        h, t, c = TILES[i]
                        width = min(BT, (t + 1) * P - c * BT)
                        ins = dve.tensor_reduce(mh[:, h * KT + t, c:c + 1], PS[:, bank, 0:width], AX.X, ALU.max)
                    elif kind == "m":
                        dve.wait_ge(*rows)
                        ins = dve.tensor_scalar(nm[:, :], PS[0:2 * KT, bank, 0:P], -1.0, None, ALU.mult)
                    elif kind == "z":
                        ins = dve.tensor_copy(su[:, :], PS[:, bank, :])
                    else:
                        dve.wait_ge(s_rd, num)
                        y = YT[:, (n + NP - 1) // NP if i else n // NP + 1, i * BT:(i + 1) * BT]
                        ins = dve.tensor_tensor(y, y, PS[:, bank, :], ALU.add)
                    ins.then_inc(s_rd, 1)

                def invert(num, past, chunk):
                    if chunk < CHUNKS:
                        cols = slice(chunk * BT // CHUNKS, (chunk + 1) * BT // CHUNKS)
                        dve.wait_ge(s_rd, num + 1)
                        dve.reciprocal(z[:, cols], su[:, cols]).then_inc(s_z, 1)
                    else:
                        dve.wait_ge(s_z, CHUNKS * (past + 1))
                        dve.wait_ge(s_ot, past)
                        dve.tensor_tensor(on[:, :], ot[:, :], z[:, :], ALU.mult).then_inc(s_on, 1)

                def maxima(num):
                    dve.wait_ge(s_rd, num)
                    dve.tensor_reduce(m[:, :], mh[:, :, :], AX.X, ALU.max).then_inc(s_mx, 1)

                dve.wait_ge(s_wl[0], 48)
                for i, use in enumerate(PREP):
                    if use[0] == "m":
                        maxima(i)
                    read(i, i, use, 0, 0, (s_set, SETS))
                with dve.Fori(0, ITERS // 2) as it:
                    for u in range(2):
                        n = 2 * it + u
                        for s in range(NS):
                            for use in RING[s]:
                                if use == ("q", 0):
                                    dve.wait_ge(s_wl[1 - u], 48 * (it + 1 + u))
                                if use[0] == "m":
                                    maxima(number(n, use))
                                read(number(n, use), PRO + PLACE[use], use, 1 - u, n, (s_mr[u], 32 * (it + 1)))
                                for chunk in range(CHUNKS + 1):
                                    z_use = AT.get(PLACE[use] - 1 - chunk)
                                    if z_use and z_use[0] == "z":
                                        invert(number(n, z_use), behind(n, z_use[1]), chunk)
                read(PRO + USES * ITERS, PRO, ("z", 1), 1, ITERS)
                for chunk in range(CHUNKS + 1):
                    invert(PRO + USES * ITERS, behind(ITERS, 1), chunk)
                read(PRO + USES * ITERS + 1, PRO + 1, ("y", 1), 1, ITERS)


def causal_output(nc, a, g, YT):
    X, IDN, PS = (g[k] for k in ("X", "IDN", "PS"))
    with ExitStack() as ctx:
        sb, sem = stage(nc, ctx)
        bo = sb("co_bo", [P, 1])
        yb = sb("co_yb", [P, 2, BT])
        s_c, s_y, s_t, s_a = (sem("co_" + n) for n in ("bias", "y_biased", "y_turned", "added"))
        with nc.Block() as block:
            @block.sync
            def _(sp):
                sp.dma_start(bo[:, :], a["L1_attn_b_out"].rearrange("(f o) -> f o", o=1),
                             allow_slow_non_contiguous=True).then_inc(s_c, 16)
                sp.wait_ge(s_c, 16)

            @block.scalar
            def _(act):
                act.wait_ge(s_c, 16)
                with act.Fori(0, BATCH) as b:
                    for u in range(2):
                        act.wait_ge(s_t, 2 * b)
                        act.activation(yb[:, u, :], YT[:, b + 1, u * BT:(u + 1) * BT], ACT.Identity,
                                       bias=bo[:, 0:1]).then_inc(s_y, 1)

            @block.tensor
            def _(pe):
                with pe.Fori(0, BATCH) as b:
                    for u in range(2):
                        n = 2 * b + u
                        pe.wait_ge(s_y, n + 1)
                        pe.wait_ge(s_a, 2 * b)
                        for j in range(TPB):
                            mm = pe.transpose(PS[:, u, j * P:(j + 1) * P], yb[:, u, j * P:(j + 1) * P], IDN[:, :])
                        mm.then_inc(s_t, 1)

            @block.vector
            def _(dve):
                with dve.Fori(0, BATCH) as b:
                    for u in range(2):
                        n = 2 * b + u
                        dve.wait_ge(s_t, n + 1)
                        xb = X[:, bass.ds(TPB * n, TPB), :]
                        dve.tensor_tensor(xb, xb, PS[:, u, :].rearrange("p (j c) -> p j c", j=TPB),
                                          ALU.add).then_inc(s_a, 1)


def constants():
    dim = np.arange(P) % DH
    inv = np.float32(1.0) / np.float32(10000.0) ** (np.arange(0, DH, 2, dtype=np.float32) / np.float32(DH))
    angle = (np.arange(SEQ, dtype=np.float32)[None, :] * inv.astype(np.float32)[dim // 2][:, None]).astype(np.float32)
    pb = BT // P
    spread = np.zeros((P, NP, P), np.float32)
    rows = np.zeros((P, NP // pb, VW), np.float32)
    for h in range(2):
        for p in range(NP):
            spread[32 * (p % pb) + 2 * (p // pb) + h, p, h * HD:(h + 1) * HD] = 1.0
        for k in range(NP // pb):
            rows[h * HD:(h + 1) * HD, k, 2 * k + h] = 1.0
    return {
        "c_ident": np.eye(P, dtype=np.float32),
        "c_rope": np.stack([np.cos(angle), np.sin(angle)]).astype(np.float32),
        "c_lower0": np.tril(np.ones((E0, E0), np.float32), -1),
        "c_spread": spread,
        "c_rows": rows,
        "c_blocks": np.kron(np.eye(2, dtype=np.float32), np.ones((HD, HD), np.float32)),
        "c_masks": np.stack([np.eye(P) * MASK_ROW, np.triu(np.ones((P, P)), 1) * MASK_COL,
                             np.tril(np.ones((P, P)), -1) * MASK_COL], axis=1).astype(np.float32),
        "c_lower1": np.tril(np.ones((E1, E1), np.float32), -1),
    }


_INS = ["L0_attn_x", "L0_attn_wq", "L0_attn_bq", "L0_attn_wk", "L0_attn_bk", "L0_attn_wv", "L0_attn_bv", "L0_attn_wo",
        "L0_attn_bo", "L0_ffn_Wq", "L0_ffn_Wk_c", "L0_ffn_Wv_c", "L0_ffn_Wk", "L0_ffn_Wv", "L0_ffn_Wo",
        "L0_ffn_W_shared_in", "L0_ffn_W_shared_out", "L0_ffn_W1_shared", "L0_ffn_W2_experts", "L0_ffn_Wg_gate",
        "L0_ffn_We_gate", "L0_ffn_group_bias", "L0_ffn_expert_bias", "L0_ffn_norm1_w", "L0_ffn_norm2_w",
        "L1_attn_W_qkv", "L1_attn_b_qkv", "L1_attn_W_out", "L1_attn_b_out", "L1_ffn_gate_w", "L1_ffn_w1", "L1_ffn_b1",
        "L1_ffn_w2", "L1_ffn_b2"]


def kernel(**inputs):
    import concourse.bacc as bacc
    from concourse.bass_utils import run_bass_kernel_spmd

    nc = bacc.Bacc("TRN2", target_bir_lowering=False, num_devices=1)
    arrays, args = {}, {}
    for name, value in [(n, inputs[n]) for n in _INS] + list(constants().items()):
        array = np.ascontiguousarray(value)
        arrays[f"in_{name}"] = array
        args[name] = nc.dram_tensor(f"in_{name}", array.shape, mybir.dt.from_np(array.dtype), kind="ExternalInput").ap()
    out = nc.dram_tensor("out_0_dram", [BATCH, SEQ, D], F32, kind="ExternalOutput").ap()
    build(nc, args, out)
    results = run_bass_kernel_spmd(nc, [arrays], core_ids=[0])
    return results.results[0]["out_0_dram"]
```

```python
from contextlib import ExitStack
from itertools import count

import numpy as np

import concourse.bass as bass
from concourse import mybir

F32 = mybir.dt.float32
BF16 = mybir.dt.bfloat16
ALU = mybir.AluOpType
ACT = mybir.ActivationFunctionType
AX = mybir.AxisListType

P = 128
BATCH, SEQ, D = 4, 1024, 128
TOKENS = BATCH * SEQ
BT = 512
TPB = BT // P
NBLK = TOKENS // BT
NT = TOKENS // P
HALVES = SEQ // BT

H0, DH = 16, 8
GH = 4
NG = H0 // GH
PARTS = 3
STK = PARTS * PARTS * DH
KMAX = 96
KROWS = KMAX + PARTS
VW = 32
KT = SEQ // P

HID, E0, EPG = 256, 8, 4
GA = 2
H1, HD = 16, 64
NP = H1 // 2
E1, F1 = 14, 256

LN_EPS, RMS_EPS, LIN_EPS = 1e-5, 1e-6, 1e-6
MASK_ROW, MASK_COL = 250.0, -320.0


class Chain:

    def __init__(self, engine, sem, start=0):
        self.engine, self.sem, self.start, self.n = engine, sem, start, 0

    def tick(self, ins):
        ins.then_inc(self.sem, 1)
        self.n += 1

    def wait(self):
        self.engine.wait_ge(self.sem, self.start + self.n)

    def link(self, ins):
        self.tick(ins)
        self.wait()


def bc(ap, dims):
    return bass.AP(ap.tensor, ap.offset, [list(ap.ap[0])] + [list(d) for d in dims])


def build(nc, a, out):
    SEMS.clear()
    with ExitStack() as ctx:
        X = ctx.enter_context(nc.sbuf_tensor("X", [P, NT + TPB, D], F32))
        XN = ctx.enter_context(nc.sbuf_tensor("XN", [P, NT, D], F32))
        XNT = ctx.enter_context(nc.sbuf_tensor("XNT", [P, TOKENS], F32))
        IDN = ctx.enter_context(nc.sbuf_tensor("IDN", [P, P], F32))
        PS = ctx.enter_context(nc.psum_tensor("PS", [P, 8, BT], F32))
        PW = ctx.enter_context(nc.sbuf_tensor("PW", [P, TPB], F32))
        scratch = dict(
            QK=nc.dram_tensor("qk_parts", [2, BATCH * H0, PARTS, DH, SEQ], BF16, kind="Internal").ap(),
            V=nc.dram_tensor("v_heads", [BATCH * NG, SEQ, GH * DH], F32, kind="Internal").ap(),
            O=nc.dram_tensor("o_heads", [BATCH * NG + 1, P, SEQ], F32, kind="Internal").ap(),
        )
        g = dict(X=X, XN=XN, XNT=XNT, IDN=IDN, PS=PS, PW=PW, **scratch)
        start(nc, a, g)
        rope(nc, a, g)
        ffn0(nc, a, g)
        clear_semaphores(nc)
        linear_attention(nc, a, g)
        clear_semaphores(nc)
        rope(nc, a, g)
        ffn0(nc, a, g)
        clear_semaphores(nc)
        ffn1(nc, a, g)
        clear_semaphores(nc)
        causal(nc, a, g)
        clear_semaphores(nc)
        ffn1(nc, a, g)
        finish(nc, g, out)


STAGES = count()
SEMS = []


def stage(nc, ctx):
    number = next(STAGES)

    def sb(name, shape, dt=F32):
        return ctx.enter_context(nc.sbuf_tensor(f"{name}_{number}", shape, dt))

    def sem(name):
        SEMS.append(nc.alloc_semaphore(f"{name}_{number}"))
        return SEMS[-1]
    return sb, sem


def clear_semaphores(nc):
    nc.clear_and_free_semaphores(list(SEMS))
    nc.all_engine_barrier()
    SEMS.clear()


def start(nc, a, g):
    X, IDN, PW = g["X"], g["IDN"], g["PW"]
    with ExitStack() as ctx:
        _, sem = stage(nc, ctx)
        loaded = sem("loaded")
        with nc.Block() as block:
            @block.sync
            def _(sp):
                sp.dma_start(X[:, 0:NT, :], a["L0_attn_x"].rearrange("b (t p) d -> p (b t) d", p=P)).then_inc(loaded, 16)
                sp.dma_start(IDN[:, :], a["c_ident"]).then_inc(loaded, 16)
                sp.wait_ge(loaded, 32)

            @block.gpsimd
            def _(pool):
                pool.memset(X[:, NT:NT + TPB, :], 0.0)
                pool.memset(PW[:, :], -0.5)


def finish(nc, g, out):
    X = g["X"]
    with ExitStack() as ctx:
        _, sem = stage(nc, ctx)
        stored = sem("stored")
        with nc.Block() as block:
            @block.sync
            def _(sp):
                sp.dma_start(out.rearrange("b (t p) d -> p (b t) d", p=P), X[:, 0:NT, :]).then_inc(stored, 16)
                sp.wait_ge(stored, 16)


class LayerNorm:

    COPIES = 2 * NBLK + 2

    def __init__(self, g, sb, sem):
        self.X, self.XN, self.XNT, self.IDN, self.PS, self.PW = (g[k] for k in ("X", "XN", "XNT", "IDN", "PS", "PW"))
        self.st = sb("ln_st", [P, 2, TPB, 6])
        self.mv = sb("ln_mv", [P, 2, TPB, 2])
        self.ve = sb("ln_ve", [P, 2, TPB])
        self.rs = sb("ln_rs", [P, 2, TPB])
        self.xn = sb("ln_xn", [P, 2, TPB, D])
        self.eps = sb("ln_eps", [P, TPB])
        self.mark = sb("ln_mark", [P, 1])
        self.stats_done, self.meanvar, self.vareps, self.rstd, self.normed, self.turned, self.copied = (
            sem("ln_" + n) for n in ("stats", "meanvar", "vareps", "rstd", "normed", "turned", "copied"))

    def vector(self, dve):
        st, mv, xn, X = self.st, self.mv, self.xn, self.X

        def stats(n, u):
            for j in range(TPB):
                dve.bn_stats(st[:, u, j, :], X[:, TPB * n + j, :]).then_inc(self.stats_done, 1)
            dve.wait_ge(self.stats_done, (TPB + 1) * n + TPB)
            dve.memset(self.mark[:, :], 0.0).then_inc(self.stats_done, 1)
            for j in range(TPB):
                dve.bn_aggr(mv[:, u, j, :], st[:, u, j, :]).then_inc(self.meanvar, 1)

        dve.memset(self.eps[:, :], LN_EPS)
        stats(0, 0)
        with dve.Fori(0, NBLK // 2) as it:
            for u in range(2):
                n = 2 * it + u
                stats(n + 1, 1 - u)
                dve.wait_ge(self.rstd, n + 1)
                dve.wait_ge(self.copied, 2 * n)
                for j in range(TPB):
                    dve.tensor_scalar(xn[:, u, j, :], X[:, TPB * n + j, :], mv[:, u, j, 0:1],
                                      self.rs[:, u, j:j + 1], ALU.subtract, ALU.mult).then_inc(self.normed, 1)

    def gpsimd(self, pool):
        with pool.Fori(0, NBLK // 2) as it:
            for u in range(2):
                n = 2 * it + u
                pool.wait_ge(self.meanvar, TPB * n + TPB)
                pool.tensor_tensor(self.ve[:, u, :], self.mv[:, u, :, 1], self.eps[:, :], ALU.add).then_inc(self.vareps, 1)
                pool.wait_ge(self.vareps, n + 1)
                pool.wait_ge(self.normed, TPB * n)
                pool.tensor_tensor(self.rs[:, u, :], self.ve[:, u, :], self.PW[:, :], ALU.pow).then_inc(self.rstd, 1)

    def tensor(self, pe):
        with pe.Fori(0, NBLK // 2) as it:
            for u in range(2):
                n = 2 * it + u
                pe.wait_ge(self.normed, TPB * n + TPB)
                pe.wait_ge(self.copied, 2 * n)
                for j in range(TPB):
                    mm = pe.transpose(self.PS[:, u, j * P:(j + 1) * P], self.xn[:, u, j, :], self.IDN[:, :])
                mm.then_inc(self.turned, 1)
        pe.wait_ge(self.copied, self.COPIES)

    def scalar(self, act):
        act.drain().then_inc(self.copied, 2)
        with act.Fori(0, NBLK // 2) as it:
            for u in range(2):
                n = 2 * it + u
                act.wait_ge(self.normed, TPB * n + TPB)
                act.activation(self.XN[:, bass.ds(TPB * n, TPB), :], self.xn[:, u, :, :], ACT.Copy).then_inc(self.copied, 1)
                act.wait_ge(self.turned, n + 1)
                act.activation(self.XNT[:, bass.ds(BT * n, BT)], self.PS[:, u, :], ACT.Copy).then_inc(self.copied, 1)
        act.wait_ge(self.copied, self.COPIES)


def rope(nc, a, g):
    with ExitStack() as ctx:
        sb, _ = stage(nc, ctx)
        buffers = dict(
            Q=sb("ra_q", [P, 2, GH, SEQ], BF16),
            K=sb("ra_k", [P, 2, GH, SEQ], BF16),
            VA=sb("ra_va", [P, 2, KT, GH, VW]),
            PR=sb("ra_p", [P, 2, GH, BT]),
        )
        rope_project(nc, a, g, buffers)
        rope_attention(nc, g, buffers)


def rope_project(nc, a, g, buffers):
    XNT, IDN, PS = g["XNT"], g["IDN"], g["PS"]
    DC = a["L0_ffn_Wk_c"].shape[1]
    with ExitStack() as ctx:
        sb, sem = stage(nc, ctx)
        ln = LayerNorm(g, sb, sem)
        wq = sb("rp_wq", [P, D])
        wc = sb("rp_wc", [P, 2, DC])
        wkv = sb("rp_wkv", [DC, 2, D])
        wcT = sb("rp_wcT", [DC, 2, P])
        W = sb("rp_W", [P, 5, D])
        ROT = sb("rp_rot", [P, 2, SEQ])
        xs = sb("rp_xs", [P, 2, BT])
        t1 = sb("rp_t1", [P, 2, BT])
        t2 = sb("rp_t2", [P, 2, BT])
        qk = sb("rp_qk", [P, 2, BT])
        res = sb("rp_res", [P, 2, BT])
        parts = sb("rp_parts", [P, 2, PARTS, 2, BT], BF16)
        vs = sb("rp_vs", [P, 2, TPB, D])
        s_ld, s_w, s_wt, s_xs, s_pj, s_rd, s_v, s_pt, s_qk, s_h, s_set = (sem("rp_" + n) for n in (
            "loaded", "weights", "wturned", "x_ready", "projected", "psum_read", "v_copied", "parts_done", "qk_done", "high_done", "set"))
        s_st = [sem(f"rp_qk_stored{u}") for u in range(2)]
        s_vst = [sem(f"rp_v_stored{u}") for u in range(2)]
        with nc.Block() as block:
            @block.sync
            def _(sp):
                sp.dma_start(wq[:, :], a["L0_ffn_Wq"]).then_inc(s_ld, 16)
                sp.dma_start(wc[:, 0, :], a["L0_ffn_Wk_c"]).then_inc(s_ld, 16)
                sp.dma_start(wc[:, 1, :], a["L0_ffn_Wv_c"]).then_inc(s_ld, 16)
                sp.dma_start(wkv[:, 0, :], a["L0_ffn_Wk"]).then_inc(s_ld, 16)
                sp.dma_start(wkv[:, 1, :], a["L0_ffn_Wv"]).then_inc(s_ld, 16)
                sp.dma_start(ROT[:, :, :], a["c_rope"].rearrange("t p s -> p t s")).then_inc(s_ld, 16)
                with sp.Fori(0, BATCH) as b:
                    for u in range(2):
                        n = 2 * b + u
                        sp.wait_ge(s_v, n + 1)
                        for gi in range(NG):
                            sp.dma_start(g["V"][NG * b + gi, u * BT:(u + 1) * BT, :].rearrange("(j p) c -> p j c", p=P),
                                         vs[:, u, :, gi * GH * DH:(gi + 1) * GH * DH]).then_inc(s_vst[u], 16)
                        sp.wait_ge(s_pt, n + 1)
                        for t in range(2):
                            for w in range(PARTS):
                                sp.dma_start(g["QK"][t, bass.ds(H0 * b, H0), w, :, u * BT:(u + 1) * BT],
                                             parts[:, u, w, t, :]).then_inc(s_st[u], 16)
                for u in range(2):
                    sp.wait_ge(s_vst[u], 16 * NG * BATCH)
                    sp.wait_ge(s_st[u], 16 * 2 * PARTS * BATCH)

            @block.tensor
            def _(pe):
                ln.tensor(pe)
                pe.wait_ge(s_ld, 96)
                for t in range(2):
                    mm = pe.transpose(PS[0:DC, 7, t * P:(t + 1) * P], wc[:, t, :], IDN[:, :])
                mm.then_inc(s_wt, 1)
                pe.wait_ge(s_w, 1)
                for t in range(2):
                    mm = pe.matmul(PS[:, 6, t * P:(t + 1) * P], wcT[:, t, :], wkv[:, t, :], start=True, stop=True)
                mm.then_inc(s_wt, 1)
                pe.wait_ge(s_w, 6)
                with pe.Fori(0, BATCH) as b:
                    for u in range(2):
                        n = 2 * b + u
                        pe.wait_ge(s_xs, n + 1)
                        pe.wait_ge(s_rd, 2 * n)
                        for k in range(4):
                            mm = pe.matmul(PS[:, k, :], W[:, k, :], xs[:, u, :], start=True, stop=True)
                        mm.then_inc(s_pj, 1)
                        pe.wait_ge(s_v, n)
                        for j in range(TPB):
                            mm = pe.matmul(PS[:, 4, j * P:(j + 1) * P], xs[:, u, j * P:(j + 1) * P], W[:, 4, :],
                                           start=True, stop=True)
                        mm.then_inc(s_pj, 1)

            @block.gpsimd
            def _(pool):
                ln.gpsimd(pool)
                Q, K, VA, PR = (buffers[k] for k in ("Q", "K", "VA", "PR"))
                second = slice(GH // 2, GH)
                for i, (to, value) in enumerate((
                        (Q[64:128, :, :, :], 0.0), (K[64:96, :, :, :], 0.0), (K[96:128, :, :, :], 1.0),
                        (Q[0:64, 1, second, :], 0.0), (K[0:64, 1, second, :], 0.0), (PR[:, :, :, :], 0.0),
                        (VA[:, :, :, :, :], 0.0), (VA[:, :, :, :, DH:DH + 1], 1.0))):
                    if i:
                        pool.wait_ge(s_set, i)
                    else:
                        pool.wait_ge(ln.rstd, NBLK)
                    pool.memset(to, value).then_inc(s_set, 1)

            @block.vector
            def _(dve):
                ln.vector(dve)
                dve.wait_ge(s_wt, 1)
                dve.tensor_copy(wcT[:, :, :], PS[0:DC, 7, 0:2 * P].rearrange("p (t m) -> p t m", t=2)).then_inc(s_w, 1)
                dve.wait_ge(s_wt, 2)
                dve.tensor_copy(W[:, 0, :], wq[:, :]).then_inc(s_w, 1)
                dve.tensor_copy(W[:, 1, :], PS[:, 6, 0:P]).then_inc(s_w, 1)
                dve.tensor_copy(W[:, 4, :], PS[:, 6, P:2 * P]).then_inc(s_w, 1)
                dve.wait_ge(s_w, 4)
                wv = W[:, 0:4, :].rearrange("p k (i two) -> p k i two", two=2)
                dve.tensor_scalar(wv[:, 2:4, :, 0], wv[:, 0:2, :, 1], -1.0, None, ALU.mult).then_inc(s_w, 1)
                dve.tensor_copy(wv[:, 2:4, :, 1], wv[:, 0:2, :, 0]).then_inc(s_w, 1)
                with dve.Fori(0, BATCH) as b:
                    for u in range(2):
                        n = 2 * b + u
                        cos = bc(ROT[:, 0, u * BT:(u + 1) * BT], [[0, 2], [1, BT]])
                        sin = bc(ROT[:, 1, u * BT:(u + 1) * BT], [[0, 2], [1, BT]])
                        dve.wait_ge(s_pj, 2 * n + 1)
                        dve.tensor_tensor(t1[:, :, :], PS[:, 0:2, :], cos, ALU.mult).then_inc(s_rd, 1)
                        dve.tensor_tensor(t2[:, :, :], PS[:, 2:4, :], sin, ALU.mult).then_inc(s_rd, 1)
                        dve.wait_ge(s_rd, 2 * n + 2)
                        dve.wait_ge(s_h, 4 * n)
                        for t in range(2):
                            dve.tensor_tensor(qk[:, t, :], t1[:, t, :], t2[:, t, :], ALU.add).then_inc(s_qk, 1)
                        for t in range(2):
                            dve.wait_ge(s_h, 4 * n + t + 1)
                            dve.tensor_tensor(res[:, t, :], qk[:, t, :], parts[:, u, 0, t, :],
                                              ALU.subtract).then_inc(s_qk, 1)
                        for t in range(2):
                            dve.wait_ge(s_h, 4 * n + t + 3)
                            ins = dve.tensor_tensor(parts[:, u, 2, t, :], res[:, t, :], parts[:, u, 1, t, :], ALU.subtract)
                        ins.then_inc(s_pt, 1)

            @block.scalar
            def _(act):
                ln.scalar(act)
                act.activation(xs[:, 0, :], XNT[:, 0:BT], ACT.Copy).then_inc(s_xs, 1)
                with act.Fori(0, BATCH) as b:
                    for u in range(2):
                        n = 2 * b + u
                        act.wait_ge(s_pj, 2 * n)
                        act.activation(xs[:, 1 - u, :], XNT[:, bass.ds(BT * ((n + 1) % NBLK), BT)], ACT.Copy).then_inc(s_xs, 1)
                        act.wait_ge(s_pj, 2 * n + 2)
                        act.wait_ge(s_vst[u], 16 * NG * b)
                        act.activation(vs[:, u, :, :], PS[:, 4, :].rearrange("p (j c) -> p j c", j=TPB),
                                       ACT.Copy).then_inc(s_v, 1)
                        act.wait_ge(s_st[u], 16 * 2 * PARTS * b)
                        for w, src in ((0, qk), (1, res)):
                            for t in range(2):
                                act.wait_ge(s_qk, 4 * n + 2 * w + t + 1)
                                act.activation(parts[:, u, w, t, :], src[:, t, :], ACT.Copy).then_inc(s_h, 1)



def rope_attention(nc, g, buffers):
    IDN, PS, QK, V, O = (g[k] for k in ("IDN", "PS", "QK", "V", "O"))
    ITERS = BATCH * NG
    STEPS = HALVES * KT
    PH = GH // 2
    TILES = PH * KT * HALVES
    LOADS = PH * (PARTS + 1)
    LATE = 3
    REST = [(1, c) for c in range(TILES // 2, TILES)]
    FIRST = [(0, c) for c in range(TILES)]
    BEGIN = [(1, c) for c in range(TILES // 2)]
    PRO = FIRST + BEGIN[:LATE] + [("turn", 0)] + BEGIN[LATE:]
    RING = REST + FIRST[:LATE] + [("turn", 1)] + FIRST[LATE:] + BEGIN[:LATE] + [("turn", 0)] + BEGIN[LATE:]
    assert len(RING) % 3 == 0
    with ExitStack() as ctx:
        sb, sem = stage(nc, ctx)
        Q, K, VA, PR = (buffers[k] for k in ("Q", "K", "VA", "PR"))
        vc = sb("ra_vc", [P, 2, KT, GH * DH])
        ot = sb("ra_ot", [P, 2, BT])
        mh = sb("ra_mh", [P, 2, PH * KT, HALVES])
        m = sb("ra_m", [P, 2, PH * KT])
        nm = sb("ra_nm", [PH * KT, P])
        nr = sb("ra_nr", [PH * KT, P])
        mp = sb("ra_mp", [PH * KT, 2, 2, PARTS, P], BF16)
        s_qk = [[sem(f"ra_qk{p}_loaded{u}") for u in range(2)] for p in range(2)]
        s_mr = [[sem(f"ra_max_rows{p}_{u}") for u in range(2)] for p in range(2)]
        s_vl = [sem(f"ra_v_loaded{u}") for u in range(2)]
        s_st = [sem(f"ra_scores_ready{p}") for p in range(2)]
        s_exp = [sem(f"ra_exp_done{p}") for p in range(2)]
        s_os = [sem(f"ra_o_stored{h}") for h in range(2)]
        s_va, s_tile, s_max, s_mx, s_mp, s_pv, s_of, s_ch = (
            sem("ra_" + n) for n in ("v_ready", "tile_ready", "tile_read", "m_ready", "m_parts", "pv_done",
                                     "o_free", "chain"))

        def behind(s, pair, u):
            if pair == 0:
                return u, s
            return (u if s >= KT else 1 - u), (s - KT) % STEPS

        with nc.Block() as block:
            @block.sync
            def _(sp):
                def load(n, pair, u):
                    for j in range(PH * pair, PH * (pair + 1)):
                        k = QK[1, GH * n + j, 0, :, :]
                        sp.dma_start(K[0:STK, u, j, :], bass.AP(k.tensor, k.offset, [
                            [0, PARTS], [SEQ, PARTS * DH], [1, SEQ]])).then_inc(s_qk[pair][u], 16)
                        for i in range(PARTS):
                            q = QK[0, GH * n + j, i, :, :]
                            sp.dma_start(Q[i * PARTS * DH:(i + 1) * PARTS * DH, u, j, :], bass.AP(q.tensor, q.offset, [
                                [0, PARTS], [SEQ, DH], [1, SEQ]])).then_inc(s_qk[pair][u], 16)

                def values(n, u):
                    sp.dma_start(vc[:, u, :, :], V[n].rearrange("(t p) c -> p t c", p=P)).then_inc(s_vl[u], 16)

                def max_rows(ready, pair, u):
                    sp.wait_ge(s_mp, ready)
                    for i in range(PARTS):
                        sp.dma_start(Q[KMAX + i:KMAX + i + 1, u, PH * pair:PH * (pair + 1), :].rearrange(
                            "o j (t p) -> o (j t) p", p=P), mp[:, pair, u, i, :]).then_inc(s_mr[pair][u], 16)

                load(0, 0, 0)
                load(0, 1, 0)
                values(0, 0)
                max_rows(1, 0, 0)
                with sp.Fori(0, ITERS // 2) as it:
                    for u in range(2):
                        n = 2 * it + u
                        after = n + 1 if u == 0 else (n + 1) % ITERS
                        sp.wait_ge(s_st[0], STEPS * n)
                        load(after, 0, 1 - u)
                        max_rows(2 * n + 2, 1, u)
                        sp.wait_ge(s_st[1], STEPS * n + KT)
                        load(after, 1, 1 - u)
                        sp.wait_ge(s_va, n + 1)
                        values(after, 1 - u)
                        max_rows(2 * n + 3, 0, 1 - u)
                sp.wait_ge(s_mr[0][0], 16 * PARTS * (ITERS // 2 + 1))

            @block.gpsimd
            def _(pool):
                def store(n, h, pairs=(0, 1)):
                    pool.wait_ge(s_of, 2 * n + h + 1)
                    for pair in pairs:
                        rows, half = slice(VW * PH * pair, VW * PH * (pair + 1)), (pair + h + 1) % 2
                        pool.dma_start(O[n + (1 if pair < h else 0), rows, half * BT:(half + 1) * BT],
                                       ot[rows, h, :]).then_inc(s_os[h], 16)

                with pool.Fori(0, ITERS) as n:
                    for h in range(2):
                        store(n, h)
                store(ITERS, 0)
                store(ITERS, 1, (1,))
                pool.wait_ge(s_os[0], 32 * (ITERS + 1))
                pool.wait_ge(s_os[1], 32 * ITERS + 16)

            @block.tensor
            def _(pe):
                def ring(number, place, use, n2, u):
                    if not isinstance(number, int) or number >= 3:
                        pe.wait_ge(s_max, number - 2)
                    if use[0] == "turn":
                        pe.wait_ge(s_mx, n2)
                        pe.transpose(PS[0:PH * KT, 5 + place % 3, 0:P], m[:, use[1], :], IDN[:, :]).then_inc(s_tile, 1)
                    else:
                        pair, c = use
                        j, t, h = PH * pair + c // (KT * HALVES), c // HALVES % KT, c % HALVES
                        pe.matmul(PS[:, 5 + place % 3, :], Q[0:KMAX, u, j, t * P:(t + 1) * P],
                                  K[0:KMAX, u, j, h * BT:(h + 1) * BT], start=True, stop=True).then_inc(s_tile, 1)

                def scores(n, s, pair, u):
                    ub, step = behind(s, pair, u)
                    pe.wait_ge(s_exp[pair], STEPS * n + s)
                    for j in (PH * pair, PH * pair + 1):
                        mm = pe.matmul(PS[:, j, :], K[0:KROWS, ub, j, (step % KT) * P:(step % KT + 1) * P],
                                       Q[0:KROWS, ub, j, (step // KT) * BT:(step // KT + 1) * BT], start=True, stop=True)
                    mm.then_inc(s_st[pair], 1)

                def weigh(s, u, pairs=(0, 1), start=None):
                    for pair in pairs:
                        ub, step = behind(s, pair, u)
                        for j in (PH * pair, PH * pair + 1):
                            mm = pe.matmul(PS[VW * j:VW * (j + 1), 4, :], VA[:, ub, step % KT, j, :], PR[:, s % 2, j, :],
                                           start=(s % KT == 0) if start is None else start, stop=(s % KT == KT - 1),
                                           skip_group_check=True)
                    mm.then_inc(s_pv, 1)

                pe.wait_ge(s_va, 1)
                weigh(0, 1, start=True)
                pe.wait_ge(s_qk[0][0], 16 * LOADS)
                for i, use in enumerate(PRO):
                    if use == BEGIN[0]:
                        pe.wait_ge(s_qk[1][0], 16 * LOADS)
                    ring(i, i, use, 1, 0)
                with pe.Fori(0, ITERS // 2) as it:
                    for u in range(2):
                        n = 2 * it + u
                        done = 0
                        for s in range(STEPS):
                            for pair in range(2):
                                if s == KT * pair:
                                    pe.wait_ge(s_mr[pair][u], 16 * PARTS * (it + 1))
                                scores(n, s, pair, u)
                                upto = len(RING) * (2 * s + pair + 1) // (2 * STEPS)
                                while done < upto:
                                    use = RING[done]
                                    if use in (FIRST[0], BEGIN[0]):
                                        pe.wait_ge(s_qk[use[0]][1 - u], 16 * LOADS * (it + 1 + u))
                                    ring(len(PRO) + len(RING) * n + done, len(PRO) + done, use,
                                         2 * n + 2 if use[1] == 1 else 2 * n + 3, u if use in REST else 1 - u)
                                    done += 1
                            if s % KT == 1:
                                pe.wait_ge(s_of, 2 * n + s // KT + 1)
                            if s == 1:
                                pe.wait_ge(s_va, n + 1)
                            weigh((s - 1) % STEPS, u if s else 1 - u)
                for s in range(KT):
                    scores(ITERS, s, 1, 0)
                    if s == 1:
                        pe.wait_ge(s_of, 2 * ITERS + 1)
                    weigh((s - 1) % STEPS, 0 if s else 1, (1,) if s else (0, 1))
                pe.wait_ge(s_exp[1], STEPS * ITERS + KT)
                weigh(KT - 1, 0, (1,))

            @block.scalar
            def _(act):
                def values(u, loads):
                    act.wait_ge(s_vl[u], loads)
                    act.activation(VA[:, u, :, :, 0:DH], vc[:, u, :, :].rearrange("p t (j d) -> p t j d", j=GH),
                                   ACT.Copy).then_inc(s_va, 1)

                def exps(n, s, pair):
                    e = STEPS * n + s + 1
                    act.wait_ge(s_st[pair], e)
                    act.wait_ge(s_pv, e)
                    act.activation(PR[:, s % 2, PH * pair:PH * (pair + 1), :], PS[:, PH * pair:PH * (pair + 1), :],
                                   ACT.Exp, scale=float(DH) ** -0.5).then_inc(s_exp[pair], 1)

                def output(n, h, rows=slice(0, P)):
                    act.wait_ge(s_pv, STEPS * n + KT * h + 2)
                    act.wait_ge(s_os[h], 32 * n)
                    act.activation(ot[rows, h, :], PS[rows, 4, :], ACT.Copy).then_inc(s_of, 1)

                values(0, 16)
                with act.Fori(0, ITERS // 2) as it:
                    for u in range(2):
                        n = 2 * it + u
                        for s in range(STEPS):
                            for pair in range(2):
                                exps(n, s, pair)
                            if s % KT == 0:
                                output(n, s // KT)
                            if s == KT + 4:
                                values(1 - u, 16 * (it + 1 + u))
                for s in range(KT):
                    exps(ITERS, s, 1)
                    if s == 0:
                        output(ITERS, 0)
                output(ITERS, 1, slice(VW * PH, P))

            @block.vector
            def _(dve):
                def read(number, place, use, passes, u, rows):
                    bank = 5 + place % 3
                    dve.wait_ge(s_tile, number + 1)
                    if use[0] == "turn":
                        pair = use[1]
                        dve.tensor_scalar(nm[:, :], PS[0:PH * KT, bank, 0:P], -1.0, None, ALU.mult).then_inc(s_max, 1)
                        dve.wait_ge(s_max, number + 1)
                        dve.wait_ge(s_mr[pair][u], rows)
                        ch = Chain(dve, s_ch, 3 * passes)
                        ch.link(dve.tensor_copy(mp[:, pair, u, 0, :], nm[:, :]))
                        ch.link(dve.tensor_tensor(nr[:, :], nm[:, :], mp[:, pair, u, 0, :], ALU.subtract))
                        ch.link(dve.tensor_copy(mp[:, pair, u, 1, :], nr[:, :]))
                        dve.tensor_tensor(mp[:, pair, u, 2, :], nr[:, :], mp[:, pair, u, 1, :],
                                          ALU.subtract).then_inc(s_mp, 1)
                    else:
                        pair, c = use
                        dve.tensor_reduce(mh[:, pair, c // HALVES, c % HALVES:c % HALVES + 1], PS[:, bank, :],
                                          AX.X, ALU.max).then_inc(s_max, 1)
                        if c == TILES - 1:
                            dve.wait_ge(s_max, number + 1)
                            dve.tensor_reduce(m[:, pair, :], mh[:, pair, :, :], AX.X, ALU.max).then_inc(s_mx, 1)

                for i, use in enumerate(PRO):
                    read(i, i, use, 0, 0, 0)
                with dve.Fori(0, ITERS // 2) as it:
                    for u in range(2):
                        n = 2 * it + u
                        for i, use in enumerate(RING):
                            second = use == ("turn", 1)
                            read(len(PRO) + len(RING) * n + i, len(PRO) + i, use, 2 * n + (1 if second else 2),
                                 u if second else 1 - u, 16 * PARTS * (it if second else it + u))


def broadcast_rows(ap, parts, n):
    return bass.AP(ap.tensor, ap.offset, [[0, parts], [1, n]])


def top2(dve, ch, p, w, lower, t1, t2, rank, n, e, part=None):
    def axes(ap, d):
        return bc(ap, [[e, n], d[0], d[1]])
    mine, other = axes(p, ([1, e], [0, e])), axes(p, ([0, e], [1, e]))
    if part != 1:
        ch.tick(dve.tensor_tensor(t1, other, mine, ALU.is_gt))
        ch.link(dve.tensor_tensor(t2, other, mine, ALU.is_equal))
        ch.link(dve.tensor_tensor(t2, t2, bc(lower, [[0, n], [e, e], [1, e]]), ALU.mult))
    if part != 0:
        ch.link(dve.tensor_tensor(t1, t1, t2, ALU.add))
        ch.link(dve.tensor_reduce(rank, t1, AX.X, ALU.add))
        ch.link(dve.scalar_tensor_tensor(w, rank, 1.5, p, ALU.is_lt, ALU.mult))


def ffn0(nc, a, g):
    with ExitStack() as ctx:
        sb, _ = stage(nc, ctx)
        LG = sb("f0_lg", [P, NT, GA + E0])
        weights = dict(
            wi=sb("f0_wi", [P, 2, 2 * HID]),
            ws=sb("f0_ws", [P, HID // P, D]),
            w2=sb("f0_w2", [P, HID // P, E0, D]),
            n2=sb("f0_n2", [P, D]),
            low=sb("f0_low", [P, E0 * E0]),
        )
        attention_output(nc, a, g, LG, weights)
        experts0(nc, g, LG, weights)


def attention_output(nc, a, g, LG, weights):
    XN, XNT, IDN, PS, PW, O = (g[k] for k in ("XN", "XNT", "IDN", "PS", "PW", "O"))
    G = GA + E0
    with ExitStack() as ctx:
        sb, sem = stage(nc, ctx)
        wo = sb("ao_wo", [P, D])
        wg = sb("ao_wg", [P, G])
        gb = sb("ao_gb", [P, G])
        n1 = sb("ao_n1", [P, D])
        ot = sb("ao_ot", [P, 2, NG, BT])
        rc = sb("ao_rc", [P, 2, TPB * H0])
        sa = sb("ao_sa", [P, 2, TPB, D])
        saT = sb("ao_saT", [P, 2, BT])
        y = sb("ao_y", [P, 2, TPB, D])
        sq = sb("ao_sq", [P, 2, TPB, D])
        ss = sb("ao_ss", [P, 2, TPB])
        ms = sb("ao_ms", [P, 2, TPB])
        r = sb("ao_r", [P, 2, TPB])
        x1 = sb("ao_x1", [P, 2, TPB, D])
        x1T = sb("ao_x1T", [P, 2, BT])
        s_ot = [sem(f"ao_o_loaded{u}") for u in range(2)]
        s_ew = sem("ao_experts_weights")
        s_w, s_o, s_rc, s_sa, s_saT, s_T, s_pr, s_y, s_ss, s_ms, s_r, s_x1, s_x1T, s_cp, s_xt, s_lt, s_lg = (
            sem("ao_" + n) for n in ("weights", "o_turned", "recip", "normalised", "sa_turned", "saT_ready",
                                     "projected", "y_ready", "squares", "mean", "rms", "x1_ready", "x1_turned",
                                     "x1T_copied", "xnt_copied", "logits", "logits_read"))
        with nc.Block() as block:
            @block.sync
            def _(sp):
                with sp.Fori(0, BATCH) as b:
                    for u in range(2):
                        sp.wait_ge(s_o, 2 * b)
                        sp.dma_start(ot[:, u, :, :], O[bass.ds(NG * b + 1, NG), :, u * BT:(u + 1) * BT].rearrange(
                            "g p s -> p g s")).then_inc(s_ot[u], 16)
                wi, ws, w2, n2, low = (weights[k] for k in ("wi", "ws", "w2", "n2", "low"))
                sp.dma_start(wi[:, 0, :], a["L0_ffn_W_shared_in"]).then_inc(s_ew, 16)
                sp.dma_start(wi[:, 1, :], a["L0_ffn_W1_shared"]).then_inc(s_ew, 16)
                sp.dma_start(ws[:, :, :], a["L0_ffn_W_shared_out"].rearrange("(f p) d -> p f d", p=P)).then_inc(s_ew, 16)
                for f in range(HID // P):
                    sp.dma_start(w2[:, f, :, :], a["L0_ffn_W2_experts"][:, f * P:(f + 1) * P, :].rearrange(
                        "e p d -> p e d")).then_inc(s_ew, 16)
                sp.dma_start(n2[:, :], broadcast_rows(a["L0_ffn_norm2_w"], P, D)).then_inc(s_ew, 16)
                sp.dma_start(low[:, :], broadcast_rows(a["c_lower0"], P, E0 * E0)).then_inc(s_ew, 16)
                sp.wait_ge(s_ew, 7 * 16)

            @block.tensor
            def _(pe):
                with pe.Fori(0, BATCH) as b:
                    blocks = [(u, 4 * u, 2 * b + u) for u in range(2)]
                    for u, bank, n in blocks:
                        pe.wait_ge(s_ot[u], 16 * (b + 1))
                        pe.wait_ge(s_lg, 2 * b)
                        for j in range(TPB):
                            for gi in range(NG):
                                mm = pe.transpose(PS[:, bank + j, gi * P:(gi + 1) * P], ot[:, u, gi, j * P:(j + 1) * P],
                                                  IDN[:, :])
                        mm.then_inc(s_o, 1)
                    for u, bank, n in blocks:
                        pe.wait_ge(s_sa, n + 1)
                        for j in range(TPB):
                            mm = pe.transpose(PS[:, bank, j * P:(j + 1) * P], sa[:, u, j, :], IDN[:, :])
                        mm.then_inc(s_saT, 1)
                    pe.wait_ge(s_w, 96)
                    for u, bank, n in blocks:
                        pe.wait_ge(s_T, n + 1)
                        for j in range(TPB):
                            mm = pe.matmul(PS[:, bank + 1, j * P:(j + 1) * P], saT[:, u, j * P:(j + 1) * P], wo[:, :],
                                           start=True, stop=True)
                        mm.then_inc(s_pr, 1)
                    for u, bank, n in blocks:
                        pe.wait_ge(s_x1, TPB * (n + 1))
                        for j in range(TPB):
                            mm = pe.transpose(PS[:, bank + 2, j * P:(j + 1) * P], x1[:, u, j, :], IDN[:, :])
                        mm.then_inc(s_x1T, 1)
                    for u, bank, n in blocks:
                        pe.wait_ge(s_cp, n + 1)
                        for j in range(TPB):
                            mm = pe.matmul(PS[:, bank + 3, j * G:(j + 1) * G], x1T[:, u, j * P:(j + 1) * P], wg[:, :],
                                           start=True, stop=True)
                        mm.then_inc(s_lt, 1)

            @block.vector
            def _(dve):
                with dve.Fori(0, BATCH) as b:
                    blocks = [(u, 4 * u, 2 * b + u) for u in range(2)]
                    for u, bank, n in blocks:
                        heads = PS[:, bank:bank + TPB, :].rearrange("p j (h c) -> p (j h) c", c=VW)
                        dve.wait_ge(s_o, n + 1)
                        dve.reciprocal(rc[:, u, :], heads[:, :, DH]).then_inc(s_rc, 1)
                        dve.wait_ge(s_rc, n + 1)
                        dve.tensor_tensor(sa[:, u, :, :].rearrange("p j (h d) -> p (j h) d", d=DH), heads[:, :, 0:DH],
                                          bc(rc[:, u, :], [[1, TPB * H0], [0, DH]]), ALU.mult).then_inc(s_sa, 1)
                    for u, bank, n in blocks:
                        dve.wait_ge(s_pr, n + 1)
                        dve.tensor_tensor(y[:, u, :, :], PS[:, bank + 1, :].rearrange("p (j c) -> p j c", j=TPB),
                                          XN[:, bass.ds(TPB * n, TPB), :], ALU.add).then_inc(s_y, 1)
                    for u, bank, n in blocks:
                        dve.wait_ge(s_ss, TPB * (n + 1))
                        dve.tensor_scalar(ms[:, u, :], ss[:, u, :], 1.0 / D, RMS_EPS, ALU.mult, ALU.add).then_inc(s_ms, 1)
                    dve.wait_ge(s_w, 96)
                    for u, bank, n in blocks:
                        dve.wait_ge(s_r, n + 1)
                        dve.wait_ge(s_xt, 2 * b)
                        for j in range(TPB):
                            dve.scalar_tensor_tensor(x1[:, u, j, :], y[:, u, j, :], r[:, u, j:j + 1], n1[:, :],
                                                     ALU.mult, ALU.mult).then_inc(s_x1, 1)
                    for u, bank, n in blocks:
                        dve.wait_ge(s_lt, n + 1)
                        dve.tensor_tensor(LG[:, bass.ds(TPB * n, TPB), :],
                                          PS[:, bank + 3, 0:TPB * G].rearrange("p (j c) -> p j c", j=TPB),
                                          bc(gb[:, :], [[0, TPB], [1, G]]), ALU.add).then_inc(s_lg, 1)

            @block.gpsimd
            def _(pool):
                with pool.Fori(0, BATCH) as b:
                    for u in range(2):
                        pool.wait_ge(s_ms, 2 * b + u + 1)
                        pool.tensor_tensor(r[:, u, :], ms[:, u, :], PW[:, :], ALU.pow).then_inc(s_r, 1)

            @block.scalar
            def _(act):
                act.dma_start(wo[:, :], a["L0_ffn_Wo"]).then_inc(s_w, 16)
                act.dma_start(wg[:, 0:GA], a["L0_ffn_Wg_gate"]).then_inc(s_w, 16)
                act.dma_start(wg[:, GA:G], a["L0_ffn_We_gate"]).then_inc(s_w, 16)
                act.dma_start(gb[:, 0:GA], broadcast_rows(a["L0_ffn_group_bias"], P, GA)).then_inc(s_w, 16)
                act.dma_start(gb[:, GA:G], broadcast_rows(a["L0_ffn_expert_bias"], P, E0)).then_inc(s_w, 16)
                act.dma_start(n1[:, :], broadcast_rows(a["L0_ffn_norm1_w"], P, D)).then_inc(s_w, 16)
                with act.Fori(0, BATCH) as b:
                    blocks = [(u, 4 * u, 2 * b + u) for u in range(2)]
                    for u, bank, n in blocks:
                        act.wait_ge(s_saT, n + 1)
                        act.activation(saT[:, u, :], PS[:, bank, :], ACT.Copy).then_inc(s_T, 1)
                    for u, bank, n in blocks:
                        act.wait_ge(s_y, n + 1)
                        for j in range(TPB):
                            act.activation(sq[:, u, j, :], y[:, u, j, :], ACT.Square,
                                           accum_out=ss[:, u, j:j + 1]).then_inc(s_ss, 1)
                    for u, bank, n in blocks:
                        act.wait_ge(s_x1T, n + 1)
                        act.activation(x1T[:, u, :], PS[:, bank + 2, :], ACT.Copy).then_inc(s_cp, 1)
                    for u, bank, n in blocks:
                        act.wait_ge(s_cp, n + 1)
                        act.activation(XNT[:, bass.ds(BT * n, BT)], x1T[:, u, :], ACT.Copy)
                        act.activation(XN[:, bass.ds(TPB * n, TPB), :], x1[:, u, :, :], ACT.Copy).then_inc(s_xt, 1)


def experts0(nc, g, LG, weights):
    X, XN, XNT, PS, PW = (g[k] for k in ("X", "XN", "XNT", "PS", "PW"))
    FT = HID // P
    EB = BT // D
    HB = E0 // EB
    UNITS = [(k, f) for k in range(2) for f in range(FT)]
    assert len(UNITS) == TPB
    with ExitStack() as ctx:
        sb, sem = stage(nc, ctx)
        wi, ws, w2, n2, low = (weights[k] for k in ("wi", "ws", "w2", "n2", "low"))
        W = sb("e0_w", [P, NT, E0])
        gm = sb("r0_gm", [P, NT])
        ge = sb("r0_ge", [P, NT, GA])
        gs = sb("r0_gs", [P, NT])
        gp = sb("r0_gp", [P, NT])
        em = sb("r0_em", [P, NT * GA])
        ee = sb("r0_ee", [P, NT * GA, EPG])
        es = sb("r0_es", [P, NT * GA])
        er = sb("r0_er", [P, NT, GA])
        mg = sb("r0_mg", [P, NT, GA])
        p = sb("r0_p", [P, NT, E0])
        t1 = sb("r0_t1", [P, NT, E0, E0])
        t2 = sb("r0_t2", [P, NT, E0, E0])
        rank = sb("r0_rank", [P, NT, E0])
        sg = sb("e0_sg", [P, 2, BT])
        hT = sb("e0_hT", [P, 2, len(UNITS), BT])
        acc = sb("e0_acc", [P, TPB, D])
        y = sb("e0_y", [P, TPB, D])
        sq = sb("e0_sq", [P, TPB, D])
        ss = sb("e0_ss", [P, TPB])
        ms = sb("e0_ms", [P, TPB])
        r = sb("e0_r", [P, TPB])
        z = sb("e0_z", [P, TPB, D])
        s_d, s_e, s_c, s_up, s_sg, s_h, s_dn, s_sh, s_ac, s_y, s_ss, s_ms, s_r, s_z, s_n2, s_x = (
            sem("e0_" + n) for n in ("differences", "exps", "chain", "up_done", "silu_done", "hidden", "down_done", "shared_done", "combined",
                                     "y_ready", "squares", "mean", "rms", "z_ready", "norm_halved", "x_added"))
        with nc.Block() as block:
            @block.tensor
            def _(pe):
                def up(n, i):
                    k, f = UNITS[i]
                    if i >= 2:
                        pe.wait_ge(s_h, len(UNITS) * n + i - 1)
                    for c in range(2):
                        mm = pe.matmul(PS[:, 4 + 2 * (i % 2) + c, :], wi[:, k, (FT * c + f) * P:(FT * c + f + 1) * P],
                                       XNT[:, bass.ds(BT * (n % NBLK), BT)], start=True, stop=True)
                    mm.then_inc(s_up, 1)

                for i in range(len(UNITS)):
                    up(0, i)
                with pe.Fori(0, BATCH) as b:
                    for u in range(2):
                        n = 2 * b + u
                        pe.wait_ge(s_h, len(UNITS) * (n + 1))
                        for j in range(TPB):
                            up(n + 1, j)
                            if j == 0:
                                pe.wait_ge(s_y, 2 * b)
                            for f in range(FT):
                                mm = pe.matmul(PS[:, 2 + u, j * P:(j + 1) * P], hT[:, u, f, j * P:(j + 1) * P],
                                               ws[:, f, :], start=(f == 0), stop=(f == FT - 1))
                            if j == TPB - 1:
                                mm.then_inc(s_sh, 1)
                            for h in range(HB):
                                pe.wait_ge(s_ac, E0 * (TPB * n + j - 1) + EB * (h + 1) if j else E0 * TPB * n)
                                for f in range(FT):
                                    mm = pe.matmul(PS[:, h, :], hT[:, u, FT + f, j * P:(j + 1) * P],
                                                   w2[:, f, h * EB:(h + 1) * EB, :], start=(f == 0), stop=(f == FT - 1))
                                mm.then_inc(s_dn, 1)

            @block.scalar
            def _(act):
                def silu(n, i):
                    act.wait_ge(s_up, len(UNITS) * n + i + 1)
                    if not isinstance(n, int) or i >= 2:
                        act.wait_ge(s_h, len(UNITS) * n + i - 1)
                    act.activation(sg[:, i % 2, :], PS[:, 4 + 2 * (i % 2), :], ACT.Silu).then_inc(s_sg, 1)

                for i in range(len(UNITS)):
                    silu(0, i)
                act.wait_ge(s_d, 2)
                act.activation(ge[:, :, :], ge[:, :, :], ACT.Exp).then_inc(s_e, 1)
                act.activation(ee[:, :, :], ee[:, :, :], ACT.Exp).then_inc(s_e, 1)
                with act.Fori(0, NBLK) as n:
                    for i in range(len(UNITS)):
                        silu(n + 1, i)
                    act.wait_ge(s_y, n + 1)
                    for j in range(TPB):
                        act.activation(sq[:, j, :], y[:, j, :], ACT.Square, accum_out=ss[:, j:j + 1]).then_inc(s_ss, 1)

            @block.gpsimd
            def _(pool):
                with pool.Fori(0, NBLK) as n:
                    pool.wait_ge(s_ms, n + 1)
                    pool.tensor_tensor(r[:, :], ms[:, :], PW[:, :], ALU.pow).then_inc(s_r, 1)
                    pool.wait_ge(s_z, TPB * (n + 1))
                    pool.tensor_tensor(X[:, bass.ds(TPB * n, TPB), :], X[:, bass.ds(TPB * n, TPB), :], z[:, :, :],
                                       ALU.add).then_inc(s_x, 1)

            @block.vector
            def _(dve):
                def hidden(n, i, u):
                    dve.wait_ge(s_sg, len(UNITS) * n + i + 1)
                    dve.tensor_tensor(hT[:, u, i, :], sg[:, i % 2, :], PS[:, 5 + 2 * (i % 2), :], ALU.mult).then_inc(s_h, 1)

                dve.tensor_scalar(n2[:, :], n2[:, :], 0.5, None, ALU.mult).then_inc(s_n2, 1)
                dve.wait_ge(s_n2, 1)
                ch = Chain(dve, s_c)
                gl = LG[:, :, 0:GA]
                el = bc(LG[:, :, GA:GA + E0], [[GA + E0, NT], [EPG, GA], [1, EPG]])
                ch.tick(dve.tensor_reduce(gm[:, :], gl, AX.X, ALU.max))
                ch.link(dve.tensor_reduce(em[:, :].rearrange("p (n g) -> p n g", g=GA), el, AX.X, ALU.max))
                dve.tensor_tensor(ge[:, :, :], gl, bc(gm[:, :], [[1, NT], [0, GA]]), ALU.subtract).then_inc(s_d, 1)
                dve.tensor_tensor(ee[:, :, :].rearrange("p (n g) e -> p n g e", g=GA), el,
                                  bc(em[:, :], [[GA, NT], [1, GA], [0, EPG]]), ALU.subtract).then_inc(s_d, 1)
                for i in range(len(UNITS)):
                    hidden(0, i, 0)
                dve.wait_ge(s_e, 2)
                ch.tick(dve.tensor_reduce(gs[:, :], ge[:, :, :], AX.X, ALU.add))
                ch.tick(dve.tensor_reduce(es[:, :], ee[:, :, :], AX.X, ALU.add))
                ch.link(dve.tensor_tensor(mg[:, :, 1], ge[:, :, 1], ge[:, :, 0], ALU.is_gt))
                ch.tick(dve.tensor_scalar(mg[:, :, 0], mg[:, :, 1], -1.0, 1.0, ALU.mult, ALU.add))
                ch.tick(dve.reciprocal(gp[:, :], gs[:, :]))
                ch.link(dve.reciprocal(er[:, :, :].rearrange("p n g -> p (n g)"), es[:, :]))
                ch.link(dve.tensor_tensor(er[:, :, :], er[:, :, :], mg[:, :, :], ALU.mult))
                ch.link(dve.tensor_tensor(p[:, :, :].rearrange("p n (g e) -> p (n g) e", g=GA), ee[:, :, :],
                                          bc(er[:, :, :], [[1, NT * GA], [0, EPG]]), ALU.mult))
                ch.link(dve.tensor_tensor(p[:, :, :], p[:, :, :], bc(gp[:, :], [[1, NT], [0, E0]]), ALU.mult))
                top2(dve, ch, p[:, :, :], W[:, :, :], low[:, :], t1[:, :, :, :], t2[:, :, :, :], rank[:, :, :], NT, E0)
                ch.wait()
                with dve.Fori(0, BATCH) as b:
                    for u in range(2):
                        n = 2 * b + u
                        for j in range(TPB):
                            if j == 0:
                                dve.wait_ge(s_dn, TPB * HB * n)
                            hidden(n + 1, j, 1 - u)
                            for x in range(E0):
                                if x % EB == 0:
                                    dve.wait_ge(s_dn, HB * (TPB * n + j) + x // EB + 1)
                                if x:
                                    dve.wait_ge(s_ac, E0 * (TPB * n + j) + x)
                                dve.scalar_tensor_tensor(
                                    acc[:, j, :], PS[:, x // EB, x % EB * D:(x % EB + 1) * D], W[:, TPB * n + j, x:x + 1],
                                    acc[:, j, :] if x else XN[:, TPB * n + j, :], ALU.mult, ALU.add).then_inc(s_ac, 1)
                        dve.wait_ge(s_ac, E0 * TPB * (n + 1))
                        dve.wait_ge(s_sh, n + 1)
                        dve.tensor_tensor(y[:, :, :], PS[:, 2 + u, :].rearrange("p (j c) -> p j c", j=TPB), acc[:, :, :],
                                          ALU.add).then_inc(s_y, 1)
                        dve.wait_ge(s_ss, TPB * (n + 1))
                        dve.tensor_scalar(ms[:, :], ss[:, :], 1.0 / D, RMS_EPS, ALU.mult, ALU.add).then_inc(s_ms, 1)
                        dve.wait_ge(s_r, n + 1)
                        dve.wait_ge(s_x, n)
                        for j in range(TPB):
                            dve.scalar_tensor_tensor(z[:, j, :], y[:, j, :], r[:, j:j + 1], n2[:, :],
                                                     ALU.mult, ALU.mult).then_inc(s_z, 1)


def linear_attention(nc, a, g):
    X, XNT, IDN, PS = (g[k] for k in ("X", "XNT", "IDN", "PS"))
    C = H1 * HD
    CB = C // BT
    PB = BT // P
    SB = 3
    RB = 3
    CHUNKS = 4
    DENOM = NP + 2
    LATE = 3
    TURN, MULTIPLY = 3, 5
    with ExitStack() as ctx:
        sb, sem = stage(nc, ctx)
        ln = LayerNorm(g, sb, sem)
        wq, wk, wv = (sb("la_w" + c, [P, C]) for c in "qkv")
        wo = sb("la_wo", [P, NP, D])
        bq = sb("la_bq", [P, NP])
        bo = sb("la_bo", [P, 1])
        bkv = sb("la_bkv", [P, 2, C])
        sel = sb("la_sel", [P, NP, P])
        rows = sb("la_rows", [P, NP, VW])
        blocks = sb("la_blocks", [P, P])
        xs = sb("la_xs", [P, SEQ])
        tk = sb("la_tk", [P, 2, C])
        ek = sb("la_ek", [P, 2, C])
        km = sb("la_km", [P, RB, C])
        vt = sb("la_vt", [P, RB, NP, P + 1])
        kvm = sb("la_kvm", [P, NP, P])
        kvs = sb("la_kvs", [P, NP, P])
        ksm = sb("la_ksm", [P, NP, VW])
        G = sb("la_g", [P, NP, D])
        eq = sb("la_eq", [P, RB, BT])
        rq = sb("la_rq", [P, RB, BT])
        qm = sb("la_qm", [P, HALVES, NP, BT])
        de = sb("la_de", [P, BT])
        z = sb("la_z", [P, HALVES, BT])
        oT = sb("la_oT", [P, BT])
        (s_w, s_one, s_x, s_pj, s_rd, s_ex, s_re, s_km, s_kv, s_ks, s_kst, s_kvt, s_gm, s_g, s_q, s_eq, s_qm, s_dn,
         s_de, s_z, s_zb, s_zq, s_o, s_oT, s_t, s_add) = (sem("la_" + n) for n in (
             "weights", "ones", "x_ready", "projected", "psum_read", "exp_k", "relu_k", "k_ready", "kv_done", "kv_masked",
             "kv_turned", "kvt_ready", "g_done", "g_copied", "q_done", "exp_relu_q", "q_ready", "denominators",
             "eps_added", "z_ready", "z_spread", "q_scaled", "output", "output_copied", "output_turned", "added"))

        def order(project, between, c_late, late):
            for k in range(HALVES * NP):
                project(k)
                between(k + 1)
            for c in range(HALVES):
                for p in range(NP):
                    if p == LATE:
                        c_late(c)
                    late(c, p)

        def sums(p):
            return PS[:, 4 + p // SB, p % SB * (P + 1):(p % SB + 1) * (P + 1)]

        with nc.Block() as block:
            @block.sync
            def _(sp):
                for w, name in ((wk, "wk"), (wv, "wv"), (wq, "wq")):
                    sp.dma_start(w[:, :], a["L0_attn_" + name].rearrange("f h d -> f (h d)")).then_inc(s_w, 16)
                sp.dma_start(wo[:, :, :], a["L0_attn_wo"].rearrange("(p h) m f -> (h m) p f", h=2)).then_inc(s_w, 16)
                sp.dma_start(bq[:, :], a["L0_attn_bq"].rearrange("(p h) d -> (h d) p", h=2),
                             allow_slow_non_contiguous=True).then_inc(s_w, 16)
                sp.dma_start(bo[:, :], a["L0_attn_bo"].rearrange("(f o) -> f o", o=1),
                             allow_slow_non_contiguous=True).then_inc(s_w, 16)
                sp.dma_start(bkv[:, 0, :], broadcast_rows(a["L0_attn_bk"], P, C)).then_inc(s_w, 16)
                sp.dma_start(bkv[:, 1, :], broadcast_rows(a["L0_attn_bv"], P, C)).then_inc(s_w, 16)
                sp.dma_start(sel[:, :, :], a["c_spread"]).then_inc(s_w, 16)
                sp.dma_start(rows[:, :, :], a["c_rows"]).then_inc(s_w, 16)
                sp.dma_start(blocks[:, :], a["c_blocks"]).then_inc(s_w, 16)
                sp.wait_ge(s_w, 11 * 16)

            @block.tensor
            def _(pe):
                ln.tensor(pe)
                pe.wait_ge(s_w, 11 * 16)
                pe.wait_ge(s_one, 1)
                with pe.Fori(0, BATCH) as b:
                    pe.wait_ge(s_x, b + 1)

                    def project_kv(t):
                        for k, w in enumerate((wk, wv)):
                            pe.wait_ge(s_rd, 2 * (KT * b + t) - (1 - k if t else 0))
                            for c in range(CB):
                                mm = pe.matmul(PS[:, CB * k + c, :], xs[:, t * P:(t + 1) * P], w[:, c * BT:(c + 1) * BT],
                                               start=True, stop=True)
                            mm.then_inc(s_pj, 1)

                    def gather(t):
                        pe.wait_ge(s_km, KT * b + t + 1)
                        for p in range(NP):
                            mm = pe.matmul(sums(p), km[:, t % RB, p * P:(p + 1) * P], vt[:, t % RB, p, :],
                                           start=(t == 0 and p % SB == 0), stop=(t == KT - 1), skip_group_check=True)
                        mm.then_inc(s_kv, 1)

                    project_kv(0)
                    project_kv(1)
                    pe.wait_ge(s_add, HALVES * b)
                    for t in range(KT):
                        if t + 2 < KT:
                            project_kv(t + 2)
                        gather(t)

                    def project(k):
                        c, p = divmod(k, NP)
                        if k == 0:
                            pe.wait_ge(s_rd, 2 * KT * (b + 1))
                        if k >= RB:
                            pe.wait_ge(s_qm, HALVES * NP * b + k - RB + 1)
                        pe.matmul(PS[:, k % RB, :], wq[:, p * P:(p + 1) * P], XNT[:, bass.ds(SEQ * b + c * BT, BT)],
                                  start=True, stop=True).then_inc(s_q, 1)

                    def denominators(c):
                        n = HALVES * b + c
                        pe.wait_ge(s_qm, NP * (n + 1))
                        pe.wait_ge(s_de, n)
                        for p in range(NP):
                            r = 32 * (p % PB)
                            mm = pe.matmul(PS[r:r + VW, 4, :], ksm[:, p, :], qm[:, c, p, :], start=(p < PB), stop=(p >= PB))
                        mm.then_inc(s_dn, 1)

                    def between(k):
                        if k == TURN:
                            pe.wait_ge(s_ks, b + 1)
                            for p in range(NP):
                                mm = pe.transpose(PS[:, 3 + 4 * (p // PB), p % PB * P:(p % PB + 1) * P], kvm[:, p, :], IDN[:, :])
                            mm.then_inc(s_kst, 1)
                        if k == MULTIPLY:
                            pe.wait_ge(s_kvt, b + 1)
                            for p in range(NP):
                                mm = pe.matmul(PS[:, 4 + p // PB, p % PB * P:(p % PB + 1) * P], kvs[:, p, :], wo[:, p, :],
                                               start=True, stop=True)
                            mm.then_inc(s_gm, 1)
                        if k == DENOM:
                            pe.wait_ge(s_g, b + 1)
                            denominators(0)

                    def turn(c):
                        n = HALVES * b + c
                        pe.wait_ge(s_oT, n + 1)
                        pe.wait_ge(s_de, HALVES * (b + 1))
                        pe.wait_ge(s_add, n)
                        for j in range(TPB):
                            mm = pe.transpose(PS[:, 4, j * P:(j + 1) * P], oT[:, j * P:(j + 1) * P], IDN[:, :])
                        mm.then_inc(s_t, 1)

                    def product(c, p):
                        n = HALVES * b + c
                        if p == 0:
                            pe.wait_ge(s_z, CHUNKS * (n + 1))
                        if p >= 2:
                            pe.wait_ge(s_zq, NP * n + p - 1)
                        pe.matmul(PS[:, 5 + p % 2, :], sel[:, p, :], z[:, c, :], start=True, stop=True).then_inc(s_zb, 1)
                        if p:
                            output(c, p - 1)
                        if p == NP - 1:
                            output(c, p).then_inc(s_o, 1)

                    def output(c, p):
                        n = HALVES * b + c
                        pe.wait_ge(s_zq, NP * n + p + 1)
                        if p == 0:
                            pe.wait_ge(s_oT, n)
                        return pe.matmul(PS[:, 7, :], G[:, p, :], qm[:, c, p, :], start=(p == 0), stop=(p == NP - 1))

                    order(project, between, lambda c: denominators(1) if c == 0 else turn(0), product)
                    turn(1)

            @block.scalar
            def _(act):
                ln.scalar(act)
                act.activation(xs[:, :], XNT[:, 0:SEQ], ACT.Copy).then_inc(s_x, 1)
                act.wait_ge(s_w, 11 * 16)
                with act.Fori(0, BATCH) as b:
                    for t in range(KT):
                        i = KT * b + t
                        act.wait_ge(s_rd, 2 * i + 1)
                        act.activation(ek[:, t % 2, :], tk[:, t % 2, :], ACT.Exp).then_inc(s_ex, 1)
                        act.wait_ge(s_ex, i + 1)
                        act.wait_ge(s_kv, i - RB + 1 if t >= RB else KT * b)
                        act.activation(km[:, t % RB, :], tk[:, t % 2, :], ACT.Relu).then_inc(s_re, 1)

                    def project(k):
                        c, p = divmod(k, NP)
                        act.wait_ge(s_q, HALVES * NP * b + k + 1)
                        if k >= RB:
                            act.wait_ge(s_qm, HALVES * NP * b + k - RB + 1)
                        act.activation(eq[:, k % RB, :], PS[:, k % RB, :], ACT.Exp, bias=bq[:, p:p + 1]).then_inc(s_eq, 1)
                        act.activation(rq[:, k % RB, :], PS[:, k % RB, :], ACT.Relu, bias=bq[:, p:p + 1]).then_inc(s_eq, 1)

                    def between(k):
                        if k == TURN:
                            act.wait_ge(s_kst, b + 1)
                            act.activation(kvs[:, 0:PB, :], PS[:, 3, :].rearrange("p (q f) -> p q f", f=D), ACT.Copy)
                            act.activation(kvs[:, PB:NP, :], PS[:, 7, :].rearrange("p (q f) -> p q f", f=D),
                                           ACT.Copy).then_inc(s_kvt, 1)
                        if k == MULTIPLY:
                            act.wait_ge(s_gm, b + 1)
                            act.activation(G[:, :, :], PS[:, 4:6, :].rearrange("p k (q f) -> p (k q) f", f=D),
                                           ACT.Copy).then_inc(s_g, 1)

                    def output(c):
                        n = HALVES * b + c
                        act.wait_ge(s_o, n + 1)
                        act.wait_ge(s_t, n)
                        act.activation(oT[:, :], PS[:, 7, :], ACT.Identity, bias=bo[:, 0:1]).then_inc(s_oT, 1)

                    order(project, between, lambda c: output(0) if c else None, lambda c, p: None)
                    act.activation(xs[:, :], XNT[:, bass.ds(SEQ * ((b + 1) % BATCH), SEQ)], ACT.Copy).then_inc(s_x, 1)
                    output(1)

            @block.gpsimd
            def _(pool):
                ln.gpsimd(pool)

            @block.vector
            def _(dve):
                ln.vector(dve)
                dve.memset(vt[:, :, :, P:P + 1], 1.0).then_inc(s_one, 1)
                dve.wait_ge(s_w, 11 * 16)
                with dve.Fori(0, BATCH) as b:
                    for t in range(KT + 1):
                        i = KT * b + t
                        if t < KT:
                            dve.wait_ge(s_pj, 2 * i + 1)
                            dve.tensor_tensor(tk[:, t % 2, :].rearrange("p (k c) -> p k c", k=CB), PS[:, 0:CB, :],
                                              bkv[:, 0, :].rearrange("p (k c) -> p k c", k=CB), ALU.add).then_inc(s_rd, 1)
                            dve.wait_ge(s_pj, 2 * i + 2)
                            dve.wait_ge(s_kv, i - RB + 1 if t >= RB else KT * b)
                            dve.tensor_tensor(vt[:, t % RB, :, 0:P],
                                              PS[:, CB:2 * CB, :].rearrange("p k (q c) -> p (k q) c", c=P),
                                              bkv[:, 1, :].rearrange("p (q c) -> p q c", c=P), ALU.add).then_inc(s_rd, 1)
                        if t:
                            dve.wait_ge(s_rd, 2 * i)
                            dve.wait_ge(s_re, i)
                            dve.scalar_tensor_tensor(km[:, (t - 1) % RB, :], ek[:, (t - 1) % 2, :], 1.0,
                                                     km[:, (t - 1) % RB, :], ALU.min, ALU.add).then_inc(s_km, 1)
                    dve.wait_ge(s_kv, KT * (b + 1))
                    for p0 in range(0, NP, SB):
                        q = min(SB, NP - p0)
                        kv = PS[:, 4 + p0 // SB, 0:q * (P + 1)].rearrange("p (q c) -> p q c", q=q)
                        dve.tensor_tensor(kvm[:, p0:p0 + q, :], kv[:, :, 0:P], bc(blocks[:, :], [[0, q], [1, P]]), ALU.mult)
                        ins = dve.tensor_tensor(ksm[:, p0:p0 + q, :], rows[:, p0:p0 + q, :],
                                                bc(kv[:, :, P], [[P + 1, q], [0, VW]]), ALU.mult)
                    ins.then_inc(s_ks, 1)

                    def project(k):
                        c, p = divmod(k, NP)
                        dve.wait_ge(s_eq, 2 * (HALVES * NP * b + k + 1))
                        dve.scalar_tensor_tensor(qm[:, c, p, :], eq[:, k % RB, :], 1.0, rq[:, k % RB, :],
                                                 ALU.min, ALU.add).then_inc(s_qm, 1)

                    def denominators(c):
                        n = HALVES * b + c
                        dve.wait_ge(s_dn, n + 1)
                        dve.tensor_scalar(de[:, :], PS[:, 4, :], LIN_EPS, None, ALU.add).then_inc(s_de, 1)

                    def invert(c, chunk):
                        cols = slice(chunk * BT // CHUNKS, (chunk + 1) * BT // CHUNKS)
                        dve.wait_ge(s_de, HALVES * b + c + 1)
                        dve.reciprocal(z[:, c, cols], de[:, cols]).then_inc(s_z, 1)

                    def between(k):
                        if k == DENOM:
                            denominators(0)
                        if DENOM < k <= DENOM + CHUNKS:
                            invert(0, k - DENOM - 1)

                    def add(c):
                        n = HALVES * b + c
                        dve.wait_ge(s_t, n + 1)
                        dve.tensor_tensor(X[:, bass.ds(TPB * n, TPB), :], X[:, bass.ds(TPB * n, TPB), :],
                                          PS[:, 4, :].rearrange("p (j c) -> p j c", j=TPB), ALU.add).then_inc(s_add, 1)

                    def scale(c, p):
                        n = HALVES * b + c
                        dve.wait_ge(s_zb, NP * n + p + 1)
                        dve.tensor_tensor(qm[:, c, p, :], qm[:, c, p, :], PS[:, 5 + p % 2, :], ALU.mult).then_inc(s_zq, 1)
                        if c == 0 and p >= LATE and p < LATE + CHUNKS:
                            invert(1, p - LATE)

                    order(project, between, lambda c: denominators(1) if c == 0 else add(0), scale)
                    add(1)


def ffn1(nc, a, g):
    X, XN, XNT, IDN, PS = (g[k] for k in ("X", "XN", "XNT", "IDN", "PS"))
    FT = F1 // P
    COPY, LOGITS, MAXIMA, EXP, SOFTMAX, RANK, PICK, WEIGH = range(8)
    LINKS = 14
    HEAD = 2
    with ExitStack() as ctx:
        sb, sem = stage(nc, ctx)
        ln = LayerNorm(g, sb, sem)
        w1 = sb("f1_w1", [P, E1, F1])
        w2 = sb("f1_w2", [P, E1, FT, D])
        b1 = sb("f1_b1", [P, E1, FT])
        b2 = sb("f1_b2", [P, E1, D])
        hh = sb("f1_hh", [P, 2, FT, BT])
        acc = sb("f1_acc", [P, TPB, D])
        gw = sb("f1_gw", [E1, P])
        gT = sb("f1_gT", [P, E1])
        xs = sb("f1_xs", [P, BT])
        low = sb("f1_low", [P, E1 * E1])
        gm = sb("f1_gm", [P, TPB])
        gs = sb("f1_gs", [P, TPB])
        gr = sb("f1_gr", [P, TPB])
        p = sb("f1_p", [P, TPB, E1])
        t1 = sb("f1_t1", [P, TPB, E1, E1])
        t2 = sb("f1_t2", [P, TPB, E1, E1])
        rank = sb("f1_rank", [P, TPB, E1])
        W = sb("f1_w", [P, 2, TPB, E1])
        s_g, s_h0, s_w, s_t, s_gt, s_x, s_l, s_d, s_e, s_c, s_up, s_h, s_dn, s_ac, s_cl, s_ad = (
            sem("f1_" + n) for n in ("gates_loaded", "first_weights", "weights", "gates_turned", "gates", "x_ready",
                                     "logits", "differences", "exps", "chain", "up_done", "hidden", "down_done",
                                     "combined", "clipped", "x_added"))
        adds = 2 * E1 * TPB
        logits = PS[:, 6, 0:TPB * E1].rearrange("p (j c) -> p j c", j=TPB)
        with nc.Block() as block:
            @block.sync
            def _(sp):
                sp.dma_start(gw[:, :], a["L1_ffn_gate_w"]).then_inc(s_g, 16)
                sp.dma_start(low[:, :], broadcast_rows(a["c_lower1"], P, E1 * E1)).then_inc(s_g, 16)
                sp.dma_start(b1[:, :, :], a["L1_ffn_b1"].rearrange("e (f p) -> p e f", p=P),
                             allow_slow_non_contiguous=True).then_inc(s_h0, 16)
                sp.dma_start(b2[:, :, :], broadcast_rows(a["L1_ffn_b2"], P, E1 * D).rearrange(
                    "p (e d) -> p e d", d=D)).then_inc(s_h0, 16)
                for es, s in ((slice(0, HEAD), s_h0), (slice(HEAD, E1), s_w)):
                    sp.dma_start(w1[:, es, :], a["L1_ffn_w1"][es].rearrange("e d f -> d e f")).then_inc(s, 16)
                    for f in range(FT):
                        sp.dma_start(w2[:, es, f, :], a["L1_ffn_w2"][es, f * P:(f + 1) * P, :].rearrange(
                            "e p d -> p e d")).then_inc(s, 16)
                sp.wait_ge(s_g, 32)
                sp.wait_ge(s_h0, 80)
                sp.wait_ge(s_w, 48)

            @block.tensor
            def _(pe):
                ln.tensor(pe)

                def route(n1):
                    pe.wait_ge(s_x, n1 + 1)
                    pe.wait_ge(s_d, n1)
                    for j in range(TPB):
                        mm = pe.matmul(PS[:, 6, j * E1:(j + 1) * E1], xs[:, j * P:(j + 1) * P], gT[:, :],
                                       start=True, stop=True)
                    mm.then_inc(s_l, 1)

                pe.wait_ge(s_g, 32)
                pe.transpose(PS[:, 7, 0:E1], gw[:, :], IDN[0:E1, 0:E1]).then_inc(s_t, 1)
                pe.wait_ge(s_gt, 1)
                route(0)
                pe.wait_ge(s_h0, 80)
                pe.wait_ge(s_w, 48)
                with pe.Fori(0, NBLK // 2) as it:
                    for u in range(2):
                        n = 2 * it + u

                        def up(e):
                            i = E1 * n + e
                            pe.wait_ge(s_h, FT * (i - 1) if e >= 2 else FT * E1 * n)
                            for f in range(FT):
                                pe.matmul(PS[:, FT * (e % 2) + f, :], w1[:, e, f * P:(f + 1) * P],
                                          XNT[:, bass.ds(BT * n, BT)], start=True, stop=True).then_inc(s_up, 1)

                        def down(e):
                            i = E1 * n + e
                            pe.wait_ge(s_h, FT * (i + 1))
                            pe.wait_ge(s_ac, adds * n + 2 * TPB * max(e - 1, 0))
                            for j in range(TPB):
                                for f in range(FT):
                                    mm = pe.matmul(PS[:, 4 + e % 2, j * P:(j + 1) * P], hh[:, e % 2, f, j * P:(j + 1) * P],
                                                   w2[:, e, f, :], start=(f == 0), stop=(f == FT - 1))
                            mm.then_inc(s_dn, 1)

                        up(0)
                        for e in range(E1):
                            if e + 1 < E1:
                                up(e + 1)
                            down(e)
                            if e == LOGITS:
                                route(n + 1)

            @block.scalar
            def _(act):
                ln.scalar(act)
                act.activation(xs[:, :], XNT[:, 0:BT], ACT.Copy).then_inc(s_x, 1)
                act.wait_ge(s_t, 1)
                act.activation(gT[:, :], PS[:, 7, 0:E1], ACT.Copy).then_inc(s_gt, 1)

                def exps(n1):
                    act.wait_ge(s_d, n1 + 1)
                    act.activation(p[:, :, :], p[:, :, :], ACT.Exp).then_inc(s_e, 1)

                exps(0)
                act.wait_ge(s_h0, 80)
                with act.Fori(0, NBLK // 2) as it:
                    for u in range(2):
                        n = 2 * it + u
                        for e in range(E1):
                            i = E1 * n + e
                            act.wait_ge(s_dn, i - 1 if e >= 2 else E1 * n)
                            for f in range(FT):
                                act.wait_ge(s_up, FT * i + f + 1)
                                act.activation(hh[:, e % 2, f, :], PS[:, FT * (e % 2) + f, :], ACT.Gelu,
                                               bias=b1[:, e, f:f + 1]).then_inc(s_h, 1)
                            if e == COPY:
                                act.wait_ge(s_l, n + 1)
                                act.activation(xs[:, :], XNT[:, bass.ds(BT * ((n + 1) % NBLK), BT)],
                                               ACT.Copy).then_inc(s_x, 1)
                            if e == EXP:
                                exps(n + 1)

            @block.gpsimd
            def _(pool):
                ln.gpsimd(pool)

            @block.vector
            def _(dve):
                ln.vector(dve)
                per = [[1, TPB], [0, E1]]

                def route(n1, u, part):
                    if part == MAXIMA:
                        ch = Chain(dve, s_c, LINKS * n1)
                        dve.wait_ge(s_l, n1 + 1)
                        ch.link(dve.tensor_reduce(gm[:, :], logits, AX.X, ALU.max))
                        dve.tensor_tensor(p[:, :, :], logits, bc(gm[:, :], per), ALU.subtract).then_inc(s_d, 1)
                    elif part == SOFTMAX:
                        ch = Chain(dve, s_c, LINKS * n1 + 1)
                        dve.wait_ge(s_e, n1 + 1)
                        ch.link(dve.tensor_reduce(gs[:, :], p[:, :, :], AX.X, ALU.add))
                        ch.link(dve.reciprocal(gr[:, :], gs[:, :]))
                        ch.link(dve.tensor_tensor(p[:, :, :], p[:, :, :], bc(gr[:, :], per), ALU.mult))
                    elif part in (RANK, PICK):
                        ch = Chain(dve, s_c, LINKS * n1 + (4 if part == RANK else 7))
                        top2(dve, ch, p[:, :, :], W[:, u, :, :], low[:, :], t1[:, :, :, :], t2[:, :, :, :],
                             rank[:, :, :], TPB, E1, 0 if part == RANK else 1)
                    elif part == WEIGH:
                        ch = Chain(dve, s_c, LINKS * n1 + 10)
                        ch.link(dve.tensor_reduce(gs[:, :], W[:, u, :, :], AX.X, ALU.add))
                        ch.link(dve.tensor_scalar(gm[:, :], gs[:, :], 1e-10, None, ALU.max))
                        ch.link(dve.reciprocal(gr[:, :], gm[:, :]))
                        ch.link(dve.tensor_tensor(W[:, u, :, :], W[:, u, :, :], bc(gr[:, :], per), ALU.mult))

                dve.wait_ge(s_g, 32)
                for part in range(E1):
                    route(0, 0, part)
                dve.wait_ge(s_h0, 80)
                dve.wait_ge(ln.copied, ln.COPIES)
                with dve.Fori(0, NBLK // 2) as it:
                    for u in range(2):
                        n = 2 * it + u
                        for e in range(E1):
                            for k in range(2):
                                if k:
                                    dve.wait_ge(s_dn, E1 * n + e + 1)
                                for j in range(TPB):
                                    if e or k:
                                        dve.wait_ge(s_ac, adds * n + TPB * (2 * e + k - 1) + j + 1)
                                    dve.scalar_tensor_tensor(
                                        acc[:, j, :], PS[:, 4 + e % 2, j * P:(j + 1) * P] if k else b2[:, e, :],
                                        W[:, u, j, e:e + 1], acc[:, j, :] if e or k else XN[:, TPB * n + j, :],
                                        ALU.mult, ALU.add).then_inc(s_ac, 1)
                            route(n + 1, 1 - u, e)
                        dve.wait_ge(s_ac, adds * (n + 1))
                        dve.tensor_scalar(acc[:, :, :], acc[:, :, :], 100.0, -100.0, ALU.min, ALU.max).then_inc(s_cl, 1)
                        dve.wait_ge(s_cl, n + 1)
                        xb = X[:, bass.ds(TPB * n, TPB), :]
                        dve.scalar_tensor_tensor(xb, acc[:, :, :], 0.5, xb, ALU.mult, ALU.add).then_inc(s_ad, 1)
                        dve.wait_ge(s_ad, n + 1)


def causal(nc, a, g):
    with ExitStack() as ctx:
        sb, _ = stage(nc, ctx)
        YT = sb("ca_yt", [P, BATCH + 1, SEQ])
        causal_attention(nc, a, g, YT)
        causal_output(nc, a, g, YT)


def causal_attention(nc, a, g, YT):
    XNT, IDN, PS = (g[k] for k in ("XNT", "IDN", "PS"))
    ITERS = BATCH * NP
    STEPS = [(qc, kt) for qc in range(HALVES) for kt in range(TPB * (qc + 1))]
    NS = len(STEPS)
    TILES = [(h, t, c) for h in range(2) for t in range(KT) for c in range(t // TPB + 1)]
    VTILES = [range(0, 3), range(3, 6), range(6, KT)]
    PREP = ([("q", 0), ("q", 1), ("k", 0), ("k", 1)] + [("v", i) for i in range(len(VTILES))]
            + [("t", i) for i in range(len(TILES))] + [("m", 0)])
    OUT = {2: ("z", 1), 5: ("y", 1), TPB + 2: ("z", 0), TPB + 6: ("y", 0)}
    CHUNKS = 8
    ADDS = [sum(kt > 0 for _, kt in STEPS[:s]) for s in range(NS + 1)]
    LEAD = 3
    RING, at = [], 0
    for s in range(NS):
        upto = min((len(PREP) - 1) * (s + 1) // (NS - LEAD), len(PREP) - 1)
        RING.append(([OUT[s]] if s in OUT else []) + (PREP[-1:] if s == NS - LEAD else []) + PREP[at:upto])
        at = upto
    USES = sum(map(len, RING))
    PRO = len(PREP)
    PLACE = {use: i for i, use in enumerate(x for uses in RING for x in uses)}
    AT = {i: use for use, i in PLACE.items()}
    QKS = PREP[:4]
    assert USES % 3 == 0
    assert all(PLACE["y", i] - PLACE["z", i] > CHUNKS + 1 for i in range(2))
    with ExitStack() as ctx:
        sb, sem = stage(nc, ctx)
        ln = LayerNorm(g, sb, sem)
        w = sb("ca_w", [P, 2, 3, P])
        bqk = sb("ca_bqk", [P, 2, 2])
        bv = sb("ca_bv", [P, 2, P])
        wo = sb("ca_wo", [P, 2, D])
        tri = sb("ca_tri", [P, 3, P])
        trb = sb("ca_trb", [P, 3, P], BF16)
        ones = sb("ca_ones", [P, HD])
        xs = sb("ca_xs", [P, 2, SEQ])
        Q = sb("ca_q", [P, 2, 2, SEQ])
        K = sb("ca_k", [P, 2, 2, SEQ])
        qb = sb("ca_qb", [P, 2, SEQ], BF16)
        kb = sb("ca_kb", [P, SEQ], BF16)
        VA = sb("ca_v", [P, 2, KT, P])
        PR = sb("ca_p", [P, 3, 2, BT])
        S = sb("ca_s", [P, 2, 2, BT])
        ot = sb("ca_ot", [P, BT])
        su = sb("ca_su", [P, BT])
        z = sb("ca_z", [P, BT])
        on = sb("ca_on", [P, BT])
        mh = sb("ca_mh", [P, 2 * KT, HALVES])
        m = sb("ca_m", [P, 2 * KT])
        nm = sb("ca_nm", [2 * KT, P])
        s_wl = [sem(f"ca_w_loaded{u}") for u in range(2)]
        s_mr = [sem(f"ca_max_rows{u}") for u in range(2)]
        s_wo = [sem(f"ca_wo_loaded{u}") for u in range(2)]
        (s_c, s_set, s_zero, s_x, s_ring, s_rd, s_mx, s_st, s_exp, s_pv, s_ot,
         s_full, s_first, s_sum, s_z, s_on) = (
            sem("ca_" + n) for n in (
                "constants", "set", "zeroed", "x_ready", "ring_filled", "ring_read", "m_ready", "scores_ready",
                "exp_done", "pv_done", "o_copied",
                "qk_copied", "first_exps", "exps_added", "z_ready", "o_divided"))
        SETS, ZEROS = 5, 8

        def number(n, use):
            return PRO + USES * n + PLACE[use]

        def behind(n, qc):
            return HALVES * n if qc else HALVES * n + 1

        def added(n, qc):
            return ADDS[NS] * n + (0 if qc else ADDS[TPB]) + 2

        lower, upper = slice(0, HD), slice(HD, P)

        with nc.Block() as block:
            @block.sync
            def _(sp):
                sp.dma_start(tri[:, :, :], a["c_masks"]).then_inc(s_c, 16)
                wout = a["L1_attn_W_out"].rearrange("(p c) f -> p c f", p=NP)
                wqkv = a["L1_attn_W_qkv"].rearrange("f (t p c) -> p f t c", t=3, p=NP)
                bias = a["L1_attn_b_qkv"].rearrange("(t p c) -> p c t", t=3, p=NP)

                def load(n, u):
                    sp.dma_start(w[:, u, :, :], wqkv[n]).then_inc(s_wl[u], 16)
                    sp.dma_start(bqk[:, u, :], bias[n, :, 0:2], allow_slow_non_contiguous=True).then_inc(s_wl[u], 16)
                    row = bias[n, :, 2:3]
                    sp.dma_start(bv[:, u, :], bass.AP(row.tensor, row.offset, [[0, P], [1, P]])).then_inc(s_wl[u], 16)

                def max_rows(reads, u):
                    sp.wait_ge(s_rd, reads)
                    for h in range(2):
                        sp.dma_start(Q[HD * (1 - h):HD * (1 - h) + 1, u, h, :].rearrange("o (t p) -> o t p", p=P),
                                     nm[KT * h:KT * (h + 1), :]).then_inc(s_mr[u], 16)

                load(0, 0)
                load(1, 1)
                max_rows(PRO, 0)
                with sp.Fori(0, ITERS // 2) as it:
                    for u in range(2):
                        n = 2 * it + u
                        sp.wait_ge(s_rd, PRO + USES * n)
                        load((n + 2) % NP, u)
                        sp.dma_start(wo[:, u, :], wout[n % NP]).then_inc(s_wo[u], 16)
                        max_rows(number(n, ("m", 0)) + 1, 1 - u)
                for u in range(2):
                    sp.wait_ge(s_wl[u], 48 * (ITERS // 2 + 1))
                    sp.wait_ge(s_mr[u], 32 * (ITERS // 2 + 1 - u))

            @block.tensor
            def _(pe):
                ln.tensor(pe)
                def turn(num, place, use, u, rd_k):
                    kind, i = use
                    bank = 5 + place % 3
                    if not isinstance(num, int) or num >= 3:
                        pe.wait_ge(s_rd, num - 2)
                    if kind in "qk":
                        mm = pe.matmul(PS[:, bank, :], w[:, u, "qk".index(kind), :], xs[:, u, i * BT:(i + 1) * BT],
                                       start=True, stop=True)
                    elif kind == "v":
                        for j, t in enumerate(VTILES[i]):
                            mm = pe.matmul(PS[:, bank, j * P:(j + 1) * P], xs[:, u, t * P:(t + 1) * P], w[:, u, 2, :],
                                           start=True, stop=True)
                    elif kind == "t":
                        if i == 0:
                            pe.wait_ge(s_rd, rd_k)
                        h, t, c = TILES[i]
                        width = min(BT, (t + 1) * P - c * BT)
                        diagonal = c == t // TPB
                        mm = pe.matmul(PS[:, bank, 0:width], qb[:, h, t * P:(t + 1) * P], kb[:, c * BT:c * BT + width],
                                       start=True, stop=not diagonal)
                        if diagonal:
                            mm = pe.matmul(PS[:, bank, width - P:width], trb[:, 0, :], trb[:, 1, :], start=False, stop=True)
                    elif kind == "m":
                        mm = pe.transpose(PS[0:2 * KT, bank, 0:P], m[:, :], IDN[:, :])
                    elif kind == "z":
                        for h in range(2):
                            mm = pe.matmul(PS[HD * h:HD * (h + 1), bank, :], ones[:, :], S[:, i, h, :], start=True,
                                           stop=True, skip_group_check=True)
                    else:
                        mm = pe.matmul(PS[:, bank, :], wo[:, u, :], on[:, :], start=True, stop=True)
                    mm.then_inc(s_ring, 1)

                def span(s):
                    qc, kt = STEPS[s]
                    return max(0, kt * P - qc * BT)

                def scores(n, s, u):
                    qc, kt = STEPS[s]
                    off, diagonal = span(s), kt >= qc * TPB
                    pe.wait_ge(s_exp, NS * n + s)
                    for h in range(2):
                        bank = 2 * (s % 2) + h
                        mm = pe.matmul(PS[:, bank, off:BT], K[:, u, h, kt * P:(kt + 1) * P],
                                       Q[:, u, h, qc * BT + off:(qc + 1) * BT], start=True, stop=not diagonal)
                        if diagonal:
                            mm = pe.matmul(PS[:, bank, off:off + P], trb[:, 0, :], trb[:, 2, :], start=False, stop=True)
                    mm.then_inc(s_st, 1)

                def weigh(n, s, u):
                    qc, kt = STEPS[s]
                    off, last = span(s), s + 1 == NS or STEPS[s + 1][0] != qc
                    if kt == 0:
                        pe.wait_ge(s_ot, HALVES * n + qc)
                    pe.wait_ge(s_exp, NS * n + s + 2)
                    for h in range(2):
                        mm = pe.matmul(PS[HD * h:HD * (h + 1), 4, off:BT], VA[:, u, kt, HD * h:HD * (h + 1)],
                                       PR[:, s % 3, h, off:BT], start=(kt == 0), stop=last, skip_group_check=True)
                    mm.then_inc(s_pv, 1)

                pe.wait_ge(s_c, 16)
                pe.wait_ge(s_set, SETS)
                pe.wait_ge(s_zero, ZEROS)
                pe.wait_ge(s_wl[0], 48)
                pe.wait_ge(s_x, 1)
                for i, use in enumerate(PREP):
                    if use[0] == "m":
                        pe.wait_ge(s_mx, 1)
                    turn(i, i, use, 0, PREP.index(("k", 1)) + 1)
                with pe.Fori(0, ITERS // 2) as it:
                    for u in range(2):
                        n = 2 * it + u
                        for s in range(NS):
                            if s == 0:
                                pe.wait_ge(s_mr[u], 32 * (it + 1))
                            scores(n, s, u)
                            for i, use in enumerate(RING[s] + [None]):
                                if s and i == len(RING[s]) // 2:
                                    weigh(n, s - 1, u)
                                if use is None:
                                    continue
                                kind, half = use
                                if use == ("q", 0):
                                    pe.wait_ge(s_wl[1 - u], 48 * (it + 1 + u))
                                    pe.wait_ge(s_x, n + 2)
                                elif kind == "m":
                                    pe.wait_ge(s_mx, n + 2)
                                elif kind == "z":
                                    pe.wait_ge(s_sum, added(n, half))
                                elif kind == "y":
                                    pe.wait_ge(s_on, behind(n, half) + 1)
                                    pe.wait_ge(s_wo[(u - half) % 2], 16 * (it + 1 - (half if u == 0 else 0)))
                                of_last = kind in "zy" and half == 1
                                buffers = u if kind in "zy" and half == 0 else 1 - u
                                assert of_last or kind not in "zy" or buffers == u
                                turn(number(n, use), PRO + PLACE[use], use, buffers, number(n, ("k", 1)) + 1)
                        weigh(n, NS - 1, u)
                pe.wait_ge(s_sum, added(ITERS, 1))
                turn(PRO + USES * ITERS, PRO, ("z", 1), 1, 0)
                pe.wait_ge(s_on, behind(ITERS, 1) + 1)
                turn(PRO + USES * ITERS + 1, PRO + 1, ("y", 1), 1, 0)

            @block.scalar
            def _(act):
                ln.scalar(act)
                act.drain().then_inc(s_exp, 1)
                act.wait_ge(s_c, 16)
                for n1 in range(2):
                    act.activation(xs[:, n1, :], XNT[:, 0:SEQ], ACT.Copy).then_inc(s_x, 1)

                def output(n, qc, steps):
                    act.wait_ge(s_pv, NS * n + steps + 2)
                    act.wait_ge(s_on, HALVES * n + qc + 1)
                    act.activation(ot[:, :], PS[:, 4, :], ACT.Copy).then_inc(s_ot, 1)

                def read(num, place, use, u):
                    kind, i = use
                    t = "qk".index(kind)
                    act.wait_ge(s_ring, num + 1)
                    for h, rows in enumerate((lower, upper)):
                        ins = act.activation((Q, K)[t][rows, u, h, i * BT:(i + 1) * BT], PS[rows, 5 + place % 3, :],
                                             ACT.Identity, bias=bqk[rows, u, t:t + 1])
                    ins.then_inc(s_full, 1)

                act.wait_ge(s_set, SETS)
                act.wait_ge(s_zero, ZEROS)
                for i, use in enumerate(QKS):
                    read(i, i, use, 0)
                with act.Fori(0, ITERS // 2) as it:
                    for u in range(2):
                        n = 2 * it + u
                        for s in range(NS):
                            qc, kt = STEPS[s]
                            off = max(0, kt * P - qc * BT)
                            act.wait_ge(s_st, NS * n + s + 1)
                            act.wait_ge(s_pv, NS * n + s)
                            act.wait_ge(s_sum, ADDS[NS] * n + (ADDS[s - 2] + 2 if s >= 2 else 2 - (2 - s)))
                            act.activation(PR[:, s % 3, :, off:BT], PS[:, 2 * (s % 2):2 * (s % 2) + 2, off:BT],
                                           ACT.Exp, scale=float(HD) ** -0.5).then_inc(s_exp, 1)
                            if kt == 0:
                                act.wait_ge(s_ring, number(n, ("z", qc)) + 1 - (0 if qc else USES))
                                act.wait_ge(s_exp, NS * n + s + 2)
                                act.activation(S[:, qc, :, :], PR[:, s % 3, :, :], ACT.Copy).then_inc(s_first, 1)
                            for use in RING[s]:
                                if use in QKS:
                                    read(number(n, use), PRO + PLACE[use], use, 1 - u)
                            if s == TPB:
                                output(n, 0, TPB)
                            if s == NS - 2:
                                act.wait_ge(s_ring, PRO + USES * n)
                                act.activation(xs[:, u, :], XNT[:, bass.ds(SEQ * ((n + 2) % ITERS // NP), SEQ)],
                                               ACT.Copy).then_inc(s_x, 1)
                        output(n, 1, NS)

            @block.gpsimd
            def _(pool):
                ln.gpsimd(pool)
                pool.wait_ge(ln.rstd, NBLK)
                for i, (to, value) in enumerate((
                        (Q[upper, :, 0, :], 0.0), (Q[lower, :, 1, :], 0.0), (K[upper, :, 0, :], 1.0),
                        (K[lower, :, 1, :], 1.0), (qb[upper, 0, :], 0.0), (qb[lower, 1, :], 0.0),
                        (ones[:, :], 1.0), (wo[:, 1, :], 0.0))):
                    if i:
                        pool.wait_ge(s_zero, i)
                    pool.memset(to, value).then_inc(s_zero, 1)
                pool.wait_ge(s_zero, ZEROS)
                pool.wait_ge(s_set, SETS)
                pool.drain().then_inc(s_sum, 2)
                with pool.Fori(0, ITERS) as n:
                    for s, (qc, kt) in enumerate(STEPS):
                        off = max(0, kt * P - qc * BT)
                        if kt == 0:
                            continue
                        pool.wait_ge(s_exp, NS * n + s + 2)
                        if kt == 1:
                            pool.wait_ge(s_first, HALVES * n + qc + 1)
                        else:
                            pool.wait_ge(s_sum, ADDS[NS] * n + ADDS[s] + 2)
                        pool.tensor_tensor(S[:, qc, :, off:BT], S[:, qc, :, off:BT], PR[:, s % 3, :, off:BT],
                                           ALU.add).then_inc(s_sum, 1)

            @block.vector
            def _(dve):
                ln.vector(dve)
                dve.memset(S[:, 1, :, :], 1.0).then_inc(s_set, 1)
                dve.memset(mh[:, :, :], -3e38).then_inc(s_set, 1)
                dve.memset(ot[:, :], 0.0).then_inc(s_set, 1)
                dve.memset(YT[:, :, :], 0.0).then_inc(s_set, 1)
                dve.wait_ge(s_c, 16)
                dve.tensor_copy(trb[:, :, :], tri[:, :, :]).then_inc(s_set, 1)
                dve.wait_ge(s_set, SETS)
                dve.drain().then_inc(s_pv, 2)

                def read(num, place, use, u, n, rows=None, qks=0):
                    kind, i = use
                    bank = 5 + place % 3
                    dve.wait_ge(s_ring, num + 1)
                    if use in QKS:
                        dve.wait_ge(s_full, qks + QKS.index(use) + 1)
                        cols = slice(i * BT, (i + 1) * BT)
                        for h, r in enumerate((lower, upper)):
                            ins = dve.tensor_copy(qb[r, h, cols] if kind == "q" else kb[r, cols],
                                                  (Q if kind == "q" else K)[r, u, h, cols])
                    elif kind == "v":
                        t = VTILES[i]
                        ins = dve.tensor_tensor(VA[:, u, t[0]:t[-1] + 1, :],
                                                PS[:, bank, 0:len(t) * P].rearrange("p (j c) -> p j c", j=len(t)),
                                                bc(bv[:, u, :], [[0, len(t)], [1, P]]), ALU.add)
                    elif kind == "t":
                        h, t, c = TILES[i]
                        width = min(BT, (t + 1) * P - c * BT)
                        ins = dve.tensor_reduce(mh[:, h * KT + t, c:c + 1], PS[:, bank, 0:width], AX.X, ALU.max)
                    elif kind == "m":
                        dve.wait_ge(*rows)
                        ins = dve.tensor_scalar(nm[:, :], PS[0:2 * KT, bank, 0:P], -1.0, None, ALU.mult)
                    elif kind == "z":
                        ins = dve.tensor_copy(su[:, :], PS[:, bank, :])
                    else:
                        dve.wait_ge(s_rd, num)
                        y = YT[:, (n + NP - 1) // NP if i else n // NP + 1, i * BT:(i + 1) * BT]
                        ins = dve.tensor_tensor(y, y, PS[:, bank, :], ALU.add)
                    ins.then_inc(s_rd, 1)

                def invert(num, past, chunk):
                    if chunk < CHUNKS:
                        cols = slice(chunk * BT // CHUNKS, (chunk + 1) * BT // CHUNKS)
                        dve.wait_ge(s_rd, num + 1)
                        dve.reciprocal(z[:, cols], su[:, cols]).then_inc(s_z, 1)
                    else:
                        dve.wait_ge(s_z, CHUNKS * (past + 1))
                        dve.wait_ge(s_ot, past)
                        dve.tensor_tensor(on[:, :], ot[:, :], z[:, :], ALU.mult).then_inc(s_on, 1)

                def maxima(num):
                    dve.wait_ge(s_rd, num)
                    dve.tensor_reduce(m[:, :], mh[:, :, :], AX.X, ALU.max).then_inc(s_mx, 1)

                dve.wait_ge(s_wl[0], 48)
                for i, use in enumerate(PREP):
                    if use[0] == "m":
                        maxima(i)
                    read(i, i, use, 0, 0, (s_set, SETS))
                with dve.Fori(0, ITERS // 2) as it:
                    for u in range(2):
                        n = 2 * it + u
                        for s in range(NS):
                            for use in RING[s]:
                                if use == ("q", 0):
                                    dve.wait_ge(s_wl[1 - u], 48 * (it + 1 + u))
                                if use[0] == "m":
                                    maxima(number(n, use))
                                read(number(n, use), PRO + PLACE[use], use, 1 - u, n, (s_mr[u], 32 * (it + 1)),
                                     len(QKS) * (n + 1))
                                for chunk in range(CHUNKS + 1):
                                    z_use = AT.get(PLACE[use] - 1 - chunk)
                                    if z_use and z_use[0] == "z":
                                        invert(number(n, z_use), behind(n, z_use[1]), chunk)
                read(PRO + USES * ITERS, PRO, ("z", 1), 1, ITERS)
                for chunk in range(CHUNKS + 1):
                    invert(PRO + USES * ITERS, behind(ITERS, 1), chunk)
                read(PRO + USES * ITERS + 1, PRO + 1, ("y", 1), 1, ITERS)


def causal_output(nc, a, g, YT):
    X, IDN, PS = (g[k] for k in ("X", "IDN", "PS"))
    with ExitStack() as ctx:
        sb, sem = stage(nc, ctx)
        bo = sb("co_bo", [P, 1])
        yb = sb("co_yb", [P, 2, BT])
        s_c, s_y, s_t, s_a = (sem("co_" + n) for n in ("bias", "y_biased", "y_turned", "added"))
        with nc.Block() as block:
            @block.sync
            def _(sp):
                sp.dma_start(bo[:, :], a["L1_attn_b_out"].rearrange("(f o) -> f o", o=1),
                             allow_slow_non_contiguous=True).then_inc(s_c, 16)
                sp.wait_ge(s_c, 16)

            @block.scalar
            def _(act):
                act.wait_ge(s_c, 16)
                with act.Fori(0, BATCH) as b:
                    for u in range(2):
                        act.wait_ge(s_t, 2 * b)
                        act.activation(yb[:, u, :], YT[:, b + 1, u * BT:(u + 1) * BT], ACT.Identity,
                                       bias=bo[:, 0:1]).then_inc(s_y, 1)

            @block.tensor
            def _(pe):
                with pe.Fori(0, BATCH) as b:
                    for u in range(2):
                        n = 2 * b + u
                        pe.wait_ge(s_y, n + 1)
                        pe.wait_ge(s_a, 2 * b)
                        for j in range(TPB):
                            mm = pe.transpose(PS[:, u, j * P:(j + 1) * P], yb[:, u, j * P:(j + 1) * P], IDN[:, :])
                        mm.then_inc(s_t, 1)

            @block.vector
            def _(dve):
                with dve.Fori(0, BATCH) as b:
                    for u in range(2):
                        n = 2 * b + u
                        dve.wait_ge(s_t, n + 1)
                        xb = X[:, bass.ds(TPB * n, TPB), :]
                        dve.tensor_tensor(xb, xb, PS[:, u, :].rearrange("p (j c) -> p j c", j=TPB),
                                          ALU.add).then_inc(s_a, 1)


def constants():
    dim = np.arange(P) % DH
    inv = np.float32(1.0) / np.float32(10000.0) ** (np.arange(0, DH, 2, dtype=np.float32) / np.float32(DH))
    angle = (np.arange(SEQ, dtype=np.float32)[None, :] * inv.astype(np.float32)[dim // 2][:, None]).astype(np.float32)
    pb = BT // P
    spread = np.zeros((P, NP, P), np.float32)
    rows = np.zeros((P, NP, VW), np.float32)
    for h in range(2):
        for p in range(NP):
            spread[32 * (p % pb) + 2 * (p // pb) + h, p, h * HD:(h + 1) * HD] = 1.0
            rows[h * HD:(h + 1) * HD, p, 2 * (p // pb) + h] = 1.0
    return {
        "c_ident": np.eye(P, dtype=np.float32),
        "c_rope": np.stack([np.cos(angle), np.sin(angle)]).astype(np.float32),
        "c_lower0": np.tril(np.ones((E0, E0), np.float32), -1),
        "c_spread": spread,
        "c_rows": rows,
        "c_blocks": np.kron(np.eye(2, dtype=np.float32), np.ones((HD, HD), np.float32)),
        "c_masks": np.stack([np.eye(P) * MASK_ROW, np.triu(np.ones((P, P)), 1) * MASK_COL,
                             np.tril(np.ones((P, P)), -1) * MASK_COL], axis=1).astype(np.float32),
        "c_lower1": np.tril(np.ones((E1, E1), np.float32), -1),
    }


_INS = ["L0_attn_x", "L0_attn_wq", "L0_attn_bq", "L0_attn_wk", "L0_attn_bk", "L0_attn_wv", "L0_attn_bv", "L0_attn_wo",
        "L0_attn_bo", "L0_ffn_Wq", "L0_ffn_Wk_c", "L0_ffn_Wv_c", "L0_ffn_Wk", "L0_ffn_Wv", "L0_ffn_Wo",
        "L0_ffn_W_shared_in", "L0_ffn_W_shared_out", "L0_ffn_W1_shared", "L0_ffn_W2_experts", "L0_ffn_Wg_gate",
        "L0_ffn_We_gate", "L0_ffn_group_bias", "L0_ffn_expert_bias", "L0_ffn_norm1_w", "L0_ffn_norm2_w",
        "L1_attn_W_qkv", "L1_attn_b_qkv", "L1_attn_W_out", "L1_attn_b_out", "L1_ffn_gate_w", "L1_ffn_w1", "L1_ffn_b1",
        "L1_ffn_w2", "L1_ffn_b2"]


def kernel(**inputs):
    import concourse.bacc as bacc
    from concourse.bass_utils import run_bass_kernel_spmd

    nc = bacc.Bacc("TRN2", target_bir_lowering=False, num_devices=1)
    arrays, args = {}, {}
    for name, value in [(n, inputs[n]) for n in _INS] + list(constants().items()):
        array = np.ascontiguousarray(value)
        arrays[f"in_{name}"] = array
        args[name] = nc.dram_tensor(f"in_{name}", array.shape, mybir.dt.from_np(array.dtype), kind="ExternalInput").ap()
    out = nc.dram_tensor("out_0_dram", [BATCH, SEQ, D], F32, kind="ExternalOutput").ap()
    build(nc, args, out)
    results = run_bass_kernel_spmd(nc, [arrays], core_ids=[0])
    return results.results[0]["out_0_dram"]
```
